# Optimizing a Trainium2 kernel written in Bass

```python
import numpy as np
import jax
import jax.numpy as jnp

def _softmax(x, axis=-1):
    return jax.nn.softmax(x, axis=axis)

def _gelu(x):
    return jax.nn.gelu(x, approximate=True)

def _silu(x):
    return jax.nn.silu(x)

def _sigmoid(x):
    return jax.nn.sigmoid(x)

def _layernorm(x, axis=-1, eps=1e-05):
    m = jnp.mean(x, axis=axis, keepdims=True)
    v = jnp.var(x, axis=axis, keepdims=True)
    return (x - m) / jnp.sqrt(v + eps)

def _scatter_add(tgt, idx, src, axis=0):
    return tgt.at[idx].add(src)

def _segment_sum(src, seg, n):
    return jax.ops.segment_sum(src, seg, n)
kernel_name = 'mk_gnn_resnorm_d4_gnn_r32_d249dc'

def setup_inputs(seed: int=0):
    np.random.seed(seed)
    _w = jnp.asarray

    def _rec_inputs():
        import jax
        import jax.numpy as jnp
        _gk = jax.random.key(seed)
        x = -0.0003713 + 1 * jax.random.normal(jax.random.fold_in(_gk, 1), (3125, 128), jnp.float32)
        src = jax.random.randint(jax.random.fold_in(_gk, 2), (50000,), 0, 3125, jnp.int32)
        dst = jnp.minimum((3125 * jax.random.uniform(jax.random.fold_in(_gk, 3), (50000,)) ** 2.0).astype(jnp.int32), 99999)
        _o = jnp.argsort(dst, stable=True)
        src = src[_o]
        dst = dst[_o]
        edge_attr_64 = 0.000102155 + 1.00015 * jax.random.normal(jax.random.fold_in(_gk, 11), (50000, 64), jnp.float32)
        edge_type_6 = jax.random.randint(jax.random.fold_in(_gk, 14), (50000,), 0, 6, jnp.int32)
        return (x, src, dst, edge_attr_64, edge_type_6)
    x, src, dst, edge_attr_64, edge_type_6 = _rec_inputs()

    def _L0_gnn_setup():
        import jax, jax.numpy as jnp
        import numpy as np
        N = 3125
        E = 50000
        D = 128

        def _sage_conv(x, src, dst, Wl, b, Wr):
            msgs = jnp.take(x, src, axis=0)
            agg = jax.ops.segment_sum(msgs, dst, num_segments=N)
            deg = jax.ops.segment_sum(jnp.ones((src.shape[0],), x.dtype), dst, num_segments=N)
            agg = agg / jnp.maximum(deg, 1.0)[:, None]
            return agg @ Wl.T + b + x @ Wr.T
        key = jax.random.key(seed)
        ks = jax.random.split(key, 8)
        x = jax.random.normal(ks[0], (N, D), dtype=jnp.float32)
        edge_index = jax.random.randint(ks[1], (2, E), 0, N, dtype=jnp.int64)
        s = 1.0 / jnp.sqrt(jnp.float32(D))
        W1l = jax.random.normal(ks[2], (D, D), dtype=jnp.float32) * s
        b1 = jnp.zeros((D,), dtype=jnp.float32)
        W1r = jax.random.normal(ks[3], (D, D), dtype=jnp.float32) * s
        W2l = jax.random.normal(ks[4], (D, D), dtype=jnp.float32) * s
        b2 = jnp.zeros((D,), dtype=jnp.float32)
        W2r = jax.random.normal(ks[5], (D, D), dtype=jnp.float32) * s
        return {'x': x, 'edge_index': edge_index, 'W1l': W1l, 'b1': b1, 'W1r': W1r, 'W2l': W2l, 'b2': b2, 'W2r': W2r}
    _L0_gnn_all = _L0_gnn_setup()
    _L0_gnn_in = {k: v for k, v in _L0_gnn_all.items() if k in ('W1l', 'b1', 'W1r', 'W2l', 'b2', 'W2r')}
    del _L0_gnn_all

    def _L1_gnn_setup():
        import jax, jax.numpy as jnp
        import numpy as np

        def _mlp(x, w1, b1, w2, b2):
            return jax.nn.relu(x @ w1 + b1) @ w2 + b2
        key = jax.random.key(seed)
        N, E, H, NF, EF = (3125, 15625, 128, 128, 64)

        def rn(i, shape, s=1.0):
            return jax.random.normal(jax.random.fold_in(key, i), shape, jnp.float32) * s
        inp = {'node_features': rn(0, (N, NF)), 'edge_list': jax.random.randint(jax.random.fold_in(key, 1), (E, 2), 0, N), 'edge_features': rn(2, (E, EF)), 'num_nodes': N}
        param_shapes = [('nw1', (NF, H)), ('nb1', (H,)), ('nw2', (H, H)), ('nb2', (H,)), ('ew1', (EF, H)), ('eb1', (H,)), ('ew2', (H, H)), ('eb2', (H,)), ('m0w1', (3 * H, H)), ('m0b1', (H,)), ('m0w2', (H, H)), ('m0b2', (H,)), ('m1w1', (3 * H, H)), ('m1b1', (H,)), ('m1w2', (H, H)), ('m1b2', (H,)), ('aw1', (H, H)), ('ab1', (H,)), ('aw2', (H, H)), ('ab2', (H,))]
        for i, (name, sh) in enumerate(param_shapes):
            inp[name] = rn(10 + i, sh, 0.05)
        return inp
    _L1_gnn_all = _L1_gnn_setup()
    _L1_gnn_in = {k: v for k, v in _L1_gnn_all.items() if k in ('nw1', 'nb1', 'nw2', 'nb2', 'ew1', 'eb1', 'ew2', 'eb2', 'm0w1', 'm0b1', 'm0w2', 'm0b2', 'm1w1', 'm1b1', 'm1w2', 'm1b2', 'aw1', 'ab1', 'aw2', 'ab2')}
    del _L1_gnn_all

    def _L2_gnn_setup():
        import jax, jax.numpy as jnp
        import numpy as np
        N, D, T, E = (50000, 128, 6, 18750)
        LN_EPS = 1e-05
        key = jax.random.key(seed)
        ks = jax.random.split(key, 8)
        x = jax.random.normal(ks[0], (N, D), dtype=jnp.float32)
        edge_index = jax.random.randint(ks[1], (2, E), 0, N, dtype=jnp.int64)
        edge_type = jax.random.randint(ks[2], (E,), 0, T, dtype=jnp.int64)
        s = 1.0 / np.sqrt(D)
        W_l = jax.random.normal(ks[3], (T, D, D), dtype=jnp.float32) * s
        W_r = jax.random.normal(ks[4], (T, D, D), dtype=jnp.float32) * s
        b = jax.random.normal(ks[5], (T, D), dtype=jnp.float32) * s
        emb = jax.random.normal(ks[6], (T, D), dtype=jnp.float32)
        gamma = jnp.ones((D,), dtype=jnp.float32)
        beta = jnp.zeros((D,), dtype=jnp.float32)
        return {'x': x, 'edge_index': edge_index, 'edge_type': edge_type, 'W_l': W_l, 'W_r': W_r, 'b': b, 'emb': emb, 'gamma': gamma, 'beta': beta}
    _L2_gnn_all = _L2_gnn_setup()
    _L2_gnn_in = {k: v for k, v in _L2_gnn_all.items() if k in ('W_l', 'W_r', 'b', 'emb', 'gamma', 'beta')}
    del _L2_gnn_all

    def _L3_gnn_setup():
        import jax, jax.numpy as jnp
        import numpy as np
        N = 3125
        E = 625000
        D_IN = 128
        D_OUT = 128
        EPS = 0.0
        key = jax.random.key(seed)
        k1, k2, k3 = jax.random.split(key, 3)
        x = jax.random.normal(k1, (N, D_IN), dtype=jnp.float32)
        edge_index = jax.random.randint(k2, (2, E), 0, N, dtype=jnp.int64)
        W = jax.random.normal(k3, (D_OUT, D_IN), dtype=jnp.float32) / np.sqrt(D_IN)
        b = jnp.zeros((D_OUT,), dtype=jnp.float32)
        return {'x': x, 'edge_index': edge_index, 'W': W, 'b': b}
    _L3_gnn_all = _L3_gnn_setup()
    _L3_gnn_in = {k: v for k, v in _L3_gnn_all.items() if k in ('W', 'b')}
    del _L3_gnn_all
    return {'x': x, 'src': src, 'dst': dst, 'edge_attr_64': edge_attr_64, 'edge_type_6': edge_type_6, 'L0_gnn_W1l': _L0_gnn_in['W1l'], 'L0_gnn_b1': _L0_gnn_in['b1'], 'L0_gnn_W1r': _L0_gnn_in['W1r'], 'L0_gnn_W2l': _L0_gnn_in['W2l'], 'L0_gnn_b2': _L0_gnn_in['b2'], 'L0_gnn_W2r': _L0_gnn_in['W2r'], 'L1_gnn_nw1': _L1_gnn_in['nw1'], 'L1_gnn_nb1': _L1_gnn_in['nb1'], 'L1_gnn_nw2': _L1_gnn_in['nw2'], 'L1_gnn_nb2': _L1_gnn_in['nb2'], 'L1_gnn_ew1': _L1_gnn_in['ew1'], 'L1_gnn_eb1': _L1_gnn_in['eb1'], 'L1_gnn_ew2': _L1_gnn_in['ew2'], 'L1_gnn_eb2': _L1_gnn_in['eb2'], 'L1_gnn_m0w1': _L1_gnn_in['m0w1'], 'L1_gnn_m0b1': _L1_gnn_in['m0b1'], 'L1_gnn_m0w2': _L1_gnn_in['m0w2'], 'L1_gnn_m0b2': _L1_gnn_in['m0b2'], 'L1_gnn_m1w1': _L1_gnn_in['m1w1'], 'L1_gnn_m1b1': _L1_gnn_in['m1b1'], 'L1_gnn_m1w2': _L1_gnn_in['m1w2'], 'L1_gnn_m1b2': _L1_gnn_in['m1b2'], 'L1_gnn_aw1': _L1_gnn_in['aw1'], 'L1_gnn_ab1': _L1_gnn_in['ab1'], 'L1_gnn_aw2': _L1_gnn_in['aw2'], 'L1_gnn_ab2': _L1_gnn_in['ab2'], 'L2_gnn_W_l': _L2_gnn_in['W_l'], 'L2_gnn_W_r': _L2_gnn_in['W_r'], 'L2_gnn_b': _L2_gnn_in['b'], 'L2_gnn_emb': _L2_gnn_in['emb'], 'L2_gnn_gamma': _L2_gnn_in['gamma'], 'L2_gnn_beta': _L2_gnn_in['beta'], 'L3_gnn_W': _L3_gnn_in['W'], 'L3_gnn_b': _L3_gnn_in['b']}

def reference(x, src, dst, edge_attr_64, edge_type_6, L0_gnn_W1l, L0_gnn_b1, L0_gnn_W1r, L0_gnn_W2l, L0_gnn_b2, L0_gnn_W2r, L1_gnn_nw1, L1_gnn_nb1, L1_gnn_nw2, L1_gnn_nb2, L1_gnn_ew1, L1_gnn_eb1, L1_gnn_ew2, L1_gnn_eb2, L1_gnn_m0w1, L1_gnn_m0b1, L1_gnn_m0w2, L1_gnn_m0b2, L1_gnn_m1w1, L1_gnn_m1b1, L1_gnn_m1w2, L1_gnn_m1b2, L1_gnn_aw1, L1_gnn_ab1, L1_gnn_aw2, L1_gnn_ab2, L2_gnn_W_l, L2_gnn_W_r, L2_gnn_b, L2_gnn_emb, L2_gnn_gamma, L2_gnn_beta, L3_gnn_W, L3_gnn_b):
    import jax
    import jax.numpy as jnp

    def _L0_gnn_ref(x, edge_index, W1l, b1, W1r, W2l, b2, W2r):
        import jax, jax.numpy as jnp
        import numpy as np
        N = 3125
        E = 50000
        D = 128

        def _sage_conv(x, src, dst, Wl, b, Wr):
            msgs = jnp.take(x, src, axis=0)
            agg = jax.ops.segment_sum(msgs, dst, num_segments=N)
            deg = jax.ops.segment_sum(jnp.ones((src.shape[0],), x.dtype), dst, num_segments=N)
            agg = agg / jnp.maximum(deg, 1.0)[:, None]
            return agg @ Wl.T + b + x @ Wr.T
        src, dst = (edge_index[0], edge_index[1])
        h = jax.nn.relu(_sage_conv(x, src, dst, W1l, b1, W1r))
        out = _sage_conv(h, src, dst, W2l, b2, W2r)
        return out

    def _L1_gnn_ref(node_features, edge_list, edge_features, num_nodes, nw1, nb1, nw2, nb2, ew1, eb1, ew2, eb2, m0w1, m0b1, m0w2, m0b2, m1w1, m1b1, m1w2, m1b2, aw1, ab1, aw2, ab2):
        import jax, jax.numpy as jnp
        import numpy as np

        def _mlp(x, w1, b1, w2, b2):
            return jax.nn.relu(x @ w1 + b1) @ w2 + b2
        node_emb = _mlp(node_features, nw1, nb1, nw2, nb2)
        edge_emb = _mlp(edge_features, ew1, eb1, ew2, eb2)
        src, dst = (edge_list[:, 0], edge_list[:, 1])
        for w1, b1, w2, b2 in [(m0w1, m0b1, m0w2, m0b2), (m1w1, m1b1, m1w2, m1b2)]:
            h_src, h_dst = (node_emb[src], node_emb[dst])
            m_fwd = _mlp(jnp.concatenate([h_src, edge_emb, h_dst], axis=-1), w1, b1, w2, b2)
            m_bwd = _mlp(jnp.concatenate([h_dst, edge_emb, h_src], axis=-1), w1, b1, w2, b2)
            new_emb = node_emb + jax.ops.segment_sum(m_fwd, dst, num_segments=num_nodes) + jax.ops.segment_sum(m_bwd, src, num_segments=num_nodes)
            node_emb = _mlp(new_emb, aw1, ab1, aw2, ab2)
        return node_emb

    def _L2_gnn_ref(x, edge_index, edge_type, W_l, W_r, b, emb, gamma, beta):
        import jax, jax.numpy as jnp
        import numpy as np
        N, D, T, E = (50000, 128, 6, 18750)
        LN_EPS = 1e-05
        n, d = x.shape
        t = W_l.shape[0]
        src, dst = (edge_index[0], edge_index[1])
        seg = dst * t + edge_type
        msgs = x[src]
        sums = jax.ops.segment_sum(msgs, seg, num_segments=n * t).reshape(n, t, d)
        cnt = jax.ops.segment_sum(jnp.ones((seg.shape[0],), x.dtype), seg, num_segments=n * t).reshape(n, t, 1)
        mean = sums / jnp.maximum(cnt, 1.0)
        h = jnp.einsum('ntd,tdo->no', mean, W_l) + x @ W_r.sum(0) + (b.sum(0) + emb.sum(0))
        mu = jnp.mean(h, axis=-1, keepdims=True)
        var = jnp.var(h, axis=-1, keepdims=True)
        y = (h - mu) * jax.lax.rsqrt(var + LN_EPS) * gamma + beta
        return jax.nn.relu(y)

    def _L3_gnn_ref(x, edge_index, W, b):
        import jax, jax.numpy as jnp
        import numpy as np
        N = 3125
        E = 625000
        D_IN = 128
        D_OUT = 128
        EPS = 0.0
        src, dst = (edge_index[0], edge_index[1])
        agg = jax.ops.segment_sum(x[src], dst, num_segments=N)
        h = (1.0 + EPS) * x + agg
        out = jax.nn.relu(jnp.einsum('nd,od->no', h, W) + b)
        return out
    edge_index = jnp.stack([src, dst])
    edge_index_t = jnp.stack([src, dst], axis=1)
    x = _layernorm(x + _L0_gnn_ref(x, edge_index, L0_gnn_W1l, L0_gnn_b1, L0_gnn_W1r, L0_gnn_W2l, L0_gnn_b2, L0_gnn_W2r), axis=-1)
    x = _layernorm(x + _L1_gnn_ref(x, edge_index_t, edge_attr_64, 3125, L1_gnn_nw1, L1_gnn_nb1, L1_gnn_nw2, L1_gnn_nb2, L1_gnn_ew1, L1_gnn_eb1, L1_gnn_ew2, L1_gnn_eb2, L1_gnn_m0w1, L1_gnn_m0b1, L1_gnn_m0w2, L1_gnn_m0b2, L1_gnn_m1w1, L1_gnn_m1b1, L1_gnn_m1w2, L1_gnn_m1b2, L1_gnn_aw1, L1_gnn_ab1, L1_gnn_aw2, L1_gnn_ab2), axis=-1)
    x = _layernorm(x + _L2_gnn_ref(x, edge_index, edge_type_6, L2_gnn_W_l, L2_gnn_W_r, L2_gnn_b, L2_gnn_emb, L2_gnn_gamma, L2_gnn_beta), axis=-1)
    x = _layernorm(x + _L3_gnn_ref(x, edge_index, L3_gnn_W, L3_gnn_b), axis=-1)
    return x

_drawn_inputs = setup_inputs


def setup_inputs(seed=0):
    import zlib

    import numpy as np

    out = dict(_drawn_inputs(seed))
    spreads = {'L0_gnn_b1': (0.0, 0.367),
     'L0_gnn_b2': (0.0, 0.268),
     'L2_gnn_gamma': (1.0, 0.2),
     'L2_gnn_beta': (0.0, 0.1),
     'L3_gnn_b': (0.0, 0.594)}
    factors = {'edge_attr_64': 3.412,
     'L1_gnn_ew1': 2.771,
     'L1_gnn_nb1': 2.678,
     'L1_gnn_eb1': 3.287,
     'L1_gnn_ab1': 5.892}
    for name, (base, spread) in spreads.items():
        noise = np.random.default_rng([zlib.crc32(name.encode()), seed]).standard_normal(out[name].shape)
        drawn = base * np.exp(spread * noise) if base else spread * noise
        out[name] = jnp.asarray(drawn.astype(out[name].dtype))
    for name, factor in factors.items():
        out[name] = (out[name] * factor).astype(out[name].dtype)
    return out
```

```python
from contextlib import ExitStack

import concourse.bass as bass
from concourse import mybir
from concourse.alu_op_type import AluOpType as ALU

F32 = mybir.dt.float32
I32 = mybir.dt.int32
ACT = mybir.ActivationFunctionType
AX_X = mybir.AxisListType.X
DVE_ENGINE = (mybir.EngineType.DVE,)
PE_ENGINE = (mybir.EngineType.PE,)

P = 128
N_NODES = 3125
N_EDGES = 50000
D = 128
D_EDGE = 64
TYPES = 6
EPS = 1e-5
NB = -(-N_NODES // P)
NPAD = NB * P
EC = -(-N_EDGES // P)
EPAD = EC * P
NCH = -(-(N_EDGES + NB * (P - 1)) // P // 16) * 16
NS = NCH * P
BODY = 16
HALF = BODY // 2
PAIRS = BODY // 2
ITERS = NCH // BODY
LASTI = ITERS - 1
NCHX = NCH + BODY
FIELDS = 4
REC = D_EDGE + FIELDS
HB = D + 2
ACCW = D + TYPES
PIECES = 8
PIECE = -(-EC // PIECES)
MCH = NCH // PIECES
ARENA = 36800
GROUPS = -(-NB // 4)
assert NCH % BODY == 0 and NCH % PIECES == 0 and NCH // 4 <= P
assert NCH * P >= N_EDGES + NB * (P - 1) - (P - 1)

WEIGHTS = [("w1l", D), ("w1r", D), ("w2l", D), ("w2r", D), ("nw1", D), ("nw2", D), ("aw1", D), ("aw2", D),
           ("ew1", D), ("ew2t", D), ("w3", D), ("m0w1", 3 * D), ("m0w2", D), ("m1w1", 3 * D), ("m1w2", D),
           ("wl", TYPES * D), ("wr", TYPES * D), ("nb1", 1), ("nb2", 1), ("ab1", 1), ("ab2", 1), ("eb1", 1),
           ("eb2", 1)]
ROWS = [("b1", D), ("b2", D), ("ab2", D), ("b3", D), ("m0b1", D), ("m1b1", D), ("lb", 2 * TYPES * D),
        ("m0b2", D), ("m1b2", D), ("gamma", D), ("beta", D)]


def columns(parts):
    at, out = 0, {}
    for name, n in parts:
        out[name] = (at, at + n)
        at += n
    return out, at


W_AT, W_COLS = columns(WEIGHTS)
R_AT, R_COLS = columns(ROWS)
SPREAD = ["m0b2", "m1b2", "gamma", "beta"]


def gnn_kernel(nc, src, dst, etype, x, ea, wpack, rows, out):
    ctx = ExitStack()
    with ctx:
        def sb(name, shape, dt=F32):
            return ctx.enter_context(nc.sbuf_tensor(name, shape, dt))

        def sem(name):
            return ctx.enter_context(nc.semaphore(name))

        rec_dram = nc.dram_tensor("records", (NS + EPAD - N_EDGES, REC), F32).ap()
        hb_dram = nc.dram_tensor("backward_messages", (2 * NS, HB), F32).ap()
        h1_dram = nc.dram_tensor("table_h1", (NPAD, D), F32).ap()
        uw_dram = [nc.dram_tensor(f"table_uw{m}", (NPAD, 2 * D), F32).ap() for m in range(2)]
        y_dram = nc.dram_tensor("table_y", (NPAD * TYPES, D), F32).ap()
        x3_dram = nc.dram_tensor("table_x3", (NPAD, D), F32).ap()
        blk_dram = nc.dram_tensor("chunk_blocks", (2, NCH), I32).ap()
        rec_by_lane = rec_dram[0:NS, :].rearrange("(p c) r -> p (c r)", p=P)
        hb_by_lane = hb_dram[0:NS, :].rearrange("(p c) r -> p (c r)", p=P)

        w_sb = sb("weights", [P, W_COLS])
        r_sb = sb("bias_rows", [1, R_COLS])
        spread = sb("bias_spread", [P, len(SPREAD), D])

        def W(name, lo=0, n=None):
            a, b = W_AT[name]
            return w_sb[:, a + lo:(a + lo + n if n else b)]

        def R(name):
            a, b = R_AT[name]
            return r_sb[0:1, a:b]

        iota128 = sb("iota128", [P, P])
        ident = sb("ident", [P, P])
        tri = sb("tri", [P, P])
        ones = sb("ones_sq", [P, P])
        iota_b = sb("iota_blocks", [P, NB])
        iota_t = sb("iota_types", [P, TYPES])
        chunk_no = sb("chunk_no", [P, 4])
        eps_col = sb("eps_col", [P, 1])
        we2 = sb("edge_to_hidden", [P, 2, 2, D])
        wca = sb("node_to_table", [P, 2, 2, D])
        c_row = sb("hidden_bias_rows", [1, 2, D])
        wrs = sb("wr_sum", [P, D])
        l2_row = sb("l2_bias_row", [1, D])
        start = sb("first_chunks", [P, 2, NB])
        blkrow = sb("block_of_chunk", [1, 2, NCH], I32)
        dloc = sb("dst_local", [P, NCHX])
        sloc = sb("src_local", [P, NCHX])
        cw = sb("edge_weight", [P, NCHX])
        srcidx = sb("src_rows", [P, NCHX], I32)
        yidx = sb("y_rows", [P, NCHX], I32)
        posidx = sb("back_slots", [P, NCHX], I32)
        types1h = sb("types_onehot", [P, NCHX, TYPES])
        invdeg = sb("inv_degree", [P, NB])
        indeg = sb("in_degree", [P, NB])
        icnt = sb("inv_type_count", [P, NB, TYPES])
        gring = sb("gather_index_ring", [P, BODY], I32)
        pring = sb("scatter_index_ring", [P, BODY], I32)
        lane_row = sb("blank_slot_rows", [P, NCH])
        small = sb("small", [P, 8, NB])
        ints = sb("small_ints", [P, 2, NB], I32)

        arena = sb("arena", [P, ARENA])
        top = [0]

        def take(n):
            top[0] += n
            assert top[0] <= ARENA
            return arena[:, top[0] - n:top[0]]

        key_i = take(2 * EC).bitcast(I32).rearrange("p (k e) -> p k e", k=2)
        type_i = take(EC).bitcast(I32)
        tmp_i = take(2 * EC).bitcast(I32).rearrange("p (k e) -> p k e", k=2)
        fld = take(4 * EC).rearrange("p (k e) -> p k e", k=4)
        tmp_f = take(3 * EC).rearrange("p (k e) -> p k e", k=3)
        rec_row = take(EC).bitcast(I32)
        pad_row = take(EC)
        onehot_b = take(NB * (EC + 1)).rearrange("p (b e) -> p b e", b=NB)
        running = take(NB * (EC + 1)).rearrange("p (b e) -> p b e", b=NB)
        staging = take(2 * PIECE * REC).rearrange("p (h e r) -> p h e r", h=2, r=REC)
        rec_blank = arena[:, top[0]:top[0] + 26 * REC].rearrange("p (c r) -> p c r", r=REC)
        take(26 * REC)
        hb_blank = take(13 * HB).rearrange("p (c r) -> p c r", r=HB)
        meta = onehot_b.rearrange("p b e -> p (b e)")[:, 0:2 * MCH * REC]\
            .rearrange("p (h c r) -> p h c r", h=2, r=REC)

        top[0] = 0
        acc = take(NB * ACCW).rearrange("p (b f) -> p b f", b=NB)
        nodes = [take(NB * D).rearrange("p (b f) -> p b f", b=NB) for _ in range(4)]
        nA, nB, nC, nD = nodes
        gathered = take(PAIRS * 2 * 2 * D)
        gat_sb = gathered.rearrange("p (n k f) -> p n k f", n=PAIRS, k=2)
        nE = gathered[:, 0:NB * D].rearrange("p (b f) -> p b f", b=NB)
        table = take(NB * 2 * D)
        lt = table.rearrange("p (b f) -> p b f", b=NB)
        y_ring = table[:, 0:8 * TYPES * D].rearrange("p (n f) -> p n f", n=8)
        onehot = take(4 * 2 * P).rearrange("p (n k f) -> p n k f", n=4, k=2)
        ot_sb = take(2 * 2 * P).rearrange("p (n f) -> p n f", n=2)
        eat_sb = take(2 * 2 * P).rearrange("p (n f) -> p n f", n=2)
        hid_sb = take(2 * 2 * P).rearrange("p (n f) -> p n f", n=2)
        pre = take(2 * 2 * (2 * D + 2)).rearrange("p (n k f) -> p n k f", n=2, k=2)
        hf_sb = take(2 * 2 * D).rearrange("p (n k f) -> p n k f", n=2, k=2)
        hb_sb = take(PAIRS * 2 * HB).rearrange("p (n k f) -> p n k f", n=PAIRS, k=2)
        rec_sb = take(2 * HALF * REC).rearrange("p (h c r) -> p h c r", h=2, r=REC)
        hb_in = take(4 * 4 * HB).rearrange("p (q c r) -> p q c r", q=4, r=HB)
        c6 = take(2 * TYPES).rearrange("p (k t) -> p k t", k=2)

        def flat(node):
            return node.rearrange("p b f -> p (b f)")

        banks = [ctx.enter_context(nc.psum_tensor(f"bank{i}", [P, 512], F32)) for i in range(8)]
        tr_ps, hid_ps, pre_ps, sum_ps = banks[0:2], banks[2:4], banks[4:6], banks[6:8]

        keys_in = sem("keys_in")
        x_in = sem("x_in")
        w_in = sem("w_in")
        consts = sem("consts")
        const_links = sem("const_links")
        blanks = sem("blanks")
        blanks_out = sem("blanks_out")
        rank_tot = sem("rank_tot")
        rank_sum = sem("rank_sum")
        map_ready = sem("map_ready")
        map_out = sem("map_out")
        map_in = sem("map_in")
        fields_in = [sem(f"fields_in{h}") for h in range(2)]
        ea_in = [sem(f"ea_in{h}") for h in range(2)]
        rec_out = [sem(f"rec_out{h}") for h in range(2)]
        meta_in = [sem(f"meta_in{h}") for h in range(2)]
        meta_used = sem("meta_used")
        lane_rows = sem("lane_rows")
        sort_done = sem("sort_done")
        fold_mm = sem("fold_mm")
        chain = sem("vector_chain")
        tables = sem("tables_stored")
        waits_passed = sem("waits_passed")
        y_out = [sem(f"y_out{h}") for h in range(8)]
        out_done = sem("out_done")

        stage_mm = sem("stage_matmuls")
        stage_out = {"act": sem("stage_taken_by_scalar"), "dve": sem("stage_taken_by_vector")}
        counted = {"mm": 0, "act": 0, "dve": 0}

        class Stage:
            def __init__(self, groups, taker):
                self.groups, self.mm, self.out = groups, stage_mm, stage_out[taker]
                self.mm0, self.out0 = counted["mm"], counted[taker]
                counted["mm"] += groups
                counted[taker] += groups
                self.end = self.out0 + groups

        TABLE_GROUPS = -(-NB // 2)
        S = {name: Stage(groups, taker) for name, groups, taker in [
            ("xT", GROUPS, "act"), ("aggT", GROUPS, "act"), ("h1", GROUPS, "act"), ("h1T", GROUPS, "act"),
            ("agg2T", GROUPS, "act"), ("o0", GROUPS, "dve"), ("x1T", GROUPS, "act"), ("nh", GROUPS, "act"),
            ("emb", GROUPS, "act"),
            ("uw0", TABLE_GROUPS, "act"), ("accT0", GROUPS, "act"), ("new0", GROUPS, "dve"),
            ("ah0", GROUPS, "act"), ("emb0", GROUPS, "act"),
            ("uw1", TABLE_GROUPS, "act"), ("accT1", GROUPS, "act"), ("new1", GROUPS, "dve"),
            ("ah1", GROUPS, "act"), ("o1", GROUPS, "dve"),
            ("x2T", GROUPS, "act"), ("y", 2 * NB, "act"), ("r2", GROUPS, "act"), ("hT", GROUPS, "act"),
            ("o3", GROUPS, "act")]}
        ready = {name: sem(name + "_ready") for name in
                 ["aggT", "agg2T", "x1T", "accT0", "accT1", "x2T", "hT"]}

        def blocks_of(g):
            return range(4 * g, min(4 * g + 4, NB))

        def width(g):
            return P * len(blocks_of(g))

        def span(t, g):
            return flat(t)[:, 512 * g:512 * g + width(g)]

        gathered_into = [sem(f"gathered_into{n}") for n in range(PAIRS)]
        sent_from = [sem(f"sent_from{n}") for n in range(PAIRS)]
        PER_PASS = 32 * ITERS
        class Linear:
            def __init__(self, name, number, rows_dram, index, counts=False, weighted=False, stored=0):
                self.gathered0 = number * PER_PASS
                self.rows, self.index, self.counts, self.weighted = rows_dram, index, counts, weighted
                self.stored = stored
                self.width = ACCW if counts else D
                self.idx_ready = sem(name + "_index_ready")
                self.gathered = gathered_into
                self.onehot = sem(name + "_onehot")
                self.mm = sem(name + "_mm")
                self.added = sem(name + "_added")

        class Message:
            def __init__(self, m, stored):
                self.m, self.stored = m, stored
                self.idx_ready, self.pos_ready = sem(f"m{m}_index_ready"), sem(f"m{m}_slots_ready")
                self.gathered, self.gathered0 = gathered_into, (2 + m) * PER_PASS
                self.sent, self.sent0 = sent_from, m * PER_PASS
                self.loaded = [sem(f"m{m}_loaded{h}") for h in range(2)]
                self.onehot = sem(f"m{m}_onehot")
                self.turned = sem(f"m{m}_turned")
                self.turned_out = sem(f"m{m}_turned_out")
                self.hid = sem(f"m{m}_hid")
                self.hid_out = sem(f"m{m}_hid_out")
                self.pre = sem(f"m{m}_pre")
                self.summed = sem(f"m{m}_summed")
                self.relu = sem(f"m{m}_relu")
                self.mm = sem(f"m{m}_mm")
                self.added = sem(f"m{m}_added")
                self.c6 = sem(f"m{m}_c6")
                self.b_in = [sem(f"b{m}_in{q}") for q in range(4)]
                self.b_onehot = sem(f"b{m}_onehot")
                self.b_mm = sem(f"b{m}_mm")
                self.b_added = sem(f"b{m}_added")

        pass_a = Linear("a", 0, x, srcidx, counts=True)
        pass_b = Linear("b", 1, h1_dram, srcidx, stored=16)
        layers = [Message(0, 48), Message(1, 80)]
        pass_c = Linear("c", 4, y_dram, yidx, weighted=True, stored=80)
        pass_d = Linear("d", 5, x3_dram, srcidx, stored=96)
        acc_clear = {p: sem(f"clear{k}") for k, p in enumerate([pass_a, pass_b, *layers, pass_c, pass_d])}

        norm_centred, norm_squared = sem("norm_centred"), sem("norm_squared")
        norm_var, norm_std = sem("norm_var"), sem("norm_std")

        block = ctx.enter_context(nc.Block())

        @block.sync
        def _(sp):
            sp.dma_start(key_i[:, 0, :], src).then_inc(keys_in, 16)
            sp.dma_start(key_i[:, 1, :], dst).then_inc(keys_in, 16)
            sp.dma_start(type_i, etype).then_inc(keys_in, 16)
            sp.dma_start(w_sb[:, :], wpack).then_inc(w_in, 16)
            sp.dma_start(r_sb[:, :], rows).then_inc(w_in, 16)
            for k, name in enumerate(SPREAD):
                a, b = R_AT[name]
                sp.dma_start(spread[:, k, :], rows[0:1, a:b].to_broadcast([P, D])).then_inc(w_in, 16)
            sp.wait_ge(blanks, 3)
            for k in range(NCH // 26):
                sp.dma_start(rec_by_lane[:, k * 26 * REC:(k + 1) * 26 * REC],
                             rec_blank.rearrange("p c r -> p (c r)")).then_inc(blanks_out, 16)
            for s in range(PIECES):
                h, lo, hi = s % 2, s * PIECE, min((s + 1) * PIECE, EC)
                if s >= 2:
                    sp.wait_ge(rec_out[h], 16 * PIECE * (s // 2))
                sp.dma_start(staging[:, h, 0:hi - lo, 0:D_EDGE],
                             ea.rearrange("(p e) f -> p e f", p=P)[:, lo:hi, :]).then_inc(ea_in[h], 16)
            for k in range(NCH // 13):
                sp.dma_start(hb_by_lane[:, k * 13 * HB:(k + 1) * 13 * HB],
                             hb_blank.rearrange("p c r -> p (c r)")).then_inc(blanks_out, 16)
            sp.wait_ge(map_ready, 2)
            for k in range(2):
                sp.dma_start(blk_dram[k].rearrange("(q c) -> q c", c=4),
                             ints[0:NCH // 4, k, 0:4]).then_inc(map_out, 16)
            sp.wait_ge(map_out, 32)
            sp.dma_start(blkrow[0:1, :, :], blk_dram.rearrange("(a k) c -> a k c", a=1)).then_inc(map_in, 16)
            sp.wait_ge(rec_out[0], 16 * PIECE * (PIECES // 2))
            sp.wait_ge(rec_out[1], 16 * (EC - PIECE * (PIECES // 2)))
            for s in range(PIECES):
                if s >= 2:
                    sp.wait_ge(meta_used, s - 1)
                sp.dma_start(meta[:, s % 2, :, :].rearrange("p c r -> p (c r)"),
                             rec_by_lane[:, s * MCH * REC:(s + 1) * MCH * REC]).then_inc(meta_in[s % 2], 16)
            sp.wait_ge(sort_done, 1)
            sp.wait_ge(blanks_out, 16 * (NCH // 26 + NCH // 13))
            sp.dma_start(nA, x.rearrange("(b p) f -> p b f", p=P)).then_inc(x_in, 16)
            sp.wait_ge(S["h1"].out, S["h1"].end)
            sp.dma_start(h1_dram.rearrange("(b p) f -> p b f", p=P), nD).then_inc(tables, 16)
            for L in layers:
                sp.wait_ge(S[f"uw{L.m}"].out, S[f"uw{L.m}"].end)
                table_v = uw_dram[L.m].rearrange("(b p) f -> p b f", p=P)
                sp.dma_start(table_v[:, :, 0:D], lt[:, :, D:2 * D]).then_inc(tables, 16)
                sp.dma_start(table_v[:, :, D:2 * D], lt[:, :, 0:D]).then_inc(tables, 16)

                def load_half(h, col):
                    sp.dma_start(rec_sb[:, h, :, :].rearrange("p c r -> p (c r)"),
                                 rec_by_lane[:, bass.ds(col, HALF * REC)]).then_inc(L.loaded[h], 16)

                for h in range(2):
                    load_half(h, h * HALF * REC)
                with sp.Fori(0, LASTI) as i:
                    for h in range(2):
                        sp.wait_ge(L.turned, i * PAIRS + 4 * h + 4)
                        load_half(h, (i + 1) * (BODY * REC) + h * HALF * REC)

                for n in range(PAIRS):
                    sp.wait_ge(L.sent[n], L.sent0 + PER_PASS)

                def load_quad(q, col):
                    sp.dma_start(hb_in[:, q, :, :].rearrange("p c r -> p (c r)"),
                                 hb_by_lane[:, bass.ds(col, 4 * HB)]).then_inc(L.b_in[q], 16)

                for q in range(4):
                    load_quad(q, q * 4 * HB)
                with sp.Fori(0, LASTI) as i:
                    for q in range(4):
                        sp.wait_ge(L.b_mm, i * PAIRS + 2 * q + 2)
                        load_quad(q, (i + 1) * (BODY * HB) + q * 4 * HB)
            y_v = y_dram.rearrange("(b p t) f -> p b (t f)", p=P, t=TYPES)
            for b in range(NB):
                sp.wait_ge(S["y"].out, S["y"].out0 + 2 * b + 2)
                sp.dma_start(y_v[:, b, :], y_ring[:, b % 8, :]).then_inc(y_out[b % 8], 16)
            sp.wait_ge(ready["hT"], 1)
            sp.dma_start(x3_dram.rearrange("(b p) f -> p b f", p=P), nA).then_inc(tables, 16)
            sp.wait_ge(out_done, 1)
            full = N_NODES // P
            sp.dma_start(out[0:full * P, :].rearrange("(b p) f -> p b f", p=P), nC[:, 0:full, :])\
                .then_inc(out_done, 16)
            sp.dma_start(out[full * P:N_NODES, :], nC[0:N_NODES - full * P, full, :]).then_inc(out_done, 16)
            sp.wait_ge(out_done, 33)

        @block.gpsimd
        def _(pool):
            pool.memset(ones[:, :], 1.0).then_inc(const_links, 1)
            pool.memset(ident[:, :], 0.0).then_inc(const_links, 1)
            pool.memset(rec_blank, 0.0).then_inc(const_links, 1)
            pool.memset(hb_blank, 0.0).then_inc(const_links, 1)
            pool.memset(eps_col[:, :], EPS).then_inc(consts, 1)
            pool.iota(iota128[:, :], [[1, P]], base=0, channel_multiplier=0,
                      allow_small_or_imprecise_dtypes=True).then_inc(consts, 1)
            pool.iota(iota_b[:, :], [[1, NB]], base=0, channel_multiplier=0,
                      allow_small_or_imprecise_dtypes=True).then_inc(consts, 1)
            pool.iota(iota_t[:, :], [[1, TYPES]], base=0, channel_multiplier=0,
                      allow_small_or_imprecise_dtypes=True).then_inc(consts, 1)
            pool.iota(chunk_no[:, :], [[1, 4]], base=0, channel_multiplier=4,
                      allow_small_or_imprecise_dtypes=True).then_inc(consts, 1)
            pool.iota(pad_row, [[1, EC]], base=0, channel_multiplier=EC,
                      allow_small_or_imprecise_dtypes=True).then_inc(consts, 1)
            pool.iota(lane_row[:, :], [[1, NCH]], base=NS, channel_multiplier=NCH,
                      allow_small_or_imprecise_dtypes=True).then_inc(lane_rows, 1)
            pool.wait_ge(const_links, 4)
            pool.memset(rec_blank[:, :, D_EDGE + 1:D_EDGE + 2], -1.0).then_inc(blanks, 1)
            pool.memset(hb_blank[:, :, D:D + 1], -1.0).then_inc(blanks, 1)
            pool.affine_select(out=ident[:, :], in_=ident[:, :], compare_op=ALU.not_equal, fill=1.0,
                               base=0, pattern=[[-1, P]], channel_multiplier=1).then_inc(consts, 1)
            pool.affine_select(out=tri[:, :], in_=ones[:, :], compare_op=ALU.is_ge, fill=0.0,
                               base=-1, pattern=[[1, P]], channel_multiplier=-1).then_inc(consts, 1)
            pool.memset(small[:, 7, :], 1.0).then_inc(blanks, 1)

            pool.wait_ge(blanks_out, 16 * (NCH // 26))
            for s in range(PIECES):
                h, lo, hi = s % 2, s * PIECE, min((s + 1) * PIECE, EC)
                pool.wait_ge(fields_in[h], s // 2 + 1)
                pool.wait_ge(ea_in[h], 16 * (s // 2 + 1))
                for e in range(lo, hi):
                    pool.indirect_dma_start(
                        out=rec_dram, out_offset=bass.IndirectOffsetOnAxis(ap=rec_row[:, e:e + 1], axis=0),
                        in_=staging[:, h, e - lo, :], in_offset=None).then_inc(rec_out[h], 16)

            def passed():
                pool.sem_inc(waits_passed, 1)

            def gather(p, rows, n, wide):
                for k in range(2):
                    pool.indirect_dma_start(
                        out=gat_sb[:, n, k, 0:wide], out_offset=None, in_=rows,
                        in_offset=bass.IndirectOffsetOnAxis(ap=gring[:, 2 * n + k:2 * n + k + 1], axis=0))\
                        .then_inc(p.gathered[n], 16)

            def linear(p):
                if p.stored:
                    pool.wait_ge(tables, p.stored)

                def body(i, prev):
                    for n in range(PAIRS):
                        if n % 4 == 0:
                            pool.wait_ge(p.idx_ready, i * 2 + (n // 4 + 1))
                            passed()
                        if prev is not None:
                            pool.wait_ge(p.mm, prev * PAIRS + (n + 1))
                            passed()
                        gather(p, p.rows, n, D)

                body(0, None)
                with pool.Fori(0, LASTI) as j:
                    body(j + 1, j)

            def message(L):
                def send(n, i):
                    if n % 4 == 0:
                        pool.wait_ge(L.pos_ready, i * 2 + (n // 4 + 1))
                        passed()
                    pool.wait_ge(L.relu, i * PAIRS + (n + 1))
                    passed()
                    for k in range(2):
                        pool.indirect_dma_start(
                            out=hb_dram,
                            out_offset=bass.IndirectOffsetOnAxis(ap=pring[:, 2 * n + k:2 * n + k + 1], axis=0),
                            in_=hb_sb[:, n, k, :], in_offset=None).then_inc(L.sent[n], 16)

                def body(i, prev):
                    for n in range(PAIRS):
                        if n % 4 == 0:
                            pool.wait_ge(L.idx_ready, i * 2 + (n // 4 + 1))
                            passed()
                        if prev is not None:
                            pool.wait_ge(L.summed, prev * PAIRS + (n + 1))
                            passed()
                        gather(L, uw_dram[L.m], n, 2 * D)
                        if n >= 3:
                            send(n - 3, i)
                        elif prev is not None:
                            send(n + 5, prev)

                pool.wait_ge(tables, L.stored)
                body(0, None)
                with pool.Fori(0, LASTI) as j:
                    body(j + 1, j)
                for n in range(5, PAIRS):
                    send(n, LASTI)

            linear(pass_a)
            linear(pass_b)
            message(layers[0])
            message(layers[1])
            for h in range(8):
                pool.wait_ge(y_out[h], 16 * len(range(h, NB, 8)))
            linear(pass_c)
            linear(pass_d)

        @block.scalar
        def _(act):
            def evacuate(name, dst_t, func=ACT.Copy, bias=None):
                st = S[name]
                for g in range(GROUPS):
                    act.wait_ge(st.mm, st.mm0 + g + 1)
                    src_ps = banks[g % 4][:, 0:width(g)]
                    if bias is None:
                        act.activation(span(dst_t, g), src_ps, func).then_inc(st.out, 1)
                    else:
                        act.activation(span(dst_t, g), src_ps, func, bias=bias).then_inc(st.out, 1)

            def norm(k):
                act.wait_ge(norm_centred, k + 1)
                act.activation(flat(nE), flat(nD), ACT.Square).then_inc(norm_squared, 1)
                act.wait_ge(norm_var, k + 1)
                act.activation(small[:, 2, :], small[:, 1, :], ACT.Sqrt, bias=eps_col[:, 0:1],
                               scale=1.0 / D).then_inc(norm_std, 1)

            act.wait_ge(consts, 8)
            evacuate("xT", nB)
            evacuate("aggT", nC)
            evacuate("h1", nD, ACT.Relu)
            evacuate("h1T", nB)
            evacuate("agg2T", nC)
            norm(0)
            evacuate("x1T", nB)
            evacuate("nh", nC, ACT.Relu, W("nb1"))
            evacuate("emb", nD, ACT.Identity, W("nb2"))
            for L in layers:
                m = L.m
                st = S[f"uw{m}"]
                for g in range(st.groups):
                    n = min(2, NB - 2 * g)
                    act.wait_ge(st.mm, st.mm0 + g + 1)
                    act.activation(lt[:, 2 * g:2 * g + n, :].rearrange("p b f -> p (b f)"),
                                   banks[g % 4][:, 0:n * 2 * D], ACT.Copy).then_inc(st.out, 1)

                def turned_out(i, n):
                    act.wait_ge(L.turned, i * PAIRS + (n + 1))
                    act.wait_ge(L.pre, i * PAIRS + max(n - 1, 0))
                    act.activation(ot_sb[:, n % 2, :], tr_ps[n % 2][:, 0:2 * P], ACT.Copy)
                    act.activation(eat_sb[0:D_EDGE, n % 2, :], tr_ps[n % 2][0:D_EDGE, 2 * P:4 * P], ACT.Copy)\
                        .then_inc(L.turned_out, 1)

                def hidden_out(i, n):
                    act.wait_ge(L.hid, i * PAIRS + (n + 1))
                    act.activation(hid_sb[:, n % 2, :], hid_ps[n % 2][:, 0:2 * P], ACT.Relu, bias=W("eb1"))\
                        .then_inc(L.hid_out, 1)

                def relu(i, n):
                    act.wait_ge(L.summed, i * PAIRS + (n + 1))
                    act.wait_ge(L.mm, i * PAIRS + max(n - 1, 0))
                    act.wait_ge(L.sent[n], i * 32 + L.sent0)
                    act.activation(hf_sb[:, n % 2, :, :], pre[:, n % 2, :, 0:D], ACT.Relu)
                    act.activation(hb_sb[:, n, :, :], pre[:, n % 2, :, D:2 * D + 2], ACT.Relu)\
                        .then_inc(L.relu, 1)

                with act.Fori(0, ITERS) as i:
                    for n in range(PAIRS):
                        turned_out(i, n)
                        hidden_out(i, n)
                        if n:
                            relu(i, n - 1)
                    relu(i, PAIRS - 1)
                evacuate(f"accT{m}", nB)
                evacuate(f"ah{m}", nB, ACT.Relu, W("ab1"))
                if m == 0:
                    evacuate("emb0", nD, ACT.Identity, W("ab2"))
            norm(1)
            evacuate("x2T", nB)
            st = S["y"]
            for b in range(NB):
                if b >= 8:
                    act.wait_ge(y_out[b % 8], 16 * (b // 8))
                for h, (lo, hi) in enumerate(((0, 4 * D), (4 * D, TYPES * D))):
                    act.wait_ge(st.mm, st.mm0 + 2 * b + h + 1)
                    act.activation(y_ring[:, b % 8, lo:hi], banks[(2 * b + h) % 4][:, 0:hi - lo], ACT.Copy)\
                        .then_inc(st.out, 1)
            evacuate("r2", nC)
            norm(2)
            norm(3)
            evacuate("hT", nB)
            evacuate("o3", nD, ACT.Relu)
            norm(4)

        @block.vector
        def _(dve):
            links = [0]

            def link(ins):
                links[0] += 1
                ins.then_inc(chain, 1)
                dve.wait_ge(chain, links[0])

            dve.wait_ge(consts, 8)
            dve.wait_ge(blanks, 3)
            dve.wait_ge(keys_in, 48)
            link(dve.tensor_scalar(tmp_f[:, 0, :], pad_row, float(N_EDGES), None, ALU.is_ge))
            link(dve.tensor_scalar(pad_row, pad_row, float(NS - N_EDGES), None, ALU.add))
            link(dve.tensor_tensor(pad_row, pad_row, tmp_f[:, 0, :], ALU.mult))
            link(dve.tensor_copy(fld[:, 0, :], key_i[:, 0, :]))
            link(dve.tensor_copy(fld[:, 2, :], type_i))
            link(dve.tensor_scalar(tmp_i[:, 0, :], key_i[:, 1, :], P - 1, None, ALU.bitwise_and))
            link(dve.tensor_copy(fld[:, 1, :], tmp_i[:, 0, :]))
            for key in range(2):
                link(dve.tensor_scalar(tmp_i[:, 0, :], key_i[:, key, :], 7, None, ALU.arith_shift_right))
                link(dve.tensor_copy(tmp_f[:, 0, :], tmp_i[:, 0, :]))
                shape = [P, NB, EC]
                hot = onehot_b[:, :, 1:EC + 1]
                link(dve.tensor_tensor(hot, tmp_f[:, 0, :].unsqueeze(1).to_broadcast(shape),
                                       iota_b[:, :].unsqueeze(2).to_broadcast(shape), ALU.is_equal))
                totals, nch, first, ends = (small[:, k, :] for k in range(4))
                dve.tensor_reduce(totals, hot, AX_X, ALU.add).then_inc(rank_tot, 1)
                dve.wait_ge(rank_sum, key + 1)
                before, whole = banks[0][:, 0:NB], banks[0][:, 64:64 + NB]
                link(dve.tensor_scalar(nch, whole, float(P - 1), None, ALU.add))
                link(dve.tensor_copy(ints[:, 0, :], nch))
                link(dve.tensor_scalar(ints[:, 1, :], ints[:, 0, :], 7, None, ALU.arith_shift_right))
                link(dve.tensor_copy(nch, ints[:, 1, :]))
                link(dve.tensor_tensor_scan(first, small[:, 7, :], nch, 0.0, ALU.mult, ALU.add))
                link(dve.tensor_tensor(start[:, key, :], first, nch, ALU.subtract))
                link(dve.scalar_tensor_tensor(out=first, in0=start[:, key, :], scalar=float(P), in1=before,
                                              op0=ALU.mult, op1=ALU.add))
                link(dve.tensor_tensor(ends, first, totals, ALU.add))
                link(dve.tensor_scalar(onehot_b[:, 0, 0:1], first[:, 0:1], -1.0, None, ALU.add))
                link(dve.tensor_tensor(onehot_b[:, 1:NB, 0], first[:, 1:NB], ends[:, 0:NB - 1], ALU.subtract))
                line = [P, NB * (EC + 1)]
                link(dve.tensor_tensor_scan(running.rearrange("p b e -> p (b e)"),
                                            ones[:, 0:1].to_broadcast(line),
                                            onehot_b.rearrange("p b e -> p (b e)"), 0.0, ALU.mult, ALU.add))
                link(dve.tensor_tensor(running[:, :, 1:EC + 1], running[:, :, 1:EC + 1], hot, ALU.mult))
                link(dve.tensor_reduce(tmp_f[:, 0, :], running[:, :, 1:EC + 1].rearrange("p b e -> p e b"),
                                       AX_X, ALU.add))
                link(dve.tensor_copy(tmp_i[:, 0, :], tmp_f[:, 0, :]))
                link(dve.tensor_scalar(tmp_i[:, 1, :], tmp_i[:, 0, :], P - 1, None, ALU.bitwise_and))
                link(dve.tensor_copy(tmp_f[:, 1, :], tmp_i[:, 1, :]))
                link(dve.tensor_scalar(tmp_i[:, 1, :], tmp_i[:, 0, :], 7, None, ALU.arith_shift_right))
                link(dve.tensor_copy(tmp_f[:, 2, :], tmp_i[:, 1, :]))
                link(dve.scalar_tensor_tensor(out=tmp_f[:, 0, :], in0=tmp_f[:, 1, :], scalar=float(NCH),
                                              in1=tmp_f[:, 2, :], op0=ALU.mult, op1=ALU.add))
                if key == 0:
                    link(dve.tensor_copy(fld[:, 3, :], tmp_f[:, 0, :]))
                else:
                    link(dve.tensor_tensor(tmp_f[:, 0, :], tmp_f[:, 0, :], pad_row, ALU.add))
                    link(dve.tensor_copy(rec_row, tmp_f[:, 0, :]))
            for s in range(PIECES):
                h, lo, hi = s % 2, s * PIECE, min((s + 1) * PIECE, EC)
                if s >= 2:
                    dve.wait_ge(rec_out[h], 16 * PIECE * (s // 2))
                dve.tensor_copy(staging[:, h, 0:hi - lo, D_EDGE:REC].rearrange("p e r -> p r e"),
                                fld[:, :, lo:hi]).then_inc(fields_in[h], 1)
                if s == 1:
                    shape = [P, 4, NB - 1]
                    cmp = running.rearrange("p b e -> p (b e)")[:, 0:4 * (NB - 1)].rearrange("p (c b) -> p c b", c=4)
                    for key in range(2):
                        link(dve.tensor_tensor(cmp, start[:, key, 1:NB].unsqueeze(1).to_broadcast(shape),
                                               chunk_no[:, :].unsqueeze(2).to_broadcast(shape), ALU.is_le))
                        link(dve.tensor_reduce(small[:, 0, 0:4], cmp, AX_X, ALU.add))
                        dve.tensor_copy(ints[:, key, 0:4], small[:, 0, 0:4]).then_inc(map_ready, 1)
                    dve.wait_ge(w_in, 16 * (2 + len(SPREAD)))
                    for m in range(2):
                        dve.tensor_copy(wca[:, m, 0, :], W(f"m{m}w1", 2 * D, D))
                        dve.tensor_copy(wca[:, m, 1, :], W(f"m{m}w1", 0, D))
                        dve.wait_ge(fold_mm, m + 1)
                        dve.tensor_copy(we2[:, m, :, :],
                                        banks[2 + m][:, 0:D].unsqueeze(1).to_broadcast([P, 2, D]))
                        dve.tensor_tensor(c_row[0:1, m, :], banks[2 + m][0:1, 256:256 + D], R(f"m{m}b1"), ALU.add)
                    dve.tensor_reduce(wrs[:, :], W("wr").rearrange("p (t f) -> p f t", t=TYPES), AX_X, ALU.add)
                    link(dve.tensor_reduce(l2_row[0:1, :], R("lb").rearrange("p (t f) -> p f t", t=2 * TYPES),
                                           AX_X, ALU.add))
                    link(dve.memset(cw[:, :], 0.0))
                    link(dve.memset(yidx[:, :], 0))
                    link(dve.memset(srcidx[:, :], 0))
                    link(dve.memset(posidx[:, :], 0))
                    link(dve.memset(dloc[:, :], -1.0))
                    link(dve.memset(sloc[:, :], 0.0))
            mc_i = running.rearrange("p b e -> p (b e)")[:, 0:2 * NCH].bitcast(I32).rearrange("p (k c) -> p k c", k=2)
            mc_f = running.rearrange("p b e -> p (b e)")[:, 2 * NCH:5 * NCH].rearrange("p (k c) -> p k c", k=3)
            for s in range(PIECES):
                part = slice(s * MCH, (s + 1) * MCH)
                dve.wait_ge(meta_in[s % 2], 16 * (s // 2 + 1))
                fields = meta[:, s % 2, :, D_EDGE:REC].rearrange("p c r -> p r c")
                dve.tensor_copy(mc_f[:, 0, part], fields[:, 0, :])
                dve.tensor_copy(dloc[:, part], fields[:, 1, :])
                dve.tensor_copy(mc_f[:, 1, part], fields[:, 2, :])
                dve.tensor_copy(mc_f[:, 2, part], fields[:, 3, :]).then_inc(meta_used, 1)
            dve.wait_ge(meta_used, PIECES)
            every = slice(0, NCH)
            link(dve.tensor_copy(srcidx[:, every], mc_f[:, 0, :]))
            link(dve.tensor_scalar(mc_i[:, 1, :], srcidx[:, every], P - 1, None, ALU.bitwise_and))
            link(dve.tensor_copy(sloc[:, every], mc_i[:, 1, :]))
            link(dve.tensor_tensor(types1h[:, every, :], mc_f[:, 1, :].unsqueeze(2).to_broadcast([P, NCH, TYPES]),
                                   iota_t[:, :].unsqueeze(1).to_broadcast([P, NCH, TYPES]), ALU.is_equal))
            link(dve.scalar_tensor_tensor(out=mc_f[:, 0, :], in0=mc_f[:, 0, :], scalar=float(TYPES),
                                          in1=mc_f[:, 1, :], op0=ALU.mult, op1=ALU.add))
            link(dve.tensor_copy(yidx[:, every], mc_f[:, 0, :]))
            dve.wait_ge(lane_rows, 1)
            link(dve.tensor_scalar(mc_f[:, 0, :], dloc[:, every], 0.0, None, ALU.is_lt))
            link(dve.tensor_tensor(mc_f[:, 0, :], mc_f[:, 0, :], lane_row[:, :], ALU.mult))
            link(dve.tensor_tensor(mc_f[:, 2, :], mc_f[:, 2, :], mc_f[:, 0, :], ALU.add))
            dve.tensor_copy(posidx[:, every], mc_f[:, 2, :]).then_inc(sort_done, 1)
            dve.wait_ge(sort_done, 1)

            def clear(p):
                dve.memset(acc, 0.0).then_inc(acc_clear[p], 1)
                dve.wait_ge(acc_clear[p], 1)

            def list_half(ring, index, h, col, done):
                dve.tensor_copy(ring[:, h * HALF:(h + 1) * HALF], index[:, bass.ds(col, HALF)]).then_inc(done, 1)

            def add_chunk(p_added, count, blk, part, ps):
                dve.wait_ge(p_added, count)
                slot = acc[:, bass.ds(blk, 1), 0:part].rearrange("p a f -> p (a f)")
                dve.tensor_tensor(slot, slot, ps, ALU.add).then_inc(p_added, 1)

            def block_numbers(which, i):
                return nc.values_load_multi_w_load_instructions(
                    blkrow[0:1, which, bass.ds(i * BODY, BODY)], engines=DVE_ENGINE, min_val=0, max_val=NB - 1,
                    skip_runtime_bounds_check_because="a chunk's block is a count of at most NB - 1 blocks")[1]

            def linear(p):
                def hot(i, n):
                    for k in range(2):
                        col = i * BODY + (2 * n + k)
                        last = dve.tensor_scalar(onehot[:, n % 4, k, :], iota128[:, :], dloc[:, bass.ds(col, 1)],
                                                 cw[:, bass.ds(col, 1)] if p.weighted else None, ALU.is_equal,
                                                 *([ALU.mult] if p.weighted else []))
                    last.then_inc(p.onehot, 1)

                def add(i, n, blks):
                    dve.wait_ge(p.mm, i * PAIRS + (n + 1))
                    for k in range(2):
                        add_chunk(p.added, i * BODY + (2 * n + k), blks[2 * n + k], p.width,
                                  sum_ps[n % 2][:, k * 256:k * 256 + p.width])

                clear(p)
                for h in range(2):
                    list_half(gring, p.index, h, h * HALF, p.idx_ready)
                hot(0, 0)
                with dve.Fori(0, ITERS) as i:
                    blks = block_numbers(1, i)
                    for n in range(PAIRS):
                        if n:
                            add(i, n - 1, blks)
                        if n == 4:
                            list_half(gring, p.index, 0, i * BODY + BODY, p.idx_ready)
                        hot(i, n + 1)
                    add(i, PAIRS - 1, blks)
                    list_half(gring, p.index, 1, i * BODY + (BODY + HALF), p.idx_ready)
                dve.wait_ge(p.added, NCH)

            def message(L):
                def hot(i, n):
                    for k in range(2):
                        last = dve.tensor_scalar(onehot[:, n % 4, k, :], iota128[:, :],
                                                 dloc[:, bass.ds(i * BODY + (2 * n + k), 1)], None, ALU.is_equal)
                    last.then_inc(L.onehot, 1)

                def total(i, n):
                    dve.wait_ge(L.pre, i * PAIRS + (n + 1))
                    dve.wait_ge(L.gathered[n], i * 32 + (L.gathered0 + 32))
                    dve.wait_ge(L.relu, i * PAIRS + max(n - 1, 0))
                    dve.tensor_copy(pre[:, n % 2, :, 2 * D], sloc[:, bass.ds(i * BODY + 2 * n, 2)])
                    dve.tensor_tensor(pre[:, n % 2, :, 0:2 * D],
                                      pre_ps[n % 2][:, :].rearrange("p (k f) -> p k f", k=2),
                                      gat_sb[:, n, :, :], ALU.add).then_inc(L.summed, 1)

                def add(i, n, blks):
                    dve.wait_ge(L.mm, i * PAIRS + (n + 1))
                    if L.m == 0:
                        dve.wait_ge(L.c6, i * BODY + 2 * n)
                        dve.tensor_tensor(c6, sum_ps[n % 2][:, 256:256 + 2 * TYPES].rearrange("p (k t) -> p k t", k=2),
                                          types1h[:, bass.ds(i * BODY + 2 * n, 2), :], ALU.mult).then_inc(L.c6, 1)
                    for k in range(2):
                        add_chunk(L.added, i * BODY + (2 * n + k), blks[2 * n + k], D,
                                  sum_ps[n % 2][:, k * D:(k + 1) * D])
                    if L.m == 0:
                        dve.wait_ge(L.c6, i * BODY + (2 * n + 1))
                        dve.tensor_reduce(cw[:, bass.ds(i * BODY + 2 * n, 2)], c6, AX_X, ALU.add).then_inc(L.c6, 1)

                for n in range(2):
                    dve.memset(pre[:, n, :, 2 * D + 1], 1.0)
                clear(L)
                for h in range(2):
                    list_half(gring, srcidx, h, h * HALF, L.idx_ready)
                list_half(pring, posidx, 0, 0, L.pos_ready)
                hot(0, 0)
                with dve.Fori(0, ITERS) as i:
                    blks = block_numbers(1, i)
                    for n in range(PAIRS):
                        total(i, n)
                        if n:
                            add(i, n - 1, blks)
                        if n == 4:
                            list_half(gring, srcidx, 0, i * BODY + BODY, L.idx_ready)
                            for k in range(4, PAIRS):
                                dve.wait_ge(L.sent[k], i * 32 + L.sent0)
                            list_half(pring, posidx, 1, i * BODY + HALF, L.pos_ready)
                        hot(i, n + 1)
                    add(i, PAIRS - 1, blks)
                    list_half(gring, srcidx, 1, i * BODY + (BODY + HALF), L.idx_ready)
                    for k in range(4):
                        dve.wait_ge(L.sent[k], i * 32 + (L.sent0 + 32))
                    list_half(pring, posidx, 0, i * BODY + BODY, L.pos_ready)
                dve.wait_ge(L.added, NCH)

            def backward(L):
                def hot(i, n):
                    if n % 2 == 0:
                        dve.wait_ge(L.b_in[n // 2], i * 16 + 16)
                    for k in range(2):
                        last = dve.tensor_scalar(onehot[:, n % 4, k, :], iota128[:, :],
                                                 hb_in[:, n // 2, 2 * (n % 2) + k, D:D + 1], None, ALU.is_equal)
                    last.then_inc(L.b_onehot, 1)

                def add(i, n, blks):
                    dve.wait_ge(L.b_mm, i * PAIRS + (n + 1))
                    for k in range(2):
                        add_chunk(L.b_added, i * BODY + (2 * n + k), blks[2 * n + k], HB,
                                  sum_ps[n % 2][:, k * 256:k * 256 + HB])

                with dve.Fori(0, ITERS) as i:
                    hot(i, 0)
                    blks = block_numbers(0, i)
                    for n in range(PAIRS):
                        if n < PAIRS - 1:
                            hot(i, n + 1)
                        if n:
                            add(i, n - 1, blks)
                    add(i, PAIRS - 1, blks)
                dve.wait_ge(L.b_added, NCH)

            def norm(k, to):
                link(dve.tensor_reduce(small[:, 0, :], nD, AX_X, ALU.add))
                link(dve.tensor_scalar(small[:, 0, :], small[:, 0, :], 1.0 / D, None, ALU.mult))
                dve.tensor_tensor(nD, nD, small[:, 0, :].unsqueeze(2).to_broadcast([P, NB, D]), ALU.subtract)\
                    .then_inc(norm_centred, 1)
                dve.wait_ge(norm_squared, k + 1)
                dve.tensor_reduce(small[:, 1, :], nE, AX_X, ALU.add).then_inc(norm_var, 1)
                dve.wait_ge(norm_std, k + 1)
                link(dve.reciprocal(small[:, 3, :], small[:, 2, :]))
                return dve.tensor_tensor(to, nD, small[:, 3, :].unsqueeze(2).to_broadcast([P, NB, D]), ALU.mult)

            def take_out(name, dst_t, add_t):
                st = S[name]
                for g in range(GROUPS):
                    dve.wait_ge(st.mm, st.mm0 + g + 1)
                    dve.tensor_tensor(span(dst_t, g), banks[g % 4][:, 0:width(g)], span(add_t, g), ALU.add)\
                        .then_inc(st.out, 1)
                dve.wait_ge(st.out, st.end)

            def over_features(t):
                return t.unsqueeze(2).to_broadcast([P, NB, D])

            dve.wait_ge(map_in, 16)
            linear(pass_a)
            link(dve.tensor_reduce(indeg[:, :], acc[:, :, D:ACCW], AX_X, ALU.add))
            link(dve.tensor_scalar(invdeg[:, :], indeg[:, :], 1.0, None, ALU.max))
            link(dve.reciprocal(invdeg[:, :], invdeg[:, :]))
            link(dve.tensor_scalar(icnt[:, :, :], acc[:, :, D:ACCW], 1.0, None, ALU.max))
            link(dve.reciprocal(icnt[:, :, :], icnt[:, :, :]))
            dve.tensor_tensor(acc[:, :, 0:D], acc[:, :, 0:D], over_features(invdeg[:, :]), ALU.mult)\
                .then_inc(ready["aggT"], 1)
            dve.wait_ge(S["aggT"].out, S["aggT"].end)
            linear(pass_b)
            dve.tensor_tensor(acc[:, :, 0:D], acc[:, :, 0:D], over_features(invdeg[:, :]), ALU.mult)\
                .then_inc(ready["agg2T"], 1)
            take_out("o0", nD, nA)
            norm(0, nA).then_inc(ready["x1T"], 1)
            for L in layers:
                dve.wait_ge(S[f"uw{L.m}"].out, S[f"uw{L.m}"].end)
                message(L)
                backward(L)
                link(dve.tensor_tensor(small[:, 4, :], indeg[:, :], acc[:, :, HB - 1], ALU.add))
                dve.tensor_tensor(nE, ident[:, :].unsqueeze(1).to_broadcast([P, NB, D]),
                                  over_features(small[:, 4, :]), ALU.mult).then_inc(ready[f"accT{L.m}"], 1)
                take_out(f"new{L.m}", nC, nD)
                if L.m == 0:
                    dve.wait_ge(S["emb0"].out, S["emb0"].end)
            take_out("o1", nD, nA)
            norm(1, nA).then_inc(ready["x2T"], 1)
            dve.wait_ge(S["r2"].out, S["r2"].end)
            linear(pass_c)
            link(dve.tensor_tensor(nD, acc[:, :, 0:D], nC, ALU.add))
            link(norm(2, nD))
            link(dve.tensor_tensor(nD, nD, spread[:, 2, :].unsqueeze(1).to_broadcast([P, NB, D]), ALU.mult))
            link(dve.tensor_tensor(nD, nD, spread[:, 3, :].unsqueeze(1).to_broadcast([P, NB, D]), ALU.add))
            link(dve.scalar_tensor_tensor(out=nD, in0=nD, scalar=0.0, in1=nA, op0=ALU.max, op1=ALU.add))
            norm(3, nA).then_inc(ready["hT"], 1)
            linear(pass_d)
            dve.tensor_tensor(nC, acc[:, :, 0:D], nA, ALU.add).then_inc(ready["hT"], 1)
            dve.wait_ge(S["o3"].out, S["o3"].end)
            link(dve.tensor_tensor(nD, nD, nA, ALU.add))
            norm(4, nC).then_inc(out_done, 1)

        @block.tensor
        def _(pe):
            pe.wait_ge(consts, 8)
            for key in range(2):
                pe.wait_ge(rank_tot, key + 1)
                pe.matmul(banks[0][:, 0:NB], tri[:, :], small[:, 0, :], start=True, stop=True)
                pe.matmul(banks[0][:, 64:64 + NB], ones[:, :], small[:, 0, :], start=True, stop=True)\
                    .then_inc(rank_sum, 1)
            pe.wait_ge(w_in, 16 * (2 + len(SPREAD)))
            for m in range(2):
                pe.matmul(banks[2 + m][:, 0:D], W("ew2t"), W(f"m{m}w1", D, D), start=True, stop=True)
                pe.matmul(banks[2 + m][0:1, 256:256 + D], W("eb2"), W(f"m{m}w1", D, D), start=True, stop=True)\
                    .then_inc(fold_mm, 1)

            def groups(name, emit):
                st = S[name]
                before = list(S).index(name) - 1
                if before >= 0:
                    last_stage = list(S.values())[before]
                    pe.wait_ge(last_stage.out, last_stage.end)
                for g in range(st.groups):
                    if g >= 4:
                        pe.wait_ge(st.out, st.out0 + g - 3)
                    emit(g, banks[g % 4]).then_inc(st.mm, 1)

            def turn(name, src_t):
                def emit(g, bank):
                    for j, b in enumerate(blocks_of(g)):
                        last = pe.transpose(bank[:, j * P:(j + 1) * P], src_t[:, b, 0:D], ident[:, :])
                    return last
                groups(name, emit)

            def product(name, weight, in_t):
                groups(name, lambda g, bank: pe.matmul(bank[:, 0:width(g)], weight, span(in_t, g),
                                                       start=True, stop=True))

            def node_rows(name, parts, bias):
                def emit(g, bank):
                    for j, b in enumerate(blocks_of(g)):
                        o = bank[:, j * P:(j + 1) * P]
                        pe.matmul(o, ones[0:1, :], bias, start=True, stop=False)
                        for k, (in_t, weight) in enumerate(parts):
                            last = pe.matmul(o, in_t[:, b, :], weight, start=False, stop=k == len(parts) - 1)
                    return last
                groups(name, emit)

            def block_numbers(which, i):
                return nc.values_load_multi_w_load_instructions(
                    blkrow[0:1, which, bass.ds(i * BODY, BODY)], engines=PE_ENGINE, min_val=0, max_val=NB - 1,
                    skip_runtime_bounds_check_because="a chunk's block is a count of at most NB - 1 blocks")[1]

            def linear(p):
                with pe.Fori(0, ITERS) as i:
                    for n in range(PAIRS):
                        pe.wait_ge(p.onehot, i * PAIRS + (n + 1))
                        pe.wait_ge(p.added, i * BODY + 2 * max(n - 1, 0))
                        pe.wait_ge(p.gathered[n], i * 32 + (p.gathered0 + 32))
                        for k in range(2):
                            if p.counts:
                                pe.matmul(sum_ps[n % 2][:, k * 256 + D:k * 256 + ACCW], onehot[:, n % 4, k, :],
                                          types1h[:, bass.ds(i * BODY + (2 * n + k), 1), :]
                                          .rearrange("p a t -> p (a t)"), start=True, stop=True)
                            last = pe.matmul(sum_ps[n % 2][:, k * 256:k * 256 + D], onehot[:, n % 4, k, :],
                                             gat_sb[:, n, k, 0:D], start=True, stop=True)
                        last.then_inc(p.mm, 1)

            def message(L):
                def turned(i, n):
                    pe.wait_ge(L.onehot, i * PAIRS + (n + 1))
                    pe.wait_ge(L.turned_out, i * PAIRS + max(n - 1, 0))
                    if n % 4 == 0:
                        pe.wait_ge(L.loaded[n // 4], i * 16 + 16)
                    for k in range(2):
                        pe.transpose(tr_ps[n % 2][:, k * P:(k + 1) * P], onehot[:, n % 4, k, :], ident[:, :])
                    for k in range(2):
                        last = pe.transpose(tr_ps[n % 2][0:D_EDGE, (2 + k) * P:(3 + k) * P],
                                            rec_sb[:, n // 4, 2 * (n % 4) + k, 0:D_EDGE], ident[:, :])
                    last.then_inc(L.turned, 1)

                def hidden(i, n):
                    pe.wait_ge(L.turned_out, i * PAIRS + (n + 1))
                    pe.wait_ge(L.hid_out, i * PAIRS + max(n - 1, 0))
                    pe.matmul(hid_ps[n % 2][:, 0:2 * P], W("ew1")[0:D_EDGE, :], eat_sb[0:D_EDGE, n % 2, :],
                              start=True, stop=True).then_inc(L.hid, 1)

                def before_relu(i, n, blks):
                    pe.wait_ge(L.hid_out, i * PAIRS + (n + 1))
                    pe.wait_ge(L.summed, i * PAIRS + max(n - 1, 0))
                    for k in range(2):
                        o = pre_ps[n % 2][:, k * 2 * D:(k + 1) * 2 * D]
                        pe.matmul(o, hid_sb[:, n % 2, k * P:(k + 1) * P],
                                  we2[:, L.m, :, :].rearrange("p a f -> p (a f)"), start=True, stop=False)
                        last = pe.matmul(o, ot_sb[:, n % 2, k * P:(k + 1) * P],
                                         lt[:, bass.ds(blks[2 * n + k], 1), :].rearrange("p a f -> p (a f)"),
                                         start=False, stop=True)
                    last.then_inc(L.pre, 1)

                def sums(i, n, blks):
                    pe.wait_ge(L.relu, i * PAIRS + (n + 1))
                    pe.wait_ge(L.added, i * BODY + 2 * max(n - 1, 0))
                    for k in range(2):
                        if L.m == 0:
                            if k == 0:
                                pe.wait_ge(L.c6, i * BODY + 2 * max(n - 1, 0))
                            pe.matmul(sum_ps[n % 2][:, 256 + k * TYPES:256 + (k + 1) * TYPES],
                                      ot_sb[:, n % 2, k * P:(k + 1) * P],
                                      icnt[:, bass.ds(blks[2 * n + k], 1), :].rearrange("p a t -> p (a t)"),
                                      start=True, stop=True)
                        last = pe.matmul(sum_ps[n % 2][:, k * D:(k + 1) * D], onehot[:, n % 4, k, :],
                                         hf_sb[:, n % 2, k, :], start=True, stop=True)
                    last.then_inc(L.mm, 1)

                with pe.Fori(0, ITERS) as i:
                    blks = block_numbers(1, i)
                    for n in range(PAIRS):
                        turned(i, n)
                        hidden(i, n)
                        before_relu(i, n, blks)
                        if n:
                            sums(i, n - 1, blks)
                    sums(i, PAIRS - 1, blks)

            def backward(L):
                with pe.Fori(0, ITERS) as i:
                    for n in range(PAIRS):
                        pe.wait_ge(L.b_onehot, i * PAIRS + (n + 1))
                        pe.wait_ge(L.b_added, i * BODY + 2 * max(n - 1, 0))
                        for k in range(2):
                            last = pe.matmul(sum_ps[n % 2][:, k * 256:k * 256 + HB], onehot[:, n % 4, k, :],
                                             hb_in[:, n // 2, 2 * (n % 2) + k, :], start=True, stop=True)
                        last.then_inc(L.b_mm, 1)

            pe.wait_ge(x_in, 16)
            turn("xT", nA)
            linear(pass_a)
            pe.wait_ge(ready["aggT"], 1)
            turn("aggT", acc)
            pe.wait_ge(S["aggT"].out, S["aggT"].end)
            node_rows("h1", [(nC, W("w1l")), (nB, W("w1r"))], R("b1"))
            pe.wait_ge(S["h1"].out, S["h1"].end)
            turn("h1T", nD)
            linear(pass_b)
            pe.wait_ge(ready["agg2T"], 1)
            turn("agg2T", acc)
            pe.wait_ge(S["agg2T"].out, S["agg2T"].end)
            node_rows("o0", [(nC, W("w2l")), (nB, W("w2r"))], R("b2"))
            pe.wait_ge(ready["x1T"], 1)
            turn("x1T", nA)
            pe.wait_ge(S["x1T"].out, S["x1T"].end)
            product("nh", W("nw1"), nB)
            pe.wait_ge(S["nh"].out, S["nh"].end)
            product("emb", W("nw2"), nC)
            pe.wait_ge(S["emb"].out, S["emb"].end)
            for L in layers:
                m = L.m

                def emit(g, bank):
                    for j in range(min(2, NB - 2 * g)):
                        o = bank[:, j * 2 * D:(j + 1) * 2 * D]
                        pe.matmul(o[:, D:2 * D], ones[0:1, :], c_row[0:1, m, :], start=True, stop=False,
                                  skip_group_check=True)
                        pe.matmul(o[:, D:2 * D], nD[:, 2 * g + j, :], wca[:, m, 1, :], start=False, stop=True,
                                  skip_group_check=True)
                        last = pe.matmul(o[:, 0:D], nD[:, 2 * g + j, :], wca[:, m, 0, :], start=True, stop=True)
                    return last
                groups(f"uw{m}", emit)
                pe.wait_ge(S[f"uw{m}"].out, S[f"uw{m}"].end)
                message(L)
                backward(L)
                pe.wait_ge(ready[f"accT{m}"], 1)
                turn(f"accT{m}", acc)
                pe.wait_ge(S[f"accT{m}"].out, S[f"accT{m}"].end)

                def emit_new(g, bank):
                    pe.matmul(bank[:, 0:width(g)], W(f"m{m}w2"), span(nB, g), start=True, stop=False)
                    return pe.matmul(bank[:, 0:width(g)], spread[:, m, :], span(nE, g), start=False, stop=True)
                groups(f"new{m}", emit_new)
                pe.wait_ge(S[f"new{m}"].out, S[f"new{m}"].end)
                product(f"ah{m}", W("aw1"), nC)
                pe.wait_ge(S[f"ah{m}"].out, S[f"ah{m}"].end)
                if m == 0:
                    product("emb0", W("aw2"), nB)
                    pe.wait_ge(S["emb0"].out, S["emb0"].end)
                else:
                    node_rows("o1", [(nB, W("aw2"))], R("ab2"))
            pe.wait_ge(ready["x2T"], 1)
            turn("x2T", nA)
            pe.wait_ge(S["x2T"].out, S["x2T"].end)

            def emit_y(g, bank):
                b, h = divmod(g, 2)
                lo, hi = ((0, 4 * D), (4 * D, TYPES * D))[h]
                return pe.matmul(bank[:, 0:hi - lo], nB[:, b, :], W("wl", lo, hi - lo), start=True, stop=True)
            groups("y", emit_y)
            pe.wait_ge(S["y"].out, S["y"].end)
            node_rows("r2", [(nB, wrs[:, :])], l2_row[0:1, :])
            linear(pass_c)
            linear(pass_d)
            pe.wait_ge(ready["hT"], 2)
            turn("hT", nC)
            pe.wait_ge(S["hT"].out, S["hT"].end)
            node_rows("o3", [(nB, W("w3"))], R("b3"))


def kernel(**inputs):
    import numpy as np
    import concourse.bacc as bacc
    from concourse.bass_utils import run_bass_kernel_spmd

    a = {k: np.asarray(v) for k, v in inputs.items()}

    def edge_list(v, fill):
        flat = np.full(EPAD, fill, v.dtype)
        flat[:N_EDGES] = v
        return flat.reshape(P, EC)

    parts = {
        "w1l": a["L0_gnn_W1l"].T, "w1r": a["L0_gnn_W1r"].T, "w2l": a["L0_gnn_W2l"].T, "w2r": a["L0_gnn_W2r"].T,
        "ew1": a["L1_gnn_ew1"], "ew2t": a["L1_gnn_ew2"].T, "w3": a["L3_gnn_W"].T,
        "wl": a["L2_gnn_W_l"].transpose(1, 0, 2).reshape(D, TYPES * D),
        "wr": a["L2_gnn_W_r"].transpose(1, 0, 2).reshape(D, TYPES * D),
    }
    for name in ("nw1", "nw2", "aw1", "aw2", "m0w2", "m1w2"):
        parts[name] = a["L1_gnn_" + name]
    for name in ("m0w1", "m1w1"):
        parts[name] = a["L1_gnn_" + name].reshape(3, D, D).transpose(1, 0, 2).reshape(D, 3 * D)
    for name in ("nb1", "nb2", "ab1", "ab2", "eb1", "eb2"):
        parts[name] = a["L1_gnn_" + name].reshape(D, 1)
    wpack = np.zeros((P, W_COLS), np.float32)
    for name, (lo, hi) in W_AT.items():
        wpack[:parts[name].shape[0], lo:hi] = parts[name]
    row_parts = {"b1": a["L0_gnn_b1"], "b2": a["L0_gnn_b2"], "ab2": a["L1_gnn_ab2"], "b3": a["L3_gnn_b"],
                 "m0b1": a["L1_gnn_m0b1"], "m1b1": a["L1_gnn_m1b1"], "m0b2": a["L1_gnn_m0b2"],
                 "m1b2": a["L1_gnn_m1b2"], "gamma": a["L2_gnn_gamma"], "beta": a["L2_gnn_beta"],
                 "lb": np.concatenate([a["L2_gnn_b"].reshape(-1), a["L2_gnn_emb"].reshape(-1)])}
    rows = np.zeros((1, R_COLS), np.float32)
    for name, (lo, hi) in R_AT.items():
        rows[0, lo:hi] = row_parts[name]
    x = np.zeros((NPAD, D), np.float32)
    x[:N_NODES] = a["x"]
    ea = np.zeros((EPAD, D_EDGE), np.float32)
    ea[:N_EDGES] = a["edge_attr_64"]
    arrays = {"src_in": edge_list(a["src"], NPAD), "dst_in": edge_list(a["dst"], NPAD),
              "type_in": edge_list(a["edge_type_6"], 0), "x_in_rows": x, "ea_in_rows": ea,
              "wpack_in": wpack, "rows_in": rows}
    nc = bacc.Bacc("TRN2", target_bir_lowering=False, num_devices=1)
    args = [nc.dram_tensor(n, v.shape, mybir.dt.from_np(v.dtype), kind="ExternalInput").ap()
            for n, v in arrays.items()]
    args.append(nc.dram_tensor("out_rows", (N_NODES, D), F32, kind="ExternalOutput").ap())
    gnn_kernel(nc, *args)
    r = run_bass_kernel_spmd(nc, [arrays], core_ids=[0])
    return r.results[0]["out_rows"]
```

```python
from contextlib import ExitStack

import concourse.bass as bass
from concourse import mybir
from concourse.alu_op_type import AluOpType as ALU

F32 = mybir.dt.float32
I32 = mybir.dt.int32
ACT = mybir.ActivationFunctionType
AX_X = mybir.AxisListType.X
DVE_ENGINE = (mybir.EngineType.DVE,)
PE_ENGINE = (mybir.EngineType.PE,)

P = 128
N_NODES = 3125
N_EDGES = 50000
D = 128
D_EDGE = 64
TYPES = 6
EPS = 1e-5
NB = -(-N_NODES // P)
NPAD = NB * P
SORT_GROUPS = 7
SORT_BODY = 4 * SORT_GROUPS
EC = -(-N_EDGES // P // SORT_BODY) * SORT_BODY
SORT_ITERS = EC // SORT_BODY
EPAD = EC * P
NCH = -(-(N_EDGES + NB * (P - 1)) // P // 16) * 16
NS = NCH * P
BODY = 16
HALF = BODY // 2
PAIRS = BODY // 2
ITERS = NCH // BODY
LASTI = ITERS - 1
NCHX = NCH + BODY
FIELDS = 4
EW = 2 * D
REC = EW + FIELDS
HB = D + 2
ACCW = D + TYPES
ARENA = 36800
GROUPS = -(-NB // 4)
assert NCH % BODY == 0 and NCH // 4 <= P
assert NCH * P >= N_EDGES + NB * (P - 1) - (P - 1)

WEIGHTS = [("w1l", D), ("w1r", D), ("w2l", D), ("w2r", D), ("nw1", D), ("nw2", D), ("aw1", D), ("aw2", D),
           ("ewa", D), ("ewb", D), ("ew2t", D), ("w3", D), ("m0w1", 3 * D), ("m0w2", D), ("m1w1", 3 * D), ("m1w2", D),
           ("wl", TYPES * D), ("wr", TYPES * D), ("nb1", 1), ("nb2", 1), ("ab1", 1), ("ab2", 1), ("eb1", 1),
           ("eb2", 1)]
ROWS = [("b1", D), ("b2", D), ("ab2", D), ("b3", D), ("m0b1", D), ("m1b1", D), ("lb", 2 * TYPES * D),
        ("m0b2", D), ("m1b2", D), ("gamma", D), ("beta", D)]


def columns(parts):
    at, out = 0, {}
    for name, n in parts:
        out[name] = (at, at + n)
        at += n
    return out, at


W_AT, W_COLS = columns(WEIGHTS)
R_AT, R_COLS = columns(ROWS)
SPREAD = ["m0b2", "m1b2", "gamma", "beta"]


def gnn_kernel(nc, src, dst, etype, x, ea, wpack, rows, out):
    ctx = ExitStack()
    with ctx:
        def sb(name, shape, dt=F32):
            return ctx.enter_context(nc.sbuf_tensor(name, shape, dt))

        def sem(name):
            return ctx.enter_context(nc.semaphore(name))

        rec_dram = nc.dram_tensor("records", (NS + EPAD - N_EDGES, REC), F32).ap()
        hb_dram = nc.dram_tensor("backward_messages", (2 * NS, HB), F32).ap()
        h1_dram = nc.dram_tensor("table_h1", (NPAD, D), F32).ap()
        uw_dram = [nc.dram_tensor(f"table_uw{m}", (NPAD, 2 * D), F32).ap() for m in range(2)]
        y_dram = nc.dram_tensor("table_y", (NPAD * TYPES, D), F32).ap()
        x3_dram = nc.dram_tensor("table_x3", (NPAD, D), F32).ap()
        blk_dram = nc.dram_tensor("chunk_blocks", (2, NCH), I32).ap()
        rec_by_lane = rec_dram[0:NS, :].rearrange("(p c) r -> p c r", p=P)
        hb_by_lane = hb_dram[0:NS, :].rearrange("(p c) r -> p (c r)", p=P)

        w_sb = sb("weights", [P, W_COLS])
        r_sb = sb("bias_rows", [1, R_COLS])
        spread = sb("bias_spread", [P, len(SPREAD), D])

        def W(name, lo=0, n=None):
            a, b = W_AT[name]
            return w_sb[:, a + lo:(a + lo + n if n else b)]

        def R(name):
            a, b = R_AT[name]
            return r_sb[0:1, a:b]

        iota128 = sb("iota128", [P, P])
        ident = sb("ident", [P, P])
        tri = sb("tri", [P, P])
        ones = sb("ones_sq", [P, P])
        iota_b = sb("iota_blocks", [P, NB])
        iota_t = sb("iota_types", [P, TYPES])
        chunk_no = sb("chunk_no", [P, 4])
        eps_col = sb("eps_col", [P, 1])
        we2 = sb("edge_to_hidden", [P, EW])
        wca = sb("node_to_table", [P, 2, 2, D])
        c_row = sb("hidden_bias_rows", [1, 2, D])
        wrs = sb("wr_sum", [P, D])
        l2_row = sb("l2_bias_row", [1, D])
        start = sb("first_chunks", [P, 2, NB])
        blkrow = sb("block_of_chunk", [1, 2, NCH], I32)
        dloc = sb("dst_local", [P, NCHX])
        sloc = sb("src_local", [P, NCHX])
        cw = sb("edge_weight", [P, NCHX])
        srcidx = sb("src_rows", [P, NCHX], I32)
        yidx = sb("y_rows", [P, NCHX], I32)
        posidx = sb("back_slots", [P, NCHX], I32)
        types1h = sb("types_onehot", [P, NCHX, TYPES])
        invdeg = sb("inv_degree", [P, NB])
        indeg = sb("in_degree", [P, NB])
        icnt = sb("inv_type_count", [P, NB, TYPES])
        srow = sb("sort_index_ring", [P, SORT_BODY], I32)
        gring = sb("gather_index_ring", [P, BODY], I32)
        pring = sb("scatter_index_ring", [P, BODY], I32)
        lane_row = sb("blank_slot_rows", [P, NCH])
        small = sb("small", [P, 8, NB])
        ints = sb("small_ints", [P, 2, NB], I32)

        arena = sb("arena", [P, ARENA])
        top = [0]

        def take(n):
            top[0] += n
            assert top[0] <= ARENA
            return arena[:, top[0] - n:top[0]]

        key_i = take(2 * EC).bitcast(I32).rearrange("p (k e) -> p k e", k=2)
        type_i = take(EC).bitcast(I32)
        tmp_i = take(2 * EC).bitcast(I32).rearrange("p (k e) -> p k e", k=2)
        fld = take(4 * EC).rearrange("p (k e) -> p k e", k=4)
        tmp_f = take(3 * EC).rearrange("p (k e) -> p k e", k=3)
        rec_row = take(EC).bitcast(I32)
        pad_row = take(EC)
        onehot_b = take(NB * (EC + 1)).rearrange("p (b e) -> p b e", b=NB)
        running = take(NB * (EC + 1)).rearrange("p (b e) -> p b e", b=NB)
        staging = take(SORT_BODY * REC).rearrange("p (e r) -> p e r", r=REC)
        ea_sb = take(SORT_BODY * D_EDGE).rearrange("p (g f) -> p g f", g=SORT_GROUPS)
        ea_t = take(2 * 2 * P).rearrange("p (n f) -> p n f", n=2)
        hid_sb = take(2 * 4 * P).rearrange("p (n f) -> p n f", n=2)
        rec_blank = take(REC)
        hb_blank = take(HB)
        meta = onehot_b.rearrange("p b e -> p (b e)")[:, 0:NCH * FIELDS].rearrange("p (c r) -> p c r", r=FIELDS)

        top[0] = 0
        acc = take(NB * ACCW).rearrange("p (b f) -> p b f", b=NB)
        nodes = [take(NB * D).rearrange("p (b f) -> p b f", b=NB) for _ in range(4)]
        nA, nB, nC, nD = nodes
        gathered = take(PAIRS * 2 * 2 * D)
        gat_sb = gathered.rearrange("p (n k f) -> p n k f", n=PAIRS, k=2)
        nE = gathered[:, 0:NB * D].rearrange("p (b f) -> p b f", b=NB)
        table = take(NB * 2 * D)
        lt = table.rearrange("p (b f) -> p b f", b=NB)
        y_ring = table[:, 0:8 * TYPES * D].rearrange("p (n f) -> p n f", n=8)
        onehot = take(4 * 2 * P).rearrange("p (n k f) -> p n k f", n=4, k=2)
        ot_sb = take(4 * 2 * P).rearrange("p (n f) -> p n f", n=4)
        pre = take(2 * 2 * (2 * D + 2)).rearrange("p (n k f) -> p n k f", n=2, k=2)
        hf_sb = take(2 * 2 * D).rearrange("p (n k f) -> p n k f", n=2, k=2)
        hb_sb = take(PAIRS * 2 * HB).rearrange("p (n k f) -> p n k f", n=PAIRS, k=2)
        e_sb = take(2 * HALF * D).rearrange("p (h c f) -> p h c f", h=2, f=D)
        hb_in = take(4 * 4 * HB).rearrange("p (q c r) -> p q c r", q=4, r=HB)
        c6 = take(2 * TYPES).rearrange("p (k t) -> p k t", k=2)

        def flat(node):
            return node.rearrange("p b f -> p (b f)")

        banks = [ctx.enter_context(nc.psum_tensor(f"bank{i}", [P, 512], F32)) for i in range(8)]
        tr_ps, pre_ps, sum_ps = banks[0:2], banks[2:6], banks[6:8]

        keys_in = sem("keys_in")
        x_in = sem("x_in")
        w_in = sem("w_in")
        consts = sem("consts")
        const_links = sem("const_links")
        blanks = sem("blanks")
        blanks_out = sem("blanks_out")
        hb_blanks_out = sem("hb_blanks_out")
        rank_tot = sem("rank_tot")
        rank_sum = sem("rank_sum")
        map_ready = sem("map_ready")
        map_out = sem("map_out")
        map_in = sem("map_in")
        ranked = sem("ranked")
        ea_in = [sem(f"ea_in{g}") for g in range(SORT_GROUPS)]
        ea_turned = sem("ea_turned")
        ea_turned_out = sem("ea_turned_out")
        e_hid = sem("e_hid")
        e_hid_out = sem("e_hid_out")
        e_mm = sem("e_mm")
        rec_ready = sem("rec_ready")
        meta_in = sem("meta_in")
        lane_rows = sem("lane_rows")
        sort_done = sem("sort_done")
        fold_mm = sem("fold_mm")
        folded = sem("folded")
        chain = sem("vector_chain")
        tables = sem("tables_stored")
        waits_passed = sem("waits_passed")
        y_out = [sem(f"y_out{h}") for h in range(8)]
        out_done = sem("out_done")

        stage_mm = sem("stage_matmuls")
        stage_out = {"act": sem("stage_taken_by_scalar"), "dve": sem("stage_taken_by_vector")}
        counted = {"mm": 0, "act": 0, "dve": 0}

        class Stage:
            def __init__(self, groups, taker):
                self.groups, self.mm, self.out = groups, stage_mm, stage_out[taker]
                self.mm0, self.out0 = counted["mm"], counted[taker]
                counted["mm"] += groups
                counted[taker] += groups
                self.end = self.out0 + groups

        TABLE_GROUPS = -(-NB // 2)
        S = {name: Stage(groups, taker) for name, groups, taker in [
            ("xT", GROUPS, "act"), ("aggT", GROUPS, "act"), ("h1", GROUPS, "act"), ("h1T", GROUPS, "act"),
            ("agg2T", GROUPS, "act"), ("o0", GROUPS, "dve"), ("x1T", GROUPS, "act"), ("nh", GROUPS, "act"),
            ("emb", GROUPS, "act"),
            ("uw0", TABLE_GROUPS, "act"), ("accT0", GROUPS, "act"), ("new0", GROUPS, "dve"),
            ("ah0", GROUPS, "act"), ("emb0", GROUPS, "act"),
            ("uw1", TABLE_GROUPS, "act"), ("accT1", GROUPS, "act"), ("new1", GROUPS, "dve"),
            ("ah1", GROUPS, "act"), ("o1", GROUPS, "dve"),
            ("x2T", GROUPS, "act"), ("y", 2 * NB, "act"), ("r2", GROUPS, "act"), ("hT", GROUPS, "act"),
            ("o3", GROUPS, "act")]}
        ready = {name: sem(name + "_ready") for name in
                 ["aggT", "agg2T", "x1T", "accT0", "accT1", "x2T", "hT"]}

        def blocks_of(g):
            return range(4 * g, min(4 * g + 4, NB))

        def width(g):
            return P * len(blocks_of(g))

        def span(t, g):
            return flat(t)[:, 512 * g:512 * g + width(g)]

        gathered_into = [sem(f"gathered_into{n}") for n in range(PAIRS)]
        sent_from = [sem(f"sent_from{n}") for n in range(PAIRS)]
        PER_PASS = 32 * ITERS
        rec_out = [[sent_from[g]] for g in range(SORT_GROUPS - 1)] + [sent_from[SORT_GROUPS - 1:SORT_GROUPS + 1]]
        assert SORT_GROUPS + 1 == PAIRS

        def per_body(g):
            return 16 * 4 // len(rec_out[g])

        class Linear:
            def __init__(self, name, number, rows_dram, index, counts=False, weighted=False, stored=0):
                self.gathered0 = number * PER_PASS
                self.rows, self.index, self.counts, self.weighted = rows_dram, index, counts, weighted
                self.stored = stored
                self.width = ACCW if counts else D
                self.idx_ready = sem(name + "_index_ready")
                self.gathered = gathered_into
                self.onehot = sem(name + "_onehot")
                self.mm = sem(name + "_mm")
                self.added = sem(name + "_added")

        class Message:
            def __init__(self, m, stored):
                self.m, self.stored = m, stored
                self.idx_ready, self.pos_ready = sem(f"m{m}_index_ready"), sem(f"m{m}_slots_ready")
                self.gathered, self.gathered0 = gathered_into, (2 + m) * PER_PASS
                self.sent = sent_from
                self.sent0 = [per_body(min(n, SORT_GROUPS - 1)) * SORT_ITERS + m * PER_PASS for n in range(PAIRS)]
                self.loaded = [sem(f"m{m}_loaded{h}") for h in range(2)]
                self.onehot = sem(f"m{m}_onehot")
                self.turned = sem(f"m{m}_turned")
                self.turned_out = sem(f"m{m}_turned_out")
                self.pre = sem(f"m{m}_pre")
                self.half = sem(f"m{m}_half_summed")
                self.summed = sem(f"m{m}_summed")
                self.relu = sem(f"m{m}_relu")
                self.mm = sem(f"m{m}_mm")
                self.added = sem(f"m{m}_added")
                self.c6 = sem(f"m{m}_c6")
                self.b_in = [sem(f"b{m}_in{q}") for q in range(4)]
                self.b_onehot = sem(f"b{m}_onehot")
                self.b_squares = sem(f"b{m}_squares")
                self.b_onehot_dve = sem(f"b{m}_onehot_by_vector")
                self.b_mm = sem(f"b{m}_mm")
                self.b_added = sem(f"b{m}_added")

        pass_a = Linear("a", 0, x, srcidx, counts=True)
        pass_b = Linear("b", 1, h1_dram, srcidx, stored=16)
        layers = [Message(0, 48), Message(1, 80)]
        pass_c = Linear("c", 4, y_dram, yidx, weighted=True, stored=80)
        pass_d = Linear("d", 5, x3_dram, srcidx, stored=96)
        acc_clear = {p: sem(f"clear{k}") for k, p in enumerate([pass_a, pass_b, *layers, pass_c, pass_d])}

        norm_centred, norm_squared = sem("norm_centred"), sem("norm_squared")
        norm_var, norm_std = sem("norm_var"), sem("norm_std")

        start_at_one = [ea_turned_out, e_hid_out, rec_ready, e_hid, e_mm]
        for p in [pass_a, pass_b, pass_c, pass_d]:
            start_at_one += [p.added, p.mm]
        for L in layers:
            start_at_one += [L.added, L.mm, L.c6, L.relu, L.summed, L.turned_out, L.b_added, L.b_mm, L.b_onehot]

        block = ctx.enter_context(nc.Block())

        @block.sync
        def _(sp):
            sp.dma_start(key_i[:, 0, :], src).then_inc(keys_in, 16)
            sp.dma_start(key_i[:, 1, :], dst).then_inc(keys_in, 16)
            sp.dma_start(type_i, etype).then_inc(keys_in, 16)
            sp.dma_start(w_sb[:, :], wpack).then_inc(w_in, 16)
            sp.dma_start(r_sb[:, :], rows).then_inc(w_in, 16)
            for k, name in enumerate(SPREAD):
                a, b = R_AT[name]
                sp.dma_start(spread[:, k, :], rows[0:1, a:b].to_broadcast([P, D])).then_inc(w_in, 16)
            sp.wait_ge(blanks, 3)
            sp.dma_start(rec_by_lane, rec_blank.unsqueeze(1).to_broadcast([P, NCH, REC])).then_inc(blanks_out, 16)

            def load_features(g, col):
                sp.dma_start(ea_sb[:, g, :],
                             ea.rearrange("(p e) f -> p (e f)", p=P)[:, bass.ds(col, 4 * D_EDGE)])\
                    .then_inc(ea_in[g], 16)

            for g in range(SORT_GROUPS):
                load_features(g, g * 4 * D_EDGE)
            sp.dma_start(hb_by_lane.rearrange("p (c r) -> p c r", r=HB),
                         hb_blank.unsqueeze(1).to_broadcast([P, NCH, HB])).then_inc(hb_blanks_out, 16)
            with sp.Fori(0, SORT_ITERS - 1) as i:
                for g in range(SORT_GROUPS):
                    sp.wait_ge(ea_turned, i * SORT_GROUPS + (g + 1))
                    load_features(g, (i + 1) * (SORT_BODY * D_EDGE) + g * 4 * D_EDGE)
            sp.wait_ge(map_ready, 2)
            for k in range(2):
                sp.dma_start(blk_dram[k].rearrange("(q c) -> q c", c=4),
                             ints[0:NCH // 4, k, 0:4]).then_inc(map_out, 16)
            sp.wait_ge(map_out, 32)
            sp.dma_start(blkrow[0:1, :, :], blk_dram.rearrange("(a k) c -> a k c", a=1)).then_inc(map_in, 16)
            for g in range(SORT_GROUPS):
                for sent in rec_out[g]:
                    sp.wait_ge(sent, per_body(g) * SORT_ITERS)
            for k in range(4):
                part = slice(k * NCH // 4, (k + 1) * NCH // 4)
                sp.dma_start(meta[:, part, :], rec_by_lane[:, part, EW:REC]).then_inc(meta_in, 16)
            sp.wait_ge(sort_done, 1)
            sp.wait_ge(hb_blanks_out, 16)
            sp.dma_start(nA, x.rearrange("(b p) f -> p b f", p=P)).then_inc(x_in, 16)
            sp.wait_ge(S["h1"].out, S["h1"].end)
            sp.dma_start(h1_dram.rearrange("(b p) f -> p b f", p=P), nD).then_inc(tables, 16)
            for L in layers:
                sp.wait_ge(S[f"uw{L.m}"].out, S[f"uw{L.m}"].end)
                table_v = uw_dram[L.m].rearrange("(b p) f -> p b f", p=P)
                sp.dma_start(table_v[:, :, 0:D], lt[:, :, D:2 * D]).then_inc(tables, 16)
                sp.dma_start(table_v[:, :, D:2 * D], lt[:, :, 0:D]).then_inc(tables, 16)

                def load_half(h, chunk):
                    sp.dma_start(e_sb[:, h, :, :], rec_by_lane[:, bass.ds(chunk, HALF), L.m * D:(L.m + 1) * D])\
                        .then_inc(L.loaded[h], 16)

                for h in range(2):
                    load_half(h, h * HALF)
                with sp.Fori(0, LASTI) as i:
                    for h in range(2):
                        sp.wait_ge(L.half, i * PAIRS + (4 * h + 4))
                        load_half(h, (i + 1) * BODY + h * HALF)

                for n in range(PAIRS):
                    sp.wait_ge(L.sent[n], L.sent0[n] + PER_PASS)

                def load_quad(q, col):
                    sp.dma_start(hb_in[:, q, :, :].rearrange("p c r -> p (c r)"),
                                 hb_by_lane[:, bass.ds(col, 4 * HB)]).then_inc(L.b_in[q], 16)

                for q in range(4):
                    load_quad(q, q * 4 * HB)
                with sp.Fori(0, LASTI) as i:
                    for q in range(4):
                        sp.wait_ge(L.b_mm, 1 + i * PAIRS + 2 * q + 2)
                        load_quad(q, (i + 1) * (BODY * HB) + q * 4 * HB)
            y_v = y_dram.rearrange("(b p t) f -> p b (t f)", p=P, t=TYPES)
            for b in range(NB):
                sp.wait_ge(S["y"].out, S["y"].out0 + 2 * b + 2)
                sp.dma_start(y_v[:, b, :], y_ring[:, b % 8, :]).then_inc(y_out[b % 8], 16)
            sp.wait_ge(ready["hT"], 1)
            sp.dma_start(x3_dram.rearrange("(b p) f -> p b f", p=P), nA).then_inc(tables, 16)
            sp.wait_ge(out_done, 1)
            full = N_NODES // P
            sp.dma_start(out[0:full * P, :].rearrange("(b p) f -> p b f", p=P), nC[:, 0:full, :])\
                .then_inc(out_done, 16)
            sp.dma_start(out[full * P:N_NODES, :], nC[0:N_NODES - full * P, full, :]).then_inc(out_done, 16)
            sp.wait_ge(out_done, 33)

        @block.gpsimd
        def _(pool):
            pool.memset(ones[:, :], 1.0).then_inc(const_links, 1)
            pool.memset(ident[:, :], 0.0).then_inc(const_links, 1)
            pool.memset(rec_blank, 0.0).then_inc(const_links, 1)
            pool.memset(hb_blank, 0.0).then_inc(const_links, 1)
            pool.memset(eps_col[:, :], EPS).then_inc(consts, 1)
            pool.iota(iota128[:, :], [[1, P]], base=0, channel_multiplier=0,
                      allow_small_or_imprecise_dtypes=True).then_inc(consts, 1)
            pool.iota(iota_b[:, :], [[1, NB]], base=0, channel_multiplier=0,
                      allow_small_or_imprecise_dtypes=True).then_inc(consts, 1)
            pool.iota(iota_t[:, :], [[1, TYPES]], base=0, channel_multiplier=0,
                      allow_small_or_imprecise_dtypes=True).then_inc(consts, 1)
            pool.iota(chunk_no[:, :], [[1, 4]], base=0, channel_multiplier=4,
                      allow_small_or_imprecise_dtypes=True).then_inc(consts, 1)
            pool.iota(pad_row, [[1, EC]], base=0, channel_multiplier=EC,
                      allow_small_or_imprecise_dtypes=True).then_inc(consts, 1)
            pool.iota(lane_row[:, :], [[1, NCH]], base=NS, channel_multiplier=NCH,
                      allow_small_or_imprecise_dtypes=True).then_inc(lane_rows, 1)
            pool.wait_ge(const_links, 4)
            pool.memset(rec_blank[:, EW + 1:EW + 2], -1.0).then_inc(blanks, 1)
            pool.memset(hb_blank[:, D:D + 1], -1.0).then_inc(blanks, 1)
            pool.affine_select(out=ident[:, :], in_=ident[:, :], compare_op=ALU.not_equal, fill=1.0,
                               base=0, pattern=[[-1, P]], channel_multiplier=1).then_inc(consts, 1)
            pool.affine_select(out=tri[:, :], in_=ones[:, :], compare_op=ALU.is_ge, fill=0.0,
                               base=-1, pattern=[[1, P]], channel_multiplier=-1).then_inc(consts, 1)
            pool.memset(small[:, 7, :], 1.0).then_inc(blanks, 1)

            def passed():
                pool.sem_inc(waits_passed, 1)

            for counter in start_at_one:
                pool.sem_inc(counter, 1)
            pool.wait_ge(blanks_out, 16)
            with pool.Fori(0, SORT_ITERS) as i:
                for g in range(SORT_GROUPS):
                    pool.wait_ge(rec_ready, 1 + i * SORT_GROUPS + (g + 1))
                    passed()
                    for e in range(4 * g, 4 * g + 4):
                        pool.indirect_dma_start(
                            out=rec_dram, out_offset=bass.IndirectOffsetOnAxis(ap=srow[:, e:e + 1], axis=0),
                            in_=staging[:, e, :], in_offset=None).then_inc(rec_out[g][e % len(rec_out[g])], 16)

            def gather(p, rows, n, wide):
                for k in range(2):
                    pool.indirect_dma_start(
                        out=gat_sb[:, n, k, 0:wide], out_offset=None, in_=rows,
                        in_offset=bass.IndirectOffsetOnAxis(ap=gring[:, 2 * n + k:2 * n + k + 1], axis=0))\
                        .then_inc(p.gathered[n], 16)

            def linear(p):
                if p.stored:
                    pool.wait_ge(tables, p.stored)

                def body(i, prev):
                    for n in range(PAIRS):
                        if n % 4 == 0:
                            pool.wait_ge(p.idx_ready, i * 2 + (n // 4 + 1))
                            passed()
                        if prev is not None:
                            pool.wait_ge(p.mm, 1 + prev * PAIRS + (n + 1))
                            passed()
                        gather(p, p.rows, n, D)

                body(0, None)
                with pool.Fori(0, LASTI) as j:
                    body(j + 1, j)

            def message(L):
                def send(n, i):
                    if n % 4 == 0:
                        pool.wait_ge(L.pos_ready, i * 2 + (n // 4 + 1))
                        passed()
                    pool.wait_ge(L.relu, 1 + i * PAIRS + (n + 1))
                    passed()
                    for k in range(2):
                        pool.indirect_dma_start(
                            out=hb_dram,
                            out_offset=bass.IndirectOffsetOnAxis(ap=pring[:, 2 * n + k:2 * n + k + 1], axis=0),
                            in_=hb_sb[:, n, k, :], in_offset=None).then_inc(L.sent[n], 16)

                def body(i, prev):
                    for n in range(PAIRS):
                        if n % 4 == 0:
                            pool.wait_ge(L.idx_ready, i * 2 + (n // 4 + 1))
                            passed()
                        if prev is not None:
                            pool.wait_ge(L.summed, 1 + prev * PAIRS + (n + 1))
                            passed()
                        gather(L, uw_dram[L.m], n, 2 * D)
                        if n >= 3:
                            send(n - 3, i)
                        elif prev is not None:
                            send(n + 5, prev)

                pool.wait_ge(tables, L.stored)
                body(0, None)
                with pool.Fori(0, LASTI) as j:
                    body(j + 1, j)
                for n in range(5, PAIRS):
                    send(n, LASTI)

            linear(pass_a)
            linear(pass_b)
            message(layers[0])
            message(layers[1])
            for h in range(8):
                pool.wait_ge(y_out[h], 16 * len(range(h, NB, 8)))
            linear(pass_c)
            linear(pass_d)

        @block.scalar
        def _(act):
            def evacuate(name, dst_t, func=ACT.Copy, bias=None):
                st = S[name]
                for g in range(GROUPS):
                    act.wait_ge(st.mm, st.mm0 + g + 1)
                    src_ps = banks[g % 4][:, 0:width(g)]
                    if bias is None:
                        act.activation(span(dst_t, g), src_ps, func).then_inc(st.out, 1)
                    else:
                        act.activation(span(dst_t, g), src_ps, func, bias=bias).then_inc(st.out, 1)

            def onehots_by_source(L):
                mine = [n for n in range(PAIRS) if n % 4 != 3]

                def squares(i, at):
                    n = mine[at]
                    act.wait_ge(L.b_onehot, 1 + i * len(mine) + max(at - 2, 0))
                    act.wait_ge(L.b_in[n // 2], i * 16 + 16)
                    for k in range(2):
                        last = act.activation(ot_sb[:, n % 4, k * P:(k + 1) * P], iota128[:, :], ACT.Square,
                                              scale=-1.0, bias=hb_in[:, n // 2, 2 * (n % 2) + k, D:D + 1])
                    last.then_inc(L.b_squares, 1)

                def relu_of(i, at):
                    n = mine[at]
                    act.wait_ge(L.b_squares, i * len(mine) + (at + 1))
                    act.wait_ge(L.b_mm, 1 + i * PAIRS + max(n - 3, 0))
                    act.activation(onehot[:, n % 4, :, :].rearrange("p k f -> p (k f)"), ot_sb[:, n % 4, :],
                                   ACT.Relu, scale=-1.0, bias=ones[:, 0:1]).then_inc(L.b_onehot, 1)

                act.wait_ge(L.mm, 1 + NCH // 2)
                act.wait_ge(L.onehot, NCH // 2 + 2)
                act.wait_ge(L.turned, NCH // 2 + 1)
                with act.Fori(0, ITERS) as i:
                    for at in range(len(mine)):
                        squares(i, at)
                        if at:
                            relu_of(i, at - 1)
                    relu_of(i, len(mine) - 1)

            def norm(k):
                act.wait_ge(norm_centred, k + 1)
                act.activation(flat(nE), flat(nD), ACT.Square).then_inc(norm_squared, 1)
                act.wait_ge(norm_var, k + 1)
                act.activation(small[:, 2, :], small[:, 1, :], ACT.Sqrt, bias=eps_col[:, 0:1],
                               scale=1.0 / D).then_inc(norm_std, 1)

            act.wait_ge(consts, 8)
            act.wait_ge(w_in, 16 * (2 + len(SPREAD)))
            act.wait_ge(fold_mm, 1)
            for m in range(2):
                act.activation(wca[:, m, 0, :], W(f"m{m}w1", 2 * D, D), ACT.Copy)
                act.activation(wca[:, m, 1, :], W(f"m{m}w1", 0, D), ACT.Copy)
                act.activation(c_row[0:1, m, :], banks[1][0:1, 256 + m * D:256 + (m + 1) * D], ACT.Copy)
            act.activation(we2[:, :], banks[1][:, 0:EW], ACT.Copy).then_inc(folded, 1)

            def features_out(i, g):
                act.wait_ge(ea_turned, i * SORT_GROUPS + (g + 1))
                act.wait_ge(e_hid, 1 + i * SORT_GROUPS + max(g - 1, 0))
                act.activation(ea_t[:, g % 2, :], banks[g % 2][:, 0:2 * P], ACT.Copy).then_inc(ea_turned_out, 1)

            def hidden_out(i, g):
                act.wait_ge(e_hid, 1 + i * SORT_GROUPS + (g + 1))
                act.wait_ge(e_mm, 1 + i * SORT_GROUPS + max(g - 1, 0))
                act.activation(hid_sb[:, g % 2, :], banks[2 + g % 2][:, :], ACT.Relu, bias=W("eb1"))\
                    .then_inc(e_hid_out, 1)

            with act.Fori(0, SORT_ITERS) as i:
                for g in range(SORT_GROUPS):
                    features_out(i, g)
                    hidden_out(i, g)

            evacuate("xT", nB)
            evacuate("aggT", nC)
            evacuate("h1", nD, ACT.Relu)
            evacuate("h1T", nB)
            evacuate("agg2T", nC)
            norm(0)
            evacuate("x1T", nB)
            evacuate("nh", nC, ACT.Relu, W("nb1"))
            evacuate("emb", nD, ACT.Identity, W("nb2"))
            for L in layers:
                m = L.m
                st = S[f"uw{m}"]
                for g in range(st.groups):
                    n = min(2, NB - 2 * g)
                    act.wait_ge(st.mm, st.mm0 + g + 1)
                    act.activation(lt[:, 2 * g:2 * g + n, :].rearrange("p b f -> p (b f)"),
                                   banks[g % 4][:, 0:n * 2 * D], ACT.Copy).then_inc(st.out, 1)

                def turned_out(n, count):
                    act.wait_ge(L.turned, count + 1)
                    act.activation(ot_sb[:, n % 4, :], tr_ps[n % 2][:, 0:2 * P], ACT.Copy)\
                        .then_inc(L.turned_out, 1)

                def relu(i, n):
                    act.wait_ge(L.summed, 1 + i * PAIRS + (n + 1))
                    act.wait_ge(L.mm, 1 + i * PAIRS + max(n - 1, 0))
                    act.wait_ge(L.sent[n], i * 32 + L.sent0[n])
                    act.activation(hf_sb[:, n % 2, :, :], pre[:, n % 2, :, 0:D], ACT.Relu)
                    act.activation(hb_sb[:, n, :, :], pre[:, n % 2, :, D:2 * D + 2], ACT.Relu)\
                        .then_inc(L.relu, 1)

                turned_out(0, 0)
                with act.Fori(0, ITERS) as i:
                    for n in range(PAIRS):
                        act.wait_ge(L.mm, 1 + i * PAIRS + max(n - 2, 0))
                        turned_out(n + 1, i * PAIRS + (n + 1))
                        if n:
                            relu(i, n - 1)
                    relu(i, PAIRS - 1)
                onehots_by_source(L)
                evacuate(f"accT{m}", nB)
                evacuate(f"ah{m}", nB, ACT.Relu, W("ab1"))
                if m == 0:
                    evacuate("emb0", nD, ACT.Identity, W("ab2"))
            norm(1)
            evacuate("x2T", nB)
            st = S["y"]
            for b in range(NB):
                if b >= 8:
                    act.wait_ge(y_out[b % 8], 16 * (b // 8))
                for h, (lo, hi) in enumerate(((0, 4 * D), (4 * D, TYPES * D))):
                    act.wait_ge(st.mm, st.mm0 + 2 * b + h + 1)
                    act.activation(y_ring[:, b % 8, lo:hi], banks[(2 * b + h) % 4][:, 0:hi - lo], ACT.Copy)\
                        .then_inc(st.out, 1)
            evacuate("r2", nC)
            norm(2)
            norm(3)
            evacuate("hT", nB)
            evacuate("o3", nD, ACT.Relu)
            norm(4)

        @block.vector
        def _(dve):
            links = [0]

            def link(ins):
                links[0] += 1
                ins.then_inc(chain, 1)
                dve.wait_ge(chain, links[0])

            dve.wait_ge(consts, 8)
            dve.wait_ge(blanks, 3)
            dve.wait_ge(keys_in, 48)
            link(dve.tensor_scalar(tmp_f[:, 0, :], pad_row, float(N_EDGES), None, ALU.is_ge))
            link(dve.tensor_scalar(pad_row, pad_row, float(NS - N_EDGES), None, ALU.add))
            link(dve.tensor_tensor(pad_row, pad_row, tmp_f[:, 0, :], ALU.mult))
            link(dve.tensor_copy(fld[:, 0, :], key_i[:, 0, :]))
            link(dve.tensor_copy(fld[:, 2, :], type_i))
            link(dve.tensor_scalar(tmp_i[:, 0, :], key_i[:, 1, :], P - 1, None, ALU.bitwise_and))
            link(dve.tensor_copy(fld[:, 1, :], tmp_i[:, 0, :]))
            for key in range(2):
                link(dve.tensor_scalar(tmp_i[:, 0, :], key_i[:, key, :], 7, None, ALU.arith_shift_right))
                link(dve.tensor_copy(tmp_f[:, 0, :], tmp_i[:, 0, :]))
                shape = [P, NB, EC]
                hot = onehot_b[:, :, 1:EC + 1]
                link(dve.tensor_tensor(hot, tmp_f[:, 0, :].unsqueeze(1).to_broadcast(shape),
                                       iota_b[:, :].unsqueeze(2).to_broadcast(shape), ALU.is_equal))
                totals, nch, first, ends = (small[:, k, :] for k in range(4))
                dve.tensor_reduce(totals, hot, AX_X, ALU.add).then_inc(rank_tot, 1)
                dve.wait_ge(rank_sum, key + 1)
                before, whole = banks[0][:, 0:NB], banks[0][:, 64:64 + NB]
                link(dve.tensor_scalar(nch, whole, float(P - 1), None, ALU.add))
                link(dve.tensor_copy(ints[:, 0, :], nch))
                link(dve.tensor_scalar(ints[:, 1, :], ints[:, 0, :], 7, None, ALU.arith_shift_right))
                link(dve.tensor_copy(nch, ints[:, 1, :]))
                link(dve.tensor_tensor_scan(first, small[:, 7, :], nch, 0.0, ALU.mult, ALU.add))
                link(dve.tensor_tensor(start[:, key, :], first, nch, ALU.subtract))
                link(dve.scalar_tensor_tensor(out=first, in0=start[:, key, :], scalar=float(P), in1=before,
                                              op0=ALU.mult, op1=ALU.add))
                link(dve.tensor_tensor(ends, first, totals, ALU.add))
                link(dve.tensor_scalar(onehot_b[:, 0, 0:1], first[:, 0:1], -1.0, None, ALU.add))
                link(dve.tensor_tensor(onehot_b[:, 1:NB, 0], first[:, 1:NB], ends[:, 0:NB - 1], ALU.subtract))
                line = [P, NB * (EC + 1)]
                link(dve.tensor_tensor_scan(running.rearrange("p b e -> p (b e)"),
                                            ones[:, 0:1].to_broadcast(line),
                                            onehot_b.rearrange("p b e -> p (b e)"), 0.0, ALU.mult, ALU.add))
                link(dve.tensor_tensor(running[:, :, 1:EC + 1], running[:, :, 1:EC + 1], hot, ALU.mult))
                link(dve.tensor_reduce(tmp_f[:, 0, :], running[:, :, 1:EC + 1].rearrange("p b e -> p e b"),
                                       AX_X, ALU.add))
                link(dve.tensor_copy(tmp_i[:, 0, :], tmp_f[:, 0, :]))
                link(dve.tensor_scalar(tmp_i[:, 1, :], tmp_i[:, 0, :], P - 1, None, ALU.bitwise_and))
                link(dve.tensor_copy(tmp_f[:, 1, :], tmp_i[:, 1, :]))
                link(dve.tensor_scalar(tmp_i[:, 1, :], tmp_i[:, 0, :], 7, None, ALU.arith_shift_right))
                link(dve.tensor_copy(tmp_f[:, 2, :], tmp_i[:, 1, :]))
                link(dve.scalar_tensor_tensor(out=tmp_f[:, 0, :], in0=tmp_f[:, 1, :], scalar=float(NCH),
                                              in1=tmp_f[:, 2, :], op0=ALU.mult, op1=ALU.add))
                if key == 0:
                    link(dve.tensor_copy(fld[:, 3, :], tmp_f[:, 0, :]))
                else:
                    link(dve.tensor_tensor(tmp_f[:, 0, :], tmp_f[:, 0, :], pad_row, ALU.add))
                    dve.tensor_copy(rec_row, tmp_f[:, 0, :]).then_inc(ranked, 1)
                    dve.wait_ge(ranked, 1)

            def make_records(i, prev):
                for g in range(SORT_GROUPS):
                    if prev is not None:
                        for sent in rec_out[g]:
                            dve.wait_ge(sent, prev * per_body(g) + per_body(g))
                    dve.tensor_copy(srow[:, 4 * g:4 * g + 4], rec_row[:, bass.ds(i * SORT_BODY + 4 * g, 4)])
                    dve.tensor_copy(staging[:, 4 * g:4 * g + 4, EW:REC].rearrange("p e r -> p r e"),
                                    fld[:, :, bass.ds(i * SORT_BODY + 4 * g, 4)])
                    dve.wait_ge(e_mm, 1 + i * SORT_GROUPS + (g + 1))
                    for k in range(2):
                        last = dve.tensor_copy(staging[:, 4 * g + k:4 * g + 4:2, 0:EW],
                                               banks[4 + 2 * (g % 2) + k][:, :].rearrange("p (e f) -> p e f", e=2))
                    last.then_inc(rec_ready, 1)

            make_records(0, None)
            with dve.Fori(0, SORT_ITERS - 1) as j:
                make_records(j + 1, j)

            shape = [P, 4, NB - 1]
            cmp = running.rearrange("p b e -> p (b e)")[:, 0:4 * (NB - 1)].rearrange("p (c b) -> p c b", c=4)
            for key in range(2):
                link(dve.tensor_tensor(cmp, start[:, key, 1:NB].unsqueeze(1).to_broadcast(shape),
                                       chunk_no[:, :].unsqueeze(2).to_broadcast(shape), ALU.is_le))
                link(dve.tensor_reduce(small[:, 0, 0:4], cmp, AX_X, ALU.add))
                dve.tensor_copy(ints[:, key, 0:4], small[:, 0, 0:4]).then_inc(map_ready, 1)
            dve.tensor_reduce(wrs[:, :], W("wr").rearrange("p (t f) -> p f t", t=TYPES), AX_X, ALU.add)
            dve.tensor_reduce(l2_row[0:1, :], R("lb").rearrange("p (t f) -> p f t", t=2 * TYPES), AX_X, ALU.add)
            dve.memset(cw[:, :], 0.0)
            dve.memset(yidx[:, :], 0)
            dve.memset(srcidx[:, :], 0)
            dve.memset(posidx[:, :], 0)
            dve.memset(dloc[:, :], -1.0)
            link(dve.memset(sloc[:, :], 0.0))
            mc_i = running.rearrange("p b e -> p (b e)")[:, 0:2 * NCH].bitcast(I32).rearrange("p (k c) -> p k c", k=2)
            mc_f = running.rearrange("p b e -> p (b e)")[:, 2 * NCH:5 * NCH].rearrange("p (k c) -> p k c", k=3)
            dve.wait_ge(meta_in, 64)
            fields = meta.rearrange("p c r -> p r c")
            dve.tensor_copy(mc_f[:, 0, :], fields[:, 0, :])
            dve.tensor_copy(dloc[:, 0:NCH], fields[:, 1, :])
            dve.tensor_copy(mc_f[:, 1, :], fields[:, 2, :])
            link(dve.tensor_copy(mc_f[:, 2, :], fields[:, 3, :]))
            every = slice(0, NCH)
            link(dve.tensor_copy(srcidx[:, every], mc_f[:, 0, :]))
            link(dve.tensor_scalar(mc_i[:, 1, :], srcidx[:, every], P - 1, None, ALU.bitwise_and))
            link(dve.tensor_copy(sloc[:, every], mc_i[:, 1, :]))
            link(dve.tensor_tensor(types1h[:, every, :], mc_f[:, 1, :].unsqueeze(2).to_broadcast([P, NCH, TYPES]),
                                   iota_t[:, :].unsqueeze(1).to_broadcast([P, NCH, TYPES]), ALU.is_equal))
            link(dve.scalar_tensor_tensor(out=mc_f[:, 0, :], in0=mc_f[:, 0, :], scalar=float(TYPES),
                                          in1=mc_f[:, 1, :], op0=ALU.mult, op1=ALU.add))
            link(dve.tensor_copy(yidx[:, every], mc_f[:, 0, :]))
            dve.wait_ge(lane_rows, 1)
            link(dve.tensor_scalar(mc_f[:, 0, :], dloc[:, every], 0.0, None, ALU.is_lt))
            link(dve.tensor_tensor(mc_f[:, 0, :], mc_f[:, 0, :], lane_row[:, :], ALU.mult))
            link(dve.tensor_tensor(mc_f[:, 2, :], mc_f[:, 2, :], mc_f[:, 0, :], ALU.add))
            dve.tensor_copy(posidx[:, every], mc_f[:, 2, :]).then_inc(sort_done, 1)
            dve.wait_ge(sort_done, 1)

            def clear(p):
                dve.memset(acc, 0.0).then_inc(acc_clear[p], 1)
                dve.wait_ge(acc_clear[p], 1)

            def list_half(ring, index, h, col, done):
                dve.tensor_copy(ring[:, h * HALF:(h + 1) * HALF], index[:, bass.ds(col, HALF)]).then_inc(done, 1)

            def add_chunk(p_added, count, blk, part, ps):
                dve.wait_ge(p_added, 1 + count)
                slot = acc[:, bass.ds(blk, 1), 0:part].rearrange("p a f -> p (a f)")
                dve.tensor_tensor(slot, slot, ps, ALU.add).then_inc(p_added, 1)

            def block_numbers(which, i):
                return nc.values_load_multi_w_load_instructions(
                    blkrow[0:1, which, bass.ds(i * BODY, BODY)], engines=DVE_ENGINE, min_val=0, max_val=NB - 1,
                    skip_runtime_bounds_check_because="a chunk's block is a count of at most NB - 1 blocks")[1]

            def linear(p):
                def hot(i, n):
                    for k in range(2):
                        col = i * BODY + (2 * n + k)
                        last = dve.tensor_scalar(onehot[:, n % 4, k, :], iota128[:, :], dloc[:, bass.ds(col, 1)],
                                                 cw[:, bass.ds(col, 1)] if p.weighted else None, ALU.is_equal,
                                                 *([ALU.mult] if p.weighted else []))
                    last.then_inc(p.onehot, 1)

                def add(i, n, blks):
                    dve.wait_ge(p.mm, 1 + i * PAIRS + (n + 1))
                    for k in range(2):
                        add_chunk(p.added, i * BODY + (2 * n + k), blks[2 * n + k], p.width,
                                  sum_ps[n % 2][:, k * 256:k * 256 + p.width])

                clear(p)
                for h in range(2):
                    list_half(gring, p.index, h, h * HALF, p.idx_ready)
                hot(0, 0)
                with dve.Fori(0, ITERS) as i:
                    blks = block_numbers(1, i)
                    for n in range(PAIRS):
                        if n:
                            add(i, n - 1, blks)
                        if n == 4:
                            list_half(gring, p.index, 0, i * BODY + BODY, p.idx_ready)
                        hot(i, n + 1)
                    add(i, PAIRS - 1, blks)
                    list_half(gring, p.index, 1, i * BODY + (BODY + HALF), p.idx_ready)
                dve.wait_ge(p.added, 1 + NCH)

            def message(L):
                def hot(i, n):
                    for k in range(2):
                        last = dve.tensor_scalar(onehot[:, n % 4, k, :], iota128[:, :],
                                                 dloc[:, bass.ds(i * BODY + (2 * n + k), 1)], None, ALU.is_equal)
                    last.then_inc(L.onehot, 1)

                def half_total(i, n):
                    if n % 4 == 0:
                        dve.wait_ge(L.loaded[n // 4], i * 16 + 16)
                    dve.wait_ge(L.gathered[n], i * 32 + (L.gathered0 + 32))
                    dve.wait_ge(L.relu, 1 + i * PAIRS + max(n - 1, 0))
                    dve.tensor_copy(pre[:, n % 2, :, 2 * D], sloc[:, bass.ds(i * BODY + 2 * n, 2)])
                    c = 2 * (n % 4)
                    dve.tensor_tensor(pre[:, n % 2, :, 0:2 * D].rearrange("p k (d f) -> p k d f", d=2),
                                      gat_sb[:, n, :, :].rearrange("p k (d f) -> p k d f", d=2),
                                      e_sb[:, n // 4, c:c + 2, :].unsqueeze(2).to_broadcast([P, 2, 2, D]),
                                      ALU.add).then_inc(L.half, 1)

                def total(i, n):
                    dve.wait_ge(L.half, i * PAIRS + (n + 1))
                    dve.wait_ge(L.pre, i * PAIRS + (n + 1))
                    dve.tensor_tensor(pre[:, n % 2, :, 0:2 * D], pre[:, n % 2, :, 0:2 * D],
                                      pre_ps[n % 4][:, :].rearrange("p (k f) -> p k f", k=2),
                                      ALU.add).then_inc(L.summed, 1)

                def add(i, n, blks):
                    dve.wait_ge(L.mm, 1 + i * PAIRS + (n + 1))
                    if L.m == 0:
                        dve.wait_ge(L.c6, 1 + i * BODY + 2 * n)
                        dve.tensor_tensor(c6, sum_ps[n % 2][:, 256:256 + 2 * TYPES].rearrange("p (k t) -> p k t", k=2),
                                          types1h[:, bass.ds(i * BODY + 2 * n, 2), :], ALU.mult).then_inc(L.c6, 1)
                    for k in range(2):
                        add_chunk(L.added, i * BODY + (2 * n + k), blks[2 * n + k], D,
                                  sum_ps[n % 2][:, k * D:(k + 1) * D])
                    if L.m == 0:
                        dve.wait_ge(L.c6, 1 + i * BODY + (2 * n + 1))
                        dve.tensor_reduce(cw[:, bass.ds(i * BODY + 2 * n, 2)], c6, AX_X, ALU.add).then_inc(L.c6, 1)

                for n in range(2):
                    dve.memset(pre[:, n, :, 2 * D + 1], 1.0)
                clear(L)
                for h in range(2):
                    list_half(gring, srcidx, h, h * HALF, L.idx_ready)
                list_half(pring, posidx, 0, 0, L.pos_ready)
                hot(0, 0)
                hot(0, 1)
                with dve.Fori(0, ITERS) as i:
                    blks = block_numbers(1, i)
                    half_total(i, 0)
                    for n in range(PAIRS):
                        total(i, n)
                        hot(i, n + 2)
                        if n < PAIRS - 1:
                            half_total(i, n + 1)
                        if n:
                            add(i, n - 1, blks)
                        if n == 4:
                            list_half(gring, srcidx, 0, i * BODY + BODY, L.idx_ready)
                            for k in range(4, PAIRS):
                                dve.wait_ge(L.sent[k], i * 32 + L.sent0[k])
                            list_half(pring, posidx, 1, i * BODY + HALF, L.pos_ready)
                    add(i, PAIRS - 1, blks)
                    list_half(gring, srcidx, 1, i * BODY + (BODY + HALF), L.idx_ready)
                    for k in range(4):
                        dve.wait_ge(L.sent[k], i * 32 + (L.sent0[k] + 32))
                    list_half(pring, posidx, 0, i * BODY + BODY, L.pos_ready)
                dve.wait_ge(L.added, 1 + NCH)

            def backward(L):
                def hot(i, n):
                    dve.wait_ge(L.b_in[n // 2], i * 16 + 16)
                    for k in range(2):
                        last = dve.tensor_scalar(onehot[:, n % 4, k, :], iota128[:, :],
                                                 hb_in[:, n // 2, 2 * (n % 2) + k, D:D + 1], None, ALU.is_equal)
                    last.then_inc(L.b_onehot_dve, 1)

                def add(i, n, blks):
                    dve.wait_ge(L.b_mm, 1 + i * PAIRS + (n + 1))
                    for k in range(2):
                        add_chunk(L.b_added, i * BODY + (2 * n + k), blks[2 * n + k], HB,
                                  sum_ps[n % 2][:, k * 256:k * 256 + HB])

                with dve.Fori(0, ITERS) as i:
                    blks = block_numbers(0, i)
                    for n in range(PAIRS):
                        if n % 4 == 2:
                            hot(i, n + 1)
                        if n:
                            add(i, n - 1, blks)
                    add(i, PAIRS - 1, blks)
                dve.wait_ge(L.b_added, 1 + NCH)

            def norm(k, to):
                link(dve.tensor_reduce(small[:, 0, :], nD, AX_X, ALU.add))
                link(dve.tensor_scalar(small[:, 0, :], small[:, 0, :], 1.0 / D, None, ALU.mult))
                dve.tensor_tensor(nD, nD, small[:, 0, :].unsqueeze(2).to_broadcast([P, NB, D]), ALU.subtract)\
                    .then_inc(norm_centred, 1)
                dve.wait_ge(norm_squared, k + 1)
                dve.tensor_reduce(small[:, 1, :], nE, AX_X, ALU.add).then_inc(norm_var, 1)
                dve.wait_ge(norm_std, k + 1)
                link(dve.reciprocal(small[:, 3, :], small[:, 2, :]))
                return dve.tensor_tensor(to, nD, small[:, 3, :].unsqueeze(2).to_broadcast([P, NB, D]), ALU.mult)

            def take_out(name, dst_t, add_t):
                st = S[name]
                for g in range(GROUPS):
                    dve.wait_ge(st.mm, st.mm0 + g + 1)
                    dve.tensor_tensor(span(dst_t, g), banks[g % 4][:, 0:width(g)], span(add_t, g), ALU.add)\
                        .then_inc(st.out, 1)
                dve.wait_ge(st.out, st.end)

            def over_features(t):
                return t.unsqueeze(2).to_broadcast([P, NB, D])

            dve.wait_ge(map_in, 16)
            linear(pass_a)
            link(dve.tensor_reduce(indeg[:, :], acc[:, :, D:ACCW], AX_X, ALU.add))
            link(dve.tensor_scalar(invdeg[:, :], indeg[:, :], 1.0, None, ALU.max))
            link(dve.reciprocal(invdeg[:, :], invdeg[:, :]))
            link(dve.tensor_scalar(icnt[:, :, :], acc[:, :, D:ACCW], 1.0, None, ALU.max))
            link(dve.reciprocal(icnt[:, :, :], icnt[:, :, :]))
            dve.tensor_tensor(acc[:, :, 0:D], acc[:, :, 0:D], over_features(invdeg[:, :]), ALU.mult)\
                .then_inc(ready["aggT"], 1)
            dve.wait_ge(S["aggT"].out, S["aggT"].end)
            linear(pass_b)
            dve.tensor_tensor(acc[:, :, 0:D], acc[:, :, 0:D], over_features(invdeg[:, :]), ALU.mult)\
                .then_inc(ready["agg2T"], 1)
            take_out("o0", nD, nA)
            norm(0, nA).then_inc(ready["x1T"], 1)
            for L in layers:
                dve.wait_ge(S[f"uw{L.m}"].out, S[f"uw{L.m}"].end)
                message(L)
                backward(L)
                link(dve.tensor_tensor(small[:, 4, :], indeg[:, :], acc[:, :, HB - 1], ALU.add))
                dve.tensor_tensor(nE, ident[:, :].unsqueeze(1).to_broadcast([P, NB, D]),
                                  over_features(small[:, 4, :]), ALU.mult).then_inc(ready[f"accT{L.m}"], 1)
                take_out(f"new{L.m}", nC, nD)
                if L.m == 0:
                    dve.wait_ge(S["emb0"].out, S["emb0"].end)
            take_out("o1", nD, nA)
            norm(1, nA).then_inc(ready["x2T"], 1)
            dve.wait_ge(S["r2"].out, S["r2"].end)
            linear(pass_c)
            link(dve.tensor_tensor(nD, acc[:, :, 0:D], nC, ALU.add))
            link(norm(2, nD))
            link(dve.tensor_tensor(nD, nD, spread[:, 2, :].unsqueeze(1).to_broadcast([P, NB, D]), ALU.mult))
            link(dve.tensor_tensor(nD, nD, spread[:, 3, :].unsqueeze(1).to_broadcast([P, NB, D]), ALU.add))
            link(dve.scalar_tensor_tensor(out=nD, in0=nD, scalar=0.0, in1=nA, op0=ALU.max, op1=ALU.add))
            norm(3, nA).then_inc(ready["hT"], 1)
            linear(pass_d)
            dve.tensor_tensor(nC, acc[:, :, 0:D], nA, ALU.add).then_inc(ready["hT"], 1)
            dve.wait_ge(S["o3"].out, S["o3"].end)
            link(dve.tensor_tensor(nD, nD, nA, ALU.add))
            norm(4, nC).then_inc(out_done, 1)

        @block.tensor
        def _(pe):
            pe.wait_ge(consts, 8)
            pe.wait_ge(w_in, 16 * (2 + len(SPREAD)))
            for m in range(2):
                w1b = W(f"m{m}w1", D, D)
                pe.matmul(banks[1][:, m * D:(m + 1) * D], W("ew2t"), w1b, start=True, stop=True)
                row = banks[1][0:1, 256 + m * D:256 + (m + 1) * D]
                pe.matmul(row, W("eb2"), w1b, start=True, stop=False)
                last = pe.matmul(row, ones[0:1, 0:1], R(f"m{m}b1"), start=False, stop=True)
            last.then_inc(fold_mm, 1)
            for key in range(2):
                pe.wait_ge(rank_tot, key + 1)
                pe.matmul(banks[0][:, 0:NB], tri[:, :], small[:, 0, :], start=True, stop=True)
                pe.matmul(banks[0][:, 64:64 + NB], ones[:, :], small[:, 0, :], start=True, stop=True)\
                    .then_inc(rank_sum, 1)
            pe.wait_ge(ranked, 1)
            pe.wait_ge(folded, 1)

            def features(i, g):
                pe.wait_ge(ea_in[g], i * 16 + 16)
                pe.wait_ge(ea_turned_out, 1 + i * SORT_GROUPS + max(g - 1, 0))
                for k in range(2):
                    last = pe.transpose(banks[g % 2][:, k * P:(k + 1) * P],
                                        ea_sb[:, g, k * 2 * D_EDGE:(k + 1) * 2 * D_EDGE], ident[:, :])
                last.then_inc(ea_turned, 1)

            def hidden(i, g):
                pe.wait_ge(ea_turned_out, 1 + i * SORT_GROUPS + (g + 1))
                pe.wait_ge(e_hid_out, 1 + i * SORT_GROUPS + max(g - 1, 0))
                pe.matmul(banks[2 + g % 2][:, 0:2 * P], W("ewa"), ea_t[:, g % 2, :], start=True, stop=True)
                pe.matmul(banks[2 + g % 2][:, 2 * P:4 * P], W("ewb"), ea_t[:, g % 2, :], start=True, stop=True)\
                    .then_inc(e_hid, 1)

            def own_part(i, g):
                pe.wait_ge(e_hid_out, 1 + i * SORT_GROUPS + (g + 1))
                pe.wait_ge(rec_ready, 1 + i * SORT_GROUPS + max(g - 1, 0))
                for k in range(2):
                    for j in range(2):
                        last = pe.matmul(banks[4 + 2 * (g % 2) + k][:, j * EW:(j + 1) * EW],
                                         hid_sb[:, g % 2, (2 * k + j) * P:(2 * k + j + 1) * P], we2[:, :],
                                         start=True, stop=True)
                last.then_inc(e_mm, 1)

            def sort_body(i, prev):
                for g in range(SORT_GROUPS):
                    features(i, g)
                    if g:
                        own_part(i, g - 1)
                    elif prev is not None:
                        own_part(prev, SORT_GROUPS - 1)
                    hidden(i, g)

            sort_body(0, None)
            with pe.Fori(0, SORT_ITERS - 1) as j:
                sort_body(j + 1, j)
            own_part(SORT_ITERS - 1, SORT_GROUPS - 1)

            def groups(name, emit):
                st = S[name]
                before = list(S).index(name) - 1
                if before >= 0:
                    last_stage = list(S.values())[before]
                    pe.wait_ge(last_stage.out, last_stage.end)
                for g in range(st.groups):
                    if g >= 4:
                        pe.wait_ge(st.out, st.out0 + g - 3)
                    emit(g, banks[g % 4]).then_inc(st.mm, 1)

            def turn(name, src_t):
                def emit(g, bank):
                    for j, b in enumerate(blocks_of(g)):
                        last = pe.transpose(bank[:, j * P:(j + 1) * P], src_t[:, b, 0:D], ident[:, :])
                    return last
                groups(name, emit)

            def product(name, weight, in_t):
                groups(name, lambda g, bank: pe.matmul(bank[:, 0:width(g)], weight, span(in_t, g),
                                                       start=True, stop=True))

            def node_rows(name, parts, bias):
                def emit(g, bank):
                    for j, b in enumerate(blocks_of(g)):
                        o = bank[:, j * P:(j + 1) * P]
                        pe.matmul(o, ones[0:1, :], bias, start=True, stop=False)
                        for k, (in_t, weight) in enumerate(parts):
                            last = pe.matmul(o, in_t[:, b, :], weight, start=False, stop=k == len(parts) - 1)
                    return last
                groups(name, emit)

            def block_numbers(which, i):
                return nc.values_load_multi_w_load_instructions(
                    blkrow[0:1, which, bass.ds(i * BODY, BODY)], engines=PE_ENGINE, min_val=0, max_val=NB - 1,
                    skip_runtime_bounds_check_because="a chunk's block is a count of at most NB - 1 blocks")[1]

            def linear(p):
                with pe.Fori(0, ITERS) as i:
                    for n in range(PAIRS):
                        pe.wait_ge(p.onehot, i * PAIRS + (n + 1))
                        pe.wait_ge(p.added, 1 + i * BODY + 2 * max(n - 1, 0))
                        pe.wait_ge(p.gathered[n], i * 32 + (p.gathered0 + 32))
                        for k in range(2):
                            if p.counts:
                                pe.matmul(sum_ps[n % 2][:, k * 256 + D:k * 256 + ACCW], onehot[:, n % 4, k, :],
                                          types1h[:, bass.ds(i * BODY + (2 * n + k), 1), :]
                                          .rearrange("p a t -> p (a t)"), start=True, stop=True)
                            last = pe.matmul(sum_ps[n % 2][:, k * 256:k * 256 + D], onehot[:, n % 4, k, :],
                                             gat_sb[:, n, k, 0:D], start=True, stop=True)
                        last.then_inc(p.mm, 1)

            def message(L):
                def turned(n, count):
                    pe.wait_ge(L.onehot, count + 1)
                    if n:
                        pe.wait_ge(L.turned_out, 1 + count - 1)
                    for k in range(2):
                        last = pe.transpose(tr_ps[n % 2][:, k * P:(k + 1) * P], onehot[:, n % 4, k, :], ident[:, :])
                    last.then_inc(L.turned, 1)

                def local_part(i, n, blks):
                    pe.wait_ge(L.turned_out, 1 + i * PAIRS + (n + 1))
                    pe.wait_ge(L.summed, 1 + i * PAIRS + max(n - 3, 0))
                    for k in range(2):
                        last = pe.matmul(pre_ps[n % 4][:, k * 2 * D:(k + 1) * 2 * D],
                                         ot_sb[:, n % 4, k * P:(k + 1) * P],
                                         lt[:, bass.ds(blks[2 * n + k], 1), :].rearrange("p a f -> p (a f)"),
                                         start=True, stop=True)
                    last.then_inc(L.pre, 1)

                def sums(i, n, blks):
                    pe.wait_ge(L.relu, 1 + i * PAIRS + (n + 1))
                    pe.wait_ge(L.added, 1 + i * BODY + 2 * max(n - 1, 0))
                    for k in range(2):
                        if L.m == 0:
                            if k == 0:
                                pe.wait_ge(L.c6, 1 + i * BODY + 2 * max(n - 1, 0))
                            pe.matmul(sum_ps[n % 2][:, 256 + k * TYPES:256 + (k + 1) * TYPES],
                                      ot_sb[:, n % 4, k * P:(k + 1) * P],
                                      icnt[:, bass.ds(blks[2 * n + k], 1), :].rearrange("p a t -> p (a t)"),
                                      start=True, stop=True)
                        last = pe.matmul(sum_ps[n % 2][:, k * D:(k + 1) * D], onehot[:, n % 4, k, :],
                                         hf_sb[:, n % 2, k, :], start=True, stop=True)
                    last.then_inc(L.mm, 1)

                turned(0, 0)
                with pe.Fori(0, ITERS) as i:
                    blks = block_numbers(1, i)
                    for n in range(PAIRS):
                        turned(n + 1, i * PAIRS + (n + 1))
                        local_part(i, n, blks)
                        if n:
                            sums(i, n - 1, blks)
                    sums(i, PAIRS - 1, blks)

            def backward(L):
                pe.wait_ge(L.added, 1 + NCH)
                with pe.Fori(0, ITERS) as i:
                    for n in range(PAIRS):
                        if n % 4 == 3:
                            pe.wait_ge(L.b_onehot_dve, i * 2 + (n // 4 + 1))
                        else:
                            pe.wait_ge(L.b_onehot, 1 + i * (PAIRS - 2) + (n - n // 4 + 1))
                        pe.wait_ge(L.b_added, 1 + i * BODY + 2 * max(n - 1, 0))
                        for k in range(2):
                            last = pe.matmul(sum_ps[n % 2][:, k * 256:k * 256 + HB], onehot[:, n % 4, k, :],
                                             hb_in[:, n // 2, 2 * (n % 2) + k, :], start=True, stop=True)
                        last.then_inc(L.b_mm, 1)

            pe.wait_ge(x_in, 16)
            turn("xT", nA)
            linear(pass_a)
            pe.wait_ge(ready["aggT"], 1)
            turn("aggT", acc)
            pe.wait_ge(S["aggT"].out, S["aggT"].end)
            node_rows("h1", [(nC, W("w1l")), (nB, W("w1r"))], R("b1"))
            pe.wait_ge(S["h1"].out, S["h1"].end)
            turn("h1T", nD)
            linear(pass_b)
            pe.wait_ge(ready["agg2T"], 1)
            turn("agg2T", acc)
            pe.wait_ge(S["agg2T"].out, S["agg2T"].end)
            node_rows("o0", [(nC, W("w2l")), (nB, W("w2r"))], R("b2"))
            pe.wait_ge(ready["x1T"], 1)
            turn("x1T", nA)
            pe.wait_ge(S["x1T"].out, S["x1T"].end)
            product("nh", W("nw1"), nB)
            pe.wait_ge(S["nh"].out, S["nh"].end)
            product("emb", W("nw2"), nC)
            pe.wait_ge(S["emb"].out, S["emb"].end)
            for L in layers:
                m = L.m

                def emit(g, bank):
                    for j in range(min(2, NB - 2 * g)):
                        o = bank[:, j * 2 * D:(j + 1) * 2 * D]
                        pe.matmul(o[:, D:2 * D], ones[0:1, :], c_row[0:1, m, :], start=True, stop=False,
                                  skip_group_check=True)
                        pe.matmul(o[:, D:2 * D], nD[:, 2 * g + j, :], wca[:, m, 1, :], start=False, stop=True,
                                  skip_group_check=True)
                        last = pe.matmul(o[:, 0:D], nD[:, 2 * g + j, :], wca[:, m, 0, :], start=True, stop=True)
                    return last
                groups(f"uw{m}", emit)
                pe.wait_ge(S[f"uw{m}"].out, S[f"uw{m}"].end)
                message(L)
                backward(L)
                pe.wait_ge(ready[f"accT{m}"], 1)
                turn(f"accT{m}", acc)
                pe.wait_ge(S[f"accT{m}"].out, S[f"accT{m}"].end)

                def emit_new(g, bank):
                    pe.matmul(bank[:, 0:width(g)], W(f"m{m}w2"), span(nB, g), start=True, stop=False)
                    return pe.matmul(bank[:, 0:width(g)], spread[:, m, :], span(nE, g), start=False, stop=True)
                groups(f"new{m}", emit_new)
                pe.wait_ge(S[f"new{m}"].out, S[f"new{m}"].end)
                product(f"ah{m}", W("aw1"), nC)
                pe.wait_ge(S[f"ah{m}"].out, S[f"ah{m}"].end)
                if m == 0:
                    product("emb0", W("aw2"), nB)
                    pe.wait_ge(S["emb0"].out, S["emb0"].end)
                else:
                    node_rows("o1", [(nB, W("aw2"))], R("ab2"))
            pe.wait_ge(ready["x2T"], 1)
            turn("x2T", nA)
            pe.wait_ge(S["x2T"].out, S["x2T"].end)

            def emit_y(g, bank):
                b, h = divmod(g, 2)
                lo, hi = ((0, 4 * D), (4 * D, TYPES * D))[h]
                return pe.matmul(bank[:, 0:hi - lo], nB[:, b, :], W("wl", lo, hi - lo), start=True, stop=True)
            groups("y", emit_y)
            pe.wait_ge(S["y"].out, S["y"].end)
            node_rows("r2", [(nB, wrs[:, :])], l2_row[0:1, :])
            linear(pass_c)
            linear(pass_d)
            pe.wait_ge(ready["hT"], 2)
            turn("hT", nC)
            pe.wait_ge(S["hT"].out, S["hT"].end)
            node_rows("o3", [(nB, W("w3"))], R("b3"))


def kernel(**inputs):
    import numpy as np
    import concourse.bacc as bacc
    from concourse.bass_utils import run_bass_kernel_spmd

    a = {k: np.asarray(v) for k, v in inputs.items()}

    def edge_list(v, fill):
        flat = np.full(EPAD, fill, v.dtype)
        flat[:N_EDGES] = v
        return flat.reshape(P, EC)

    parts = {
        "w1l": a["L0_gnn_W1l"].T, "w1r": a["L0_gnn_W1r"].T, "w2l": a["L0_gnn_W2l"].T, "w2r": a["L0_gnn_W2r"].T,
        "ewa": a["L1_gnn_ew1"], "ewb": np.concatenate([np.zeros_like(a["L1_gnn_ew1"]), a["L1_gnn_ew1"]]),
        "ew2t": a["L1_gnn_ew2"].T, "w3": a["L3_gnn_W"].T,
        "wl": a["L2_gnn_W_l"].transpose(1, 0, 2).reshape(D, TYPES * D),
        "wr": a["L2_gnn_W_r"].transpose(1, 0, 2).reshape(D, TYPES * D),
    }
    for name in ("nw1", "nw2", "aw1", "aw2", "m0w2", "m1w2"):
        parts[name] = a["L1_gnn_" + name]
    for name in ("m0w1", "m1w1"):
        parts[name] = a["L1_gnn_" + name].reshape(3, D, D).transpose(1, 0, 2).reshape(D, 3 * D)
    for name in ("nb1", "nb2", "ab1", "ab2", "eb1", "eb2"):
        parts[name] = a["L1_gnn_" + name].reshape(D, 1)
    wpack = np.zeros((P, W_COLS), np.float32)
    for name, (lo, hi) in W_AT.items():
        wpack[:parts[name].shape[0], lo:hi] = parts[name]
    row_parts = {"b1": a["L0_gnn_b1"], "b2": a["L0_gnn_b2"], "ab2": a["L1_gnn_ab2"], "b3": a["L3_gnn_b"],
                 "m0b1": a["L1_gnn_m0b1"], "m1b1": a["L1_gnn_m1b1"], "m0b2": a["L1_gnn_m0b2"],
                 "m1b2": a["L1_gnn_m1b2"], "gamma": a["L2_gnn_gamma"], "beta": a["L2_gnn_beta"],
                 "lb": np.concatenate([a["L2_gnn_b"].reshape(-1), a["L2_gnn_emb"].reshape(-1)])}
    rows = np.zeros((1, R_COLS), np.float32)
    for name, (lo, hi) in R_AT.items():
        rows[0, lo:hi] = row_parts[name]
    x = np.zeros((NPAD, D), np.float32)
    x[:N_NODES] = a["x"]
    ea = np.zeros((EPAD, D_EDGE), np.float32)
    ea[:N_EDGES] = a["edge_attr_64"]
    arrays = {"src_in": edge_list(a["src"], NPAD), "dst_in": edge_list(a["dst"], NPAD),
              "type_in": edge_list(a["edge_type_6"], 0), "x_in_rows": x, "ea_in_rows": ea,
              "wpack_in": wpack, "rows_in": rows}
    nc = bacc.Bacc("TRN2", target_bir_lowering=False, num_devices=1)
    args = [nc.dram_tensor(n, v.shape, mybir.dt.from_np(v.dtype), kind="ExternalInput").ap()
            for n, v in arrays.items()]
    args.append(nc.dram_tensor("out_rows", (N_NODES, D), F32, kind="ExternalOutput").ap())
    gnn_kernel(nc, *args)
    r = run_bass_kernel_spmd(nc, [arrays], core_ids=[0])
    return r.results[0]["out_rows"]
```

```python
from contextlib import ExitStack

import concourse.bass as bass
from concourse import mybir
from concourse.alu_op_type import AluOpType as ALU

F32 = mybir.dt.float32
BF16 = mybir.dt.bfloat16
I32 = mybir.dt.int32
ACT = mybir.ActivationFunctionType
AX_X = mybir.AxisListType.X
DVE_ENGINE = (mybir.EngineType.DVE,)
PE_ENGINE = (mybir.EngineType.PE,)
SP_ENGINE = (mybir.EngineType.SP,)

P = 128
N_NODES = 3125
N_EDGES = 50000
D = 128
D_EDGE = 64
TYPES = 6
EPS = 1e-5
NB = -(-N_NODES // P)
NPAD = NB * P
SORT_GROUPS = 7
SORT_BODY = 4 * SORT_GROUPS
EC = -(-N_EDGES // P // SORT_BODY) * SORT_BODY
SORT_ITERS = EC // SORT_BODY
EPAD = EC * P
NCH = -(-(N_EDGES + NB * (P - 1)) // P // 32) * 32
NS = NCH * P
BODY = 16
HALF = BODY // 2
BACK_BODY = 2 * BODY
BACK_PAIRS = BACK_BODY // 2
QUADS = BACK_BODY // 4
BACK_ITERS = NCH // BACK_BODY
PAIRS = BODY // 2
ITERS = NCH // BODY
LASTI = ITERS - 1
FULL = -(-N_EDGES // P)
NCHX = NCH + BODY
FIELDS = 4
EW = 2 * D
REC = EW + FIELDS
HB = D + 2
ACCW = D + TYPES
ARENA = 36800
GROUPS = -(-NB // 4)
START = BODY
assert NCH % BODY == 0 and NCH % BACK_BODY == 0 and NCH // 4 <= P
assert NCH * P >= N_EDGES + NB * (P - 1) - (P - 1)

WEIGHTS = [("w1l", D), ("w1r", D), ("w2l", D), ("w2r", D), ("nw1", D), ("nw2", D), ("aw1", D), ("aw2", D),
           ("ewa", D), ("ewb", D), ("ew2t", D), ("w3", D), ("m0w1", 3 * D), ("m0w2", D), ("m1w1", 3 * D), ("m1w2", D),
           ("wl", TYPES * D), ("wr", TYPES * D), ("nb1", 1), ("nb2", 1), ("ab1", 1), ("ab2", 1), ("eb1", 1),
           ("eb2", 1)]
ROWS = [("b1", D), ("b2", D), ("ab2", D), ("b3", D), ("m0b1", D), ("m1b1", D), ("lb", 2 * TYPES * D),
        ("m0b2", D), ("m1b2", D), ("gamma", D), ("beta", D)]


def columns(parts):
    at, out = 0, {}
    for name, n in parts:
        out[name] = (at, at + n)
        at += n
    return out, at


W_AT, W_COLS = columns(WEIGHTS)
R_AT, R_COLS = columns(ROWS)
SPREAD = ["m0b2", "m1b2", "gamma", "beta"]


def gnn_kernel(nc, src, dst, etype, x, ea, wpack, rows, out):
    ctx = ExitStack()
    with ctx:
        def sb(name, shape, dt=F32):
            return ctx.enter_context(nc.sbuf_tensor(name, shape, dt))

        def sem(name):
            return ctx.enter_context(nc.semaphore(name))

        rec_dram = nc.dram_tensor("records", (NS + EPAD - N_EDGES, REC), F32).ap()
        hb_dram = nc.dram_tensor("backward_messages", (2 * NS, HB), F32).ap()
        h1_dram = nc.dram_tensor("table_h1", (NPAD, D), F32).ap()
        uw_dram = [nc.dram_tensor(f"table_uw{m}", (NPAD, 2 * D), F32).ap() for m in range(2)]
        y_dram = nc.dram_tensor("table_y", (NPAD * TYPES, D), F32).ap()
        x3_dram = nc.dram_tensor("table_x3", (NPAD, D), F32).ap()
        blk_dram = nc.dram_tensor("chunk_blocks", (2, NCH), I32).ap()
        rec_by_lane = rec_dram[0:NS, :].rearrange("(p c) r -> p c r", p=P)
        hb_by_lane = hb_dram[0:NS, :].rearrange("(p c) r -> p (c r)", p=P)
        hb_chunks = hb_dram[0:NS, :].rearrange("(p c) r -> p c r", p=P)

        w_sb = sb("weights", [P, W_COLS])
        r_sb = sb("bias_rows", [1, R_COLS])
        spread = sb("bias_spread", [P, len(SPREAD), D])

        def W(name, lo=0, n=None):
            a, b = W_AT[name]
            return w_sb[:, a + lo:(a + lo + n if n else b)]

        def R(name):
            a, b = R_AT[name]
            return r_sb[0:1, a:b]

        iota128 = sb("iota128", [P, P])
        ident = sb("ident", [P, P])
        tri = sb("tri", [P, P])
        ones = sb("ones_sq", [P, P])
        iota_b = sb("iota_blocks", [P, NB])
        iota_t = sb("iota_types", [P, TYPES])
        chunk_no = sb("chunk_no", [P, 4])
        eps_col = sb("eps_col", [P, 1])
        we2 = sb("edge_to_hidden", [P, EW])
        wca = sb("node_to_table", [P, 2, 2, D])
        c_row = sb("hidden_bias_rows", [1, 2, D])
        wrs = sb("wr_sum", [P, D])
        l2_row = sb("l2_bias_row", [1, D])
        start = sb("first_chunks", [P, 2, NB])
        last_chunk = sb("last_chunks", [P, 2, NB], I32)
        blkrow = sb("block_of_chunk", [1, 2, NCH], I32)
        dloc = sb("dst_local", [P, NCHX])
        sloc = sb("src_local", [P, NCHX])
        cw = sb("edge_weight", [P, NCHX])
        srcidx = sb("src_rows", [P, NCHX], I32)
        yidx = sb("y_rows", [P, NCHX], I32)
        posidx = sb("back_slots", [P, NCHX], I32)
        types1h = sb("types_onehot", [P, NCHX, TYPES])
        invdeg = sb("inv_degree", [P, NB])
        indeg = sb("in_degree", [P, NB])
        icnt = sb("inv_type_count", [P, NB, TYPES])
        srow = sb("sort_index_ring", [P, SORT_BODY], I32)
        gring = sb("gather_index_ring", [P, BODY], I32)
        pring = sb("scatter_index_ring", [P, BODY], I32)
        lane_row = sb("blank_slot_rows", [P, NCH])
        small = sb("small", [P, 8, NB])
        ints = sb("small_ints", [P, 2, NB], I32)

        arena = sb("arena", [P, ARENA])
        top = [0]

        def take(n):
            top[0] += n
            assert top[0] <= ARENA
            return arena[:, top[0] - n:top[0]]

        key_i = take(2 * EC).bitcast(I32).rearrange("p (k e) -> p k e", k=2)
        type_i = take(EC).bitcast(I32)
        tmp_i = take(2 * EC).bitcast(I32).rearrange("p (k e) -> p k e", k=2)
        fld = take(4 * EC).rearrange("p (k e) -> p k e", k=4)
        tmp_f = take(3 * EC).rearrange("p (k e) -> p k e", k=3)
        rec_row = take(EC).bitcast(I32)
        pad_row = take(EC)
        in_block = take(NB * EC)
        block_1h = in_block.bitcast(BF16).rearrange("p (k b e) -> p k b e", k=2, b=NB)
        key_block = take(EC).bitcast(BF16).rearrange("p (k e) -> p k e", k=2)
        running = take(NB * EC).rearrange("p (b e) -> p b e", b=NB)
        staging = take(SORT_BODY * REC).rearrange("p (e r) -> p e r", r=REC)
        ea_sb = take(SORT_BODY * D_EDGE).rearrange("p (g f) -> p g f", g=SORT_GROUPS)
        ea_t = take(2 * 2 * P).rearrange("p (n f) -> p n f", n=2)
        hid_sb = take(2 * 4 * P).rearrange("p (n f) -> p n f", n=2)
        rec_blank = take(REC)
        hb_blank = take(HB)
        c_spread = take(EW)

        top[0] = 0
        acc = take(NB * ACCW).rearrange("p (b f) -> p b f", b=NB)
        nodes = [take(NB * D).rearrange("p (b f) -> p b f", b=NB) for _ in range(4)]
        nA, nB, nC, nD = nodes
        gathered = take(PAIRS * 2 * 2 * D)
        gat_sb = gathered.rearrange("p (n k f) -> p n k f", n=PAIRS, k=2)
        nE = gathered[:, 0:NB * D].rearrange("p (b f) -> p b f", b=NB)
        table = take(NB * 2 * D)
        lt = table.rearrange("p (b f) -> p b f", b=NB)
        back_hot = gathered[:, 0:8 * 2 * P].rearrange("p (n k f) -> p n k f", n=8, k=2)
        back_sq = gathered[:, 8 * 2 * P:16 * 2 * P].rearrange("p (n f) -> p n f", n=8)
        acc_odd = table[:, 0:NB * HB].rearrange("p (b f) -> p b f", b=NB)
        y_ring = table[:, 0:8 * TYPES * D].rearrange("p (n f) -> p n f", n=8)
        onehot = take(4 * 2 * P).rearrange("p (n k f) -> p n k f", n=4, k=2)
        ot_sb = take(4 * 2 * P).rearrange("p (n f) -> p n f", n=4)
        pre = take(2 * 2 * (2 * D + 2)).rearrange("p (n k f) -> p n k f", n=2, k=2)
        hf_sb = take(2 * 2 * D).rearrange("p (n k f) -> p n k f", n=2, k=2)
        hb_sb = take(PAIRS * 2 * HB).rearrange("p (n k f) -> p n k f", n=PAIRS, k=2)
        e_sb = take(2 * HALF * D).rearrange("p (h c f) -> p h c f", h=2, f=D)
        fields_at = arena[:, top[0] - (PAIRS * 2 * HB + 2 * HALF * D):]
        meta = fields_at[:, 0:NCHX * FIELDS].rearrange("p (c r) -> p c r", r=FIELDS)
        mc_i = fields_at[:, NCHX * FIELDS:NCHX * FIELDS + NCH].bitcast(I32)
        mc_f = fields_at[:, NCHX * FIELDS + NCH:NCHX * FIELDS + 3 * NCH].rearrange("p (k c) -> p k c", k=2)
        hb_in = arena[:, top[0] - (PAIRS * 2 * HB + 2 * HALF * D):][:, 0:QUADS * 4 * HB]\
            .rearrange("p (q c r) -> p q c r", q=QUADS, r=HB)
        take(max(QUADS * 4 * HB - (PAIRS * 2 * HB + 2 * HALF * D), 0))
        c6 = take(2 * TYPES).rearrange("p (k t) -> p k t", k=2)

        def flat(node):
            return node.rearrange("p b f -> p (b f)")

        banks = [ctx.enter_context(nc.psum_tensor(f"bank{i}", [P, 512], F32)) for i in range(8)]
        tr_ps, pre_ps, sum_ps, back_ps = banks[0:2], banks[2:6], banks[6:8], banks[2:6]

        keys_in = sem("keys_in")
        x_in = sem("x_in")
        w_in = sem("w_in")
        consts = sem("consts")
        const_links = sem("const_links")
        blanks = sem("blanks")
        blanks_out = sem("blanks_out")
        hb_blanks_out = sem("hb_blanks_out")
        ends_ready = sem("ends_ready")
        rank_tot = sem("rank_tot")
        rank_sum = sem("rank_sum")
        slot_rows = sem("slot_rows")
        slot_sums = sem("slot_sums")
        map_ready = sem("map_ready")
        map_out = sem("map_out")
        map_in = sem("map_in")
        ranked = sem("ranked")
        ea_in = [sem(f"ea_in{g}") for g in range(SORT_GROUPS)]
        ea_turned = sem("ea_turned")
        ea_turned_out = sem("ea_turned_out")
        e_hid = sem("e_hid")
        e_hid_out = sem("e_hid_out")
        e_mm = sem("e_mm")
        rec_ready = sem("rec_ready")
        meta_in = sem("meta_in")
        fields_taken = sem("fields_taken")
        lane_rows = sem("lane_rows")
        sort_done = sem("sort_done")
        fold_mm = sem("fold_mm")
        folded = sem("folded")
        chain = sem("vector_chain")
        tables = sem("tables_stored")
        waits_passed = sem("waits_passed")
        y_out = [sem(f"y_out{h}") for h in range(8)]
        out_done = sem("out_done")

        stage_mm = sem("stage_matmuls")
        stage_out = {"act": sem("stage_taken_by_scalar"), "dve": sem("stage_taken_by_vector")}
        counted = {"mm": 0, "act": 0, "dve": 0}

        class Stage:
            def __init__(self, groups, taker):
                self.groups, self.mm, self.out = groups, stage_mm, stage_out[taker]
                self.mm0, self.out0 = counted["mm"], counted[taker]
                counted["mm"] += groups
                counted[taker] += groups
                self.end = self.out0 + groups

        TABLE_GROUPS = -(-NB // 2)
        S = {name: Stage(groups, taker) for name, groups, taker in [
            ("xT", GROUPS, "act"), ("aggT", GROUPS, "act"), ("h1", GROUPS, "act"),
            ("h1T", GROUPS, "act"), ("own_o0", GROUPS, "act"), ("agg2T", GROUPS, "act"),
            ("o0", GROUPS, "dve"), ("x1T", GROUPS, "act"), ("nh", GROUPS, "act"),
            ("emb", GROUPS, "act"),
            ("uw0", TABLE_GROUPS, "act"), ("accT0", GROUPS, "act"), ("new0", GROUPS, "dve"),
            ("ah0", GROUPS, "act"), ("emb0", GROUPS, "act"),
            ("uw1", TABLE_GROUPS, "act"), ("accT1", GROUPS, "act"), ("new1", GROUPS, "dve"),
            ("ah1", GROUPS, "act"), ("o1", GROUPS, "dve"),
            ("x2T", GROUPS, "act"), ("y", 2 * NB, "act"), ("r2", GROUPS, "act"), ("hT", GROUPS, "act"),
            ("o3", GROUPS, "act")]}
        ready = {name: sem(name + "_ready") for name in
                 ["aggT", "agg2T", "x1T", "accT0", "accT1", "x2T", "hT"]}

        def blocks_of(g):
            return range(4 * g, min(4 * g + 4, NB))

        def width(g):
            return P * len(blocks_of(g))

        def span(t, g):
            return flat(t)[:, 512 * g:512 * g + width(g)]

        gathered_into = [sem(f"gathered_into{n}") for n in range(PAIRS)]
        sent_from = [sem(f"sent_from{n}") for n in range(PAIRS)]
        PER_PASS = 32 * ITERS
        rec_out = [[sent_from[g]] for g in range(SORT_GROUPS - 1)] + [sent_from[SORT_GROUPS - 1:SORT_GROUPS + 1]]
        assert SORT_GROUPS + 1 == PAIRS

        def per_body(g):
            return 16 * 4 // len(rec_out[g])

        class Linear:
            def __init__(self, name, number, rows_dram, index, counts=False, weighted=False, stored=0):
                self.gathered0 = number * PER_PASS
                self.rows, self.index, self.counts, self.weighted = rows_dram, index, counts, weighted
                self.stored = stored
                self.width = ACCW if counts else D
                self.idx_ready = sem(name + "_index_ready")
                self.gathered = gathered_into
                self.onehot = sem(name + "_onehot")
                self.mm = sem(name + "_mm")
                self.added = sem(name + "_added")

        class Message:
            def __init__(self, m, stored):
                self.m, self.stored = m, stored
                self.idx_ready, self.pos_ready = sem(f"m{m}_index_ready"), sem(f"m{m}_slots_ready")
                self.gathered, self.gathered0 = gathered_into, (2 + m) * PER_PASS
                self.sent = sent_from
                self.sent0 = [per_body(min(n, SORT_GROUPS - 1)) * SORT_ITERS + m * PER_PASS for n in range(PAIRS)]
                self.loaded = [sem(f"m{m}_loaded{h}") for h in range(2)]
                self.onehot = sem(f"m{m}_onehot")
                self.turned = sem(f"m{m}_turned")
                self.turned_out = sem(f"m{m}_turned_out")
                self.pre = sem(f"m{m}_pre")
                self.half = sem(f"m{m}_half_summed")
                self.summed = sem(f"m{m}_summed")
                self.relu = sem(f"m{m}_relu")
                self.mm = sem(f"m{m}_mm")
                self.added = sem(f"m{m}_added")
                self.c6 = sem(f"m{m}_c6")
                self.b_in = [sem(f"b{m}_in{q}") for q in range(QUADS)]
                self.b_onehot = {who: sem(f"b{m}_onehot_{who}") for who in ("act", "pool", "dve")}
                self.b_squares = sem(f"b{m}_squares")
                self.b_mm = sem(f"b{m}_mm")
                self.b_added = sem(f"b{m}_added")

        HOT_BY = {"act": range(0, BACK_PAIRS, 2), "dve": range(7, BACK_PAIRS, 8),
                  "pool": [n for n in range(1, BACK_PAIRS, 2) if n % 8 != 7]}

        def hot_count(who, i, n):
            return i * len(HOT_BY[who]) + (HOT_BY[who].index(n) + 1)

        TABLE_PARTS = [(g, min(g + 2, GROUPS)) for g in range(0, GROUPS, 2)]
        STORED = 16 * len(TABLE_PARTS)
        pass_a = Linear("a", 0, x, srcidx, counts=True)
        pass_b = Linear("b", 1, h1_dram, srcidx, stored=STORED)
        layers = [Message(0, 3 * STORED), Message(1, 5 * STORED)]
        pass_c = Linear("c", 4, y_dram, yidx, weighted=True, stored=5 * STORED)
        pass_d = Linear("d", 5, x3_dram, srcidx, stored=6 * STORED)
        acc_clear = {p: sem(f"clear{k}") for k, p in enumerate([pass_a, pass_b, *layers, pass_c, pass_d])}

        norm_mean = sem("norm_mean")
        norm_var, norm_std = sem("norm_var"), sem("norm_std")

        counters = [ea_turned_out, e_hid_out, rec_ready, e_hid, e_mm]
        for p in [pass_a, pass_b, pass_c, pass_d]:
            counters += [p.added, p.mm]
        for L in layers:
            counters += [L.added, L.mm, L.c6, L.relu, L.summed, L.turned_out, L.b_added, L.b_mm, *L.b_onehot.values()]

        block = ctx.enter_context(nc.Block())

        @block.sync
        def _(sp):
            sp.dma_start(key_i[:, 0, :], src).then_inc(keys_in, 16)
            sp.dma_start(key_i[:, 1, :], dst).then_inc(keys_in, 16)
            sp.dma_start(type_i, etype).then_inc(keys_in, 16)
            sp.dma_start(w_sb[:, :], wpack).then_inc(w_in, 16)
            sp.dma_start(r_sb[:, :], rows).then_inc(w_in, 16)
            for k, name in enumerate(SPREAD):
                a, b = R_AT[name]
                sp.dma_start(spread[:, k, :], rows[0:1, a:b].to_broadcast([P, D])).then_inc(w_in, 16)
            sp.wait_ge(blanks, 3)
            sp.dma_start(rec_by_lane[:, FULL:NCH, :], rec_blank.unsqueeze(1).to_broadcast([P, NCH - FULL, REC]))\
                .then_inc(blanks_out, 16)

            def blank_last_chunks(chunks, blank, key, done):
                sp.wait_ge(done, 16)
                with sp.Fori(0, NB) as b:
                    chunk = nc.values_load(last_chunk[0:1, key, bass.ds(b, 1)], engines=SP_ENGINE,
                                           min_val=0, max_val=NCH - 1,
                                           skip_runtime_bounds_check_because="a chunk's number")
                    sp.dma_start(chunks[:, bass.ds(chunk, 1), :], blank.unsqueeze(1)).then_inc(done, 16)

            def load_features(g, col):
                sp.dma_start(ea_sb[:, g, :],
                             ea.rearrange("(p e) f -> p (e f)", p=P)[:, bass.ds(col, 4 * D_EDGE)])\
                    .then_inc(ea_in[g], 16)

            for g in range(SORT_GROUPS):
                load_features(g, g * 4 * D_EDGE)
            sp.dma_start(hb_chunks[:, FULL:NCH, :], hb_blank.unsqueeze(1).to_broadcast([P, NCH - FULL, HB]))\
                .then_inc(hb_blanks_out, 16)
            sp.wait_ge(ends_ready, 1)
            blank_last_chunks(rec_by_lane, rec_blank, 1, blanks_out)
            sp.wait_ge(ends_ready, 2)
            blank_last_chunks(hb_chunks, hb_blank, 0, hb_blanks_out)
            with sp.Fori(0, SORT_ITERS - 1) as i:
                for g in range(SORT_GROUPS):
                    sp.wait_ge(ea_turned, i * SORT_GROUPS + (g + 1))
                    load_features(g, (i + 1) * (SORT_BODY * D_EDGE) + g * 4 * D_EDGE)
            sp.wait_ge(map_ready, 2)
            for k in range(2):
                sp.dma_start(blk_dram[k].rearrange("(q c) -> q c", c=4),
                             ints[0:NCH // 4, k, 0:4]).then_inc(map_out, 16)
            sp.wait_ge(map_out, 32)
            sp.dma_start(blkrow[0:1, :, :], blk_dram.rearrange("(a k) c -> a k c", a=1)).then_inc(map_in, 16)
            for g in range(SORT_GROUPS):
                for sent in rec_out[g]:
                    sp.wait_ge(sent, per_body(g) * SORT_ITERS)

            def load_fields(to, chunk):
                sp.dma_start(meta[:, bass.ds(to, BODY), :], rec_by_lane[:, bass.ds(chunk, BODY), EW:REC])\
                    .then_inc(meta_in, 16)

            load_fields(0, 0)
            sp.wait_ge(sort_done, 1)
            sp.wait_ge(hb_blanks_out, 16 * (NB + 1))
            sp.dma_start(nA, x.rearrange("(b p) f -> p b f", p=P)).then_inc(x_in, 16)
            with sp.Fori(0, LASTI) as i:
                sp.wait_ge(fields_taken, i + 1)
                load_fields((i + 1) * BODY, (i + 1) * BODY)
            sp.wait_ge(fields_taken, ITERS)
            load_fields(NCH, NCH - BODY)
            for g0, g1 in TABLE_PARTS:
                b = slice(4 * g0, min(4 * g1, NB))
                sp.wait_ge(S["h1"].out, S["h1"].out0 + g1)
                sp.dma_start(h1_dram.rearrange("(b p) f -> p b f", p=P)[:, b, :], nD[:, b, :]).then_inc(tables, 16)
            for L in layers:
                table_v = uw_dram[L.m].rearrange("(b p) f -> p b f", p=P)
                for g0, g1 in TABLE_PARTS:
                    b = slice(4 * g0, min(4 * g1, NB))
                    sp.wait_ge(S[f"uw{L.m}"].out, S[f"uw{L.m}"].out0 + min(2 * g1, TABLE_GROUPS))
                    sp.dma_start(table_v[:, b, 0:D], lt[:, b, D:2 * D]).then_inc(tables, 16)
                    sp.dma_start(table_v[:, b, D:2 * D], lt[:, b, 0:D]).then_inc(tables, 16)

                def load_half(h, chunk):
                    sp.dma_start(e_sb[:, h, :, :], rec_by_lane[:, bass.ds(chunk, HALF), L.m * D:(L.m + 1) * D])\
                        .then_inc(L.loaded[h], 16)

                for h in range(2):
                    load_half(h, h * HALF)
                with sp.Fori(0, LASTI) as i:
                    for h in range(2):
                        sp.wait_ge(L.half, i * PAIRS + (4 * h + 4))
                        load_half(h, (i + 1) * BODY + h * HALF)

                for n in range(PAIRS):
                    sp.wait_ge(L.sent[n], L.sent0[n] + PER_PASS)

                def load_quad(q, col):
                    sp.dma_start(hb_in[:, q, :, :].rearrange("p c r -> p (c r)"),
                                 hb_by_lane[:, bass.ds(col, 4 * HB)]).then_inc(L.b_in[q], 16)

                for q in range(QUADS):
                    load_quad(q, q * 4 * HB)
                with sp.Fori(0, BACK_ITERS - 1) as i:
                    for q in range(QUADS):
                        sp.wait_ge(L.b_mm, START + i * BACK_PAIRS + (2 * q + 2))
                        load_quad(q, (i + 1) * (BACK_BODY * HB) + q * 4 * HB)
            y_v = y_dram.rearrange("(b p t) f -> p b (t f)", p=P, t=TYPES)
            for b in range(NB):
                sp.wait_ge(S["y"].out, S["y"].out0 + 2 * b + 2)
                sp.dma_start(y_v[:, b, :], y_ring[:, b % 8, :]).then_inc(y_out[b % 8], 16)
            for g0, g1 in TABLE_PARTS:
                b = slice(4 * g0, min(4 * g1, NB))
                sp.wait_ge(ready["hT"], g1)
                sp.dma_start(x3_dram.rearrange("(b p) f -> p b f", p=P)[:, b, :], nA[:, b, :]).then_inc(tables, 16)
            sp.wait_ge(out_done, GROUPS)
            full = N_NODES // P
            sp.dma_start(out[0:full * P, :].rearrange("(b p) f -> p b f", p=P), nC[:, 0:full, :])\
                .then_inc(out_done, 16)
            sp.dma_start(out[full * P:N_NODES, :], nC[0:N_NODES - full * P, full, :]).then_inc(out_done, 16)
            sp.wait_ge(out_done, GROUPS + 32)

        @block.gpsimd
        def _(pool):
            pool.memset(ones[:, :], 1.0).then_inc(const_links, 1)
            pool.memset(ident[:, :], 0.0).then_inc(const_links, 1)
            pool.memset(rec_blank, 0.0).then_inc(const_links, 1)
            pool.memset(hb_blank, 0.0).then_inc(const_links, 1)
            pool.memset(eps_col[:, :], EPS).then_inc(consts, 1)
            pool.iota(iota128[:, :], [[1, P]], base=0, channel_multiplier=0,
                      allow_small_or_imprecise_dtypes=True).then_inc(consts, 1)
            pool.iota(iota_b[:, :], [[1, NB]], base=0, channel_multiplier=0,
                      allow_small_or_imprecise_dtypes=True).then_inc(consts, 1)
            pool.iota(iota_t[:, :], [[1, TYPES]], base=0, channel_multiplier=0,
                      allow_small_or_imprecise_dtypes=True).then_inc(consts, 1)
            pool.iota(chunk_no[:, :], [[1, 4]], base=0, channel_multiplier=4,
                      allow_small_or_imprecise_dtypes=True).then_inc(consts, 1)
            pool.iota(pad_row, [[1, EC]], base=0, channel_multiplier=EC,
                      allow_small_or_imprecise_dtypes=True).then_inc(consts, 1)
            pool.iota(lane_row[:, :], [[1, NCH]], base=NS, channel_multiplier=NCH,
                      allow_small_or_imprecise_dtypes=True).then_inc(lane_rows, 1)
            pool.wait_ge(const_links, 4)
            pool.memset(rec_blank[:, EW + 1:EW + 2], -1.0).then_inc(blanks, 1)
            pool.memset(hb_blank[:, D:D + 1], -1.0).then_inc(blanks, 1)
            pool.affine_select(out=ident[:, :], in_=ident[:, :], compare_op=ALU.not_equal, fill=1.0,
                               base=0, pattern=[[-1, P]], channel_multiplier=1).then_inc(consts, 1)
            pool.affine_select(out=tri[:, :], in_=ones[:, :], compare_op=ALU.is_ge, fill=0.0,
                               base=-1, pattern=[[1, P]], channel_multiplier=-1).then_inc(consts, 1)
            pool.memset(small[:, 7, :], 1.0).then_inc(blanks, 1)

            def passed():
                pool.sem_inc(waits_passed, 1)

            for counter in counters:
                pool.sem_inc(counter, START)
            pool.wait_ge(blanks_out, 16 * (NB + 1))
            with pool.Fori(0, SORT_ITERS) as i:
                for g in range(SORT_GROUPS):
                    pool.wait_ge(rec_ready, START + i * SORT_GROUPS + (g + 1))
                    passed()
                    for e in range(4 * g, 4 * g + 4):
                        pool.indirect_dma_start(
                            out=rec_dram, out_offset=bass.IndirectOffsetOnAxis(ap=srow[:, e:e + 1], axis=0),
                            in_=staging[:, e, :], in_offset=None).then_inc(rec_out[g][e % len(rec_out[g])], 16)

            def gather(p, rows, n, wide):
                for k in range(2):
                    pool.indirect_dma_start(
                        out=gat_sb[:, n, k, 0:wide], out_offset=None, in_=rows,
                        in_offset=bass.IndirectOffsetOnAxis(ap=gring[:, 2 * n + k:2 * n + k + 1], axis=0))\
                        .then_inc(p.gathered[n], 16)

            def linear(p):
                if p.stored:
                    pool.wait_ge(tables, p.stored)

                def body(i, prev):
                    for n in range(PAIRS):
                        if n % 4 == 0:
                            pool.wait_ge(p.idx_ready, i * 2 + (n // 4 + 1))
                            passed()
                        if prev is not None:
                            pool.wait_ge(p.mm, START + prev * PAIRS + (n + 1))
                            passed()
                        gather(p, p.rows, n, D)

                body(0, None)
                with pool.Fori(0, LASTI) as j:
                    body(j + 1, j)

            def message(L):
                def send(n, i):
                    if n % 4 == 0:
                        pool.wait_ge(L.pos_ready, i * 2 + (n // 4 + 1))
                        passed()
                    pool.wait_ge(L.relu, START + i * PAIRS + (n + 1))
                    passed()
                    for k in range(2):
                        pool.indirect_dma_start(
                            out=hb_dram,
                            out_offset=bass.IndirectOffsetOnAxis(ap=pring[:, 2 * n + k:2 * n + k + 1], axis=0),
                            in_=hb_sb[:, n, k, :], in_offset=None).then_inc(L.sent[n], 16)

                def body(i, prev):
                    for n in range(PAIRS):
                        if n % 4 == 0:
                            pool.wait_ge(L.idx_ready, i * 2 + (n // 4 + 1))
                            passed()
                        if prev is not None:
                            pool.wait_ge(L.summed, START + prev * PAIRS + (n + 1))
                            passed()
                        gather(L, uw_dram[L.m], n, 2 * D)
                        if n >= 3:
                            send(n - 3, i)
                        elif prev is not None:
                            send(n + 5, prev)

                pool.wait_ge(tables, L.stored)
                body(0, None)
                with pool.Fori(0, LASTI) as j:
                    body(j + 1, j)
                for n in range(5, PAIRS):
                    send(n, LASTI)

            def onehots_by_source(L):
                pool.wait_ge(L.mm, START + NCH // 2)
                pool.wait_ge(L.onehot, NCH // 2 + 2)
                with pool.Fori(0, BACK_ITERS) as i:
                    for n in HOT_BY["pool"]:
                        pool.wait_ge(L.b_in[n // 2], i * 16 + 16)
                        pool.wait_ge(L.b_mm, START + i * BACK_PAIRS + (n - 7))
                        passed()
                        for k in range(2):
                            last = pool.tensor_scalar(back_hot[:, n % 8, k, :], iota128[:, :],
                                                      hb_in[:, n // 2, 2 * (n % 2) + k, D:D + 1], None, ALU.is_equal)
                        last.then_inc(L.b_onehot["pool"], 1)

            linear(pass_a)
            linear(pass_b)
            for L in layers:
                message(L)
                onehots_by_source(L)
            for h in range(8):
                pool.wait_ge(y_out[h], 16 * len(range(h, NB, 8)))
            linear(pass_c)
            linear(pass_d)

        @block.scalar
        def _(act):
            def evacuate(name, dst_t, func=ACT.Copy, bias=None):
                st = S[name]
                for g in range(GROUPS):
                    act.wait_ge(st.mm, st.mm0 + g + 1)
                    src_ps = banks[g % 4][:, 0:width(g)]
                    if bias is None:
                        act.activation(span(dst_t, g), src_ps, func).then_inc(st.out, 1)
                    else:
                        act.activation(span(dst_t, g), src_ps, func, bias=bias).then_inc(st.out, 1)

            def onehots_by_source(L):
                mine = HOT_BY["act"]

                def scratch(at, k):
                    return back_sq[:, at, k * P:(k + 1) * P]

                def squares(i, at):
                    n = mine[at]
                    act.wait_ge(L.b_onehot["act"], START + i * len(mine) + (at - 3))
                    act.wait_ge(L.b_in[n // 2], i * 16 + 16)
                    for k in range(2):
                        last = act.activation(scratch(at, k), iota128[:, :], ACT.Square,
                                              scale=-1.0, bias=hb_in[:, n // 2, 2 * (n % 2) + k, D:D + 1])
                    last.then_inc(L.b_squares, 1)

                def relu_of(i, at):
                    n = mine[at]
                    act.wait_ge(L.b_squares, i * len(mine) + (at + 1))
                    act.wait_ge(L.b_mm, START + i * BACK_PAIRS + (n - 7))
                    act.activation(back_hot[:, n % 8, :, :].rearrange("p k f -> p (k f)"), back_sq[:, at, :],
                                   ACT.Relu, scale=-1.0, bias=ones[:, 0:1]).then_inc(L.b_onehot["act"], 1)

                act.wait_ge(L.mm, START + NCH // 2)
                act.wait_ge(L.onehot, NCH // 2 + 2)
                act.wait_ge(L.turned, NCH // 2 + 1)
                with act.Fori(0, BACK_ITERS) as i:
                    for at in range(len(mine)):
                        squares(i, at)
                        if at:
                            relu_of(i, at - 1)
                    relu_of(i, len(mine) - 1)

            def norm(k):
                for g in range(GROUPS):
                    act.wait_ge(norm_mean, k * GROUPS + g + 1)
                    for b in blocks_of(g):
                        last = act.activation(nE[:, b, :], nD[:, b, :], ACT.Square, bias=small[:, 0, b:b + 1],
                                              accum_out=small[:, 1, b:b + 1])
                last.then_inc(norm_var, 1)
                act.wait_ge(norm_var, k + 1)
                act.activation(small[:, 6, :], small[:, 1, :], ACT.Sqrt, bias=eps_col[:, 0:1],
                               scale=1.0 / D).then_inc(norm_std, 1)

            act.wait_ge(consts, 8)
            act.wait_ge(w_in, 16 * (2 + len(SPREAD)))
            act.wait_ge(fold_mm, 1)
            for m in range(2):
                act.activation(wca[:, m, 0, :], W(f"m{m}w1", 2 * D, D), ACT.Copy)
                act.activation(wca[:, m, 1, :], W(f"m{m}w1", 0, D), ACT.Copy)
                act.activation(c_row[0:1, m, :], banks[1][0:1, 256 + m * D:256 + (m + 1) * D], ACT.Copy)
            act.activation(we2[:, :], banks[1][:, 0:EW], ACT.Copy).then_inc(folded, 1)
            act.wait_ge(fold_mm, 2)
            act.activation(c_spread, banks[6][:, 0:EW], ACT.Copy).then_inc(folded, 1)

            def features_out(i, g):
                act.wait_ge(ea_turned, i * SORT_GROUPS + (g + 1))
                act.wait_ge(e_hid, START + i * SORT_GROUPS + max(g - 1, 0))
                act.activation(ea_t[:, g % 2, :], banks[g % 2][:, 0:2 * P], ACT.Copy).then_inc(ea_turned_out, 1)

            def hidden_out(i, g):
                act.wait_ge(e_hid, START + i * SORT_GROUPS + (g + 1))
                act.wait_ge(e_mm, START + i * SORT_GROUPS + max(g - 1, 0))
                act.activation(hid_sb[:, g % 2, :], banks[2 + g % 2][:, :], ACT.Relu, bias=W("eb1"))\
                    .then_inc(e_hid_out, 1)

            with act.Fori(0, SORT_ITERS) as i:
                for g in range(SORT_GROUPS):
                    features_out(i, g)
                    hidden_out(i, g)

            evacuate("xT", nB)
            evacuate("aggT", nC)
            evacuate("h1", nD, ACT.Relu)
            evacuate("h1T", nB)
            act.wait_ge(tables, STORED)
            evacuate("own_o0", nD)
            evacuate("agg2T", nC)
            norm(0)
            evacuate("x1T", nB)
            evacuate("nh", nC, ACT.Relu, W("nb1"))
            evacuate("emb", nD, ACT.Identity, W("nb2"))
            for L in layers:
                m = L.m
                st = S[f"uw{m}"]
                for g in range(st.groups):
                    n = min(2, NB - 2 * g)
                    act.wait_ge(st.mm, st.mm0 + g + 1)
                    act.activation(lt[:, 2 * g:2 * g + n, :].rearrange("p b f -> p (b f)"),
                                   banks[g % 4][:, 0:n * 2 * D], ACT.Copy).then_inc(st.out, 1)

                def turned_out(n, count):
                    act.wait_ge(L.turned, count + 1)
                    act.activation(ot_sb[:, n % 4, :], tr_ps[n % 2][:, 0:2 * P], ACT.Copy)\
                        .then_inc(L.turned_out, 1)

                def relu(i, n):
                    act.wait_ge(L.summed, START + i * PAIRS + (n + 1))
                    act.wait_ge(L.mm, START + i * PAIRS + (n - 1))
                    act.wait_ge(L.sent[n], i * 32 + L.sent0[n])
                    act.activation(hf_sb[:, n % 2, :, :], pre[:, n % 2, :, 0:D], ACT.Relu)
                    act.activation(hb_sb[:, n, :, :], pre[:, n % 2, :, D:2 * D + 2], ACT.Relu)\
                        .then_inc(L.relu, 1)

                turned_out(0, 0)
                with act.Fori(0, ITERS) as i:
                    for n in range(PAIRS):
                        act.wait_ge(L.mm, START + i * PAIRS + (n - 2))
                        turned_out(n + 1, i * PAIRS + (n + 1))
                        if n:
                            relu(i, n - 1)
                    relu(i, PAIRS - 1)
                onehots_by_source(L)
                evacuate(f"accT{m}", nB)
                evacuate(f"ah{m}", nB, ACT.Relu, W("ab1"))
                if m == 0:
                    evacuate("emb0", nD, ACT.Identity, W("ab2"))
            norm(1)
            evacuate("x2T", nB)
            st = S["y"]
            for b in range(NB):
                if b >= 8:
                    act.wait_ge(y_out[b % 8], 16 * (b // 8))
                for h, (lo, hi) in enumerate(((0, 4 * D), (4 * D, TYPES * D))):
                    act.wait_ge(st.mm, st.mm0 + 2 * b + h + 1)
                    act.activation(y_ring[:, b % 8, lo:hi], banks[(2 * b + h) % 4][:, 0:hi - lo], ACT.Copy)\
                        .then_inc(st.out, 1)
            evacuate("r2", nC)
            norm(2)
            norm(3)
            evacuate("hT", nB)
            evacuate("o3", nD, ACT.Relu)
            norm(4)

        @block.vector
        def _(dve):
            links = [0]

            def link(ins):
                links[0] += 1
                ins.then_inc(chain, 1)
                dve.wait_ge(chain, links[0])

            dve.wait_ge(consts, 8)
            dve.wait_ge(blanks, 3)
            dve.wait_ge(keys_in, 48)
            link(dve.tensor_scalar(tmp_f[:, 0, :], pad_row, float(N_EDGES), None, ALU.is_ge))
            link(dve.tensor_scalar(pad_row, pad_row, float(NS - N_EDGES), None, ALU.add))
            link(dve.tensor_tensor(pad_row, pad_row, tmp_f[:, 0, :], ALU.mult))
            link(dve.tensor_copy(fld[:, 0, :], key_i[:, 0, :]))
            link(dve.tensor_copy(fld[:, 2, :], type_i))
            link(dve.tensor_scalar(tmp_i[:, 0, :], key_i[:, 1, :], P - 1, None, ALU.bitwise_and))
            link(dve.tensor_copy(fld[:, 1, :], tmp_i[:, 0, :]))

            def blocks_of_edges(key):
                link(dve.tensor_scalar(tmp_i[:, key, :], key_i[:, key, :], 7, None, ALU.arith_shift_right))
                link(dve.tensor_copy(key_block[:, key, :], tmp_i[:, key, :]))
                for b in range(NB):
                    dve.tensor_scalar(block_1h[:, key, b, :], key_block[:, key, :], float(b), 0.0,
                                      ALU.is_equal, ALU.add, accum_out=totals[:, b:b + 1]).then_inc(rank_tot, 1)

            def ranks(turn, key):
                dve.wait_ge(rank_tot, (turn + 1) * NB)
                line = [P, NB * EC]
                link(dve.tensor_tensor_scan(running.rearrange("p b e -> p (b e)"), ones[:, 0:1].to_broadcast(line),
                                            block_1h[:, key, :, :].rearrange("p b e -> p (b e)"),
                                            0.0, ALU.mult, ALU.add))
                link(dve.tensor_tensor_scan(upto, small[:, 7, :], totals, 0.0, ALU.mult, ALU.add))
                link(dve.tensor_tensor(upto, upto, totals, ALU.subtract))
                dve.wait_ge(rank_sum, turn + 1)
                before, whole = banks[7][:, 0:NB], banks[7][:, 64:64 + NB]
                link(dve.tensor_scalar(nch, whole, float(P - 1), None, ALU.add))
                link(dve.tensor_copy(ints[:, 0, :], nch))
                link(dve.tensor_scalar(ints[:, 1, :], ints[:, 0, :], 7, None, ALU.arith_shift_right))
                link(dve.tensor_copy(nch, ints[:, 1, :]))
                link(dve.tensor_tensor_scan(first, small[:, 7, :], nch, 0.0, ALU.mult, ALU.add))
                link(dve.tensor_scalar(small[:, 5, :], first, -1.0, 0.0, ALU.add, ALU.max))
                dve.tensor_copy(last_chunk[:, key, :], small[:, 5, :]).then_inc(ends_ready, 1)
                link(dve.tensor_tensor(start[:, key, :], first, nch, ALU.subtract))
                link(dve.scalar_tensor_tensor(out=first, in0=start[:, key, :], scalar=float(P), in1=before,
                                              op0=ALU.mult, op1=ALU.add))
                link(dve.scalar_tensor_tensor(out=first, in0=first, scalar=-1.0, in1=upto,
                                              op0=ALU.add, op1=ALU.subtract))
                for b in range(NB):
                    dve.scalar_tensor_tensor(out=running[:, b, :], in0=running[:, b, :], scalar=first[:, b:b + 1],
                                             in1=block_1h[:, key, b, :], op0=ALU.add, op1=ALU.mult)\
                        .then_inc(slot_rows, 1)

            def slots(turn):
                dve.wait_ge(slot_sums, turn + 1)
                link(dve.tensor_copy(tmp_i[:, 0, :], banks[6][:, 0:EC]))
                link(dve.tensor_scalar(tmp_i[:, 1, :], tmp_i[:, 0, :], P - 1, None, ALU.bitwise_and))
                link(dve.tensor_copy(tmp_f[:, 1, :], tmp_i[:, 1, :]))
                link(dve.tensor_scalar(tmp_i[:, 1, :], tmp_i[:, 0, :], 7, None, ALU.arith_shift_right))
                link(dve.tensor_copy(tmp_f[:, 2, :], tmp_i[:, 1, :]))
                link(dve.scalar_tensor_tensor(out=tmp_f[:, 0, :], in0=tmp_f[:, 1, :], scalar=float(NCH),
                                              in1=tmp_f[:, 2, :], op0=ALU.mult, op1=ALU.add))

            totals, nch, first, upto = (small[:, k, :] for k in range(4))
            blocks_of_edges(1)
            ranks(0, 1)
            blocks_of_edges(0)
            slots(0)
            link(dve.tensor_tensor(tmp_f[:, 0, :], tmp_f[:, 0, :], pad_row, ALU.add))
            link(dve.tensor_copy(rec_row, tmp_f[:, 0, :]))
            ranks(1, 0)
            slots(1)
            dve.tensor_copy(fld[:, 3, :], tmp_f[:, 0, :]).then_inc(ranked, 1)
            dve.wait_ge(ranked, 1)

            def make_records(i, prev):
                for g in range(SORT_GROUPS):
                    if prev is not None:
                        for sent in rec_out[g]:
                            dve.wait_ge(sent, prev * per_body(g) + per_body(g))
                    dve.tensor_copy(srow[:, 4 * g:4 * g + 4], rec_row[:, bass.ds(i * SORT_BODY + 4 * g, 4)])
                    dve.tensor_copy(staging[:, 4 * g:4 * g + 4, EW:REC].rearrange("p e r -> p r e"),
                                    fld[:, :, bass.ds(i * SORT_BODY + 4 * g, 4)])
                    dve.wait_ge(e_mm, START + i * SORT_GROUPS + (g + 1))
                    for k in range(2):
                        last = dve.tensor_tensor(staging[:, 4 * g + k:4 * g + 4:2, 0:EW],
                                                 banks[4 + 2 * (g % 2) + k][:, :].rearrange("p (e f) -> p e f", e=2),
                                                 c_spread.unsqueeze(1).to_broadcast([P, 2, EW]), ALU.add)
                    last.then_inc(rec_ready, 1)

            dve.wait_ge(folded, 2)
            make_records(0, None)
            with dve.Fori(0, SORT_ITERS - 1) as j:
                make_records(j + 1, j)

            shape = [P, 4, NB - 1]
            cmp = running.rearrange("p b e -> p (b e)")[:, 0:4 * (NB - 1)].rearrange("p (c b) -> p c b", c=4)
            for key in range(2):
                link(dve.tensor_tensor(cmp, start[:, key, 1:NB].unsqueeze(1).to_broadcast(shape),
                                       chunk_no[:, :].unsqueeze(2).to_broadcast(shape), ALU.is_le))
                link(dve.tensor_reduce(small[:, 0, 0:4], cmp, AX_X, ALU.add))
                dve.tensor_copy(ints[:, key, 0:4], small[:, 0, 0:4]).then_inc(map_ready, 1)
            dve.tensor_reduce(wrs[:, :], W("wr").rearrange("p (t f) -> p f t", t=TYPES), AX_X, ALU.add)
            dve.tensor_reduce(l2_row[0:1, :], R("lb").rearrange("p (t f) -> p f t", t=2 * TYPES), AX_X, ALU.add)
            dve.memset(cw[:, :], 0.0)
            dve.memset(yidx[:, :], 0)
            dve.memset(posidx[:, :], 0)
            dve.memset(sloc[:, :], 0.0).then_inc(sort_done, 1)
            dve.wait_ge(sort_done, 1)

            def take_fields(body, count):
                dve.wait_ge(meta_in, count)
                cols = bass.ds(body * BODY, BODY)
                dve.tensor_copy(dloc[:, cols], meta[:, cols, 1])
                dve.tensor_tensor(types1h[:, cols, :], meta[:, cols, 2:3].to_broadcast([P, BODY, TYPES]),
                                  iota_t[:, :].unsqueeze(1).to_broadcast([P, BODY, TYPES]), ALU.is_equal)
                dve.tensor_copy(srcidx[:, cols], meta[:, cols, 0]).then_inc(fields_taken, 1)

            def take_other_fields():
                every = slice(0, NCH)
                link(dve.tensor_scalar(mc_i[:, :], srcidx[:, every], P - 1, None, ALU.bitwise_and))
                dve.tensor_copy(sloc[:, every], mc_i[:, :])
                link(dve.scalar_tensor_tensor(out=mc_f[:, 0, :], in0=meta[:, every, 0], scalar=float(TYPES),
                                              in1=meta[:, every, 2], op0=ALU.mult, op1=ALU.add))
                dve.tensor_copy(yidx[:, every], mc_f[:, 0, :])
                dve.wait_ge(lane_rows, 1)
                link(dve.tensor_scalar(mc_f[:, 1, :], dloc[:, every], 0.0, None, ALU.is_lt))
                link(dve.tensor_tensor(mc_f[:, 1, :], mc_f[:, 1, :], lane_row[:, :], ALU.mult))
                link(dve.tensor_tensor(mc_f[:, 1, :], mc_f[:, 1, :], meta[:, every, 3], ALU.add))
                link(dve.tensor_copy(posidx[:, every], mc_f[:, 1, :]))

            def clear(p):
                dve.memset(acc, 0.0).then_inc(acc_clear[p], 1)
                dve.wait_ge(acc_clear[p], 1)

            def list_half(ring, index, h, col, done):
                dve.tensor_copy(ring[:, h * HALF:(h + 1) * HALF], index[:, bass.ds(col, HALF)]).then_inc(done, 1)

            def add_chunk(p_added, count, blk, part, ps):
                dve.wait_ge(p_added, START + count)
                slot = acc[:, bass.ds(blk, 1), 0:part].rearrange("p a f -> p (a f)")
                dve.tensor_tensor(slot, slot, ps, ALU.add).then_inc(p_added, 1)

            def add_pair(p_added, count, blk0, blk1, part, ps0, ps1):
                for k, (sums, blk, ps) in enumerate(((acc, blk0, ps0), (acc_odd, blk1, ps1))):
                    dve.wait_ge(p_added, START + count + (k - 1))
                    slot = sums[:, bass.ds(blk, 1), 0:part].rearrange("p a f -> p (a f)")
                    dve.tensor_tensor(slot, slot, ps, ALU.add).then_inc(p_added, 1)

            def block_numbers(which, i):
                return nc.values_load_multi_w_load_instructions(
                    blkrow[0:1, which, bass.ds(i * BODY, BODY)], engines=DVE_ENGINE, min_val=0, max_val=NB - 1,
                    skip_runtime_bounds_check_because="a chunk's block is a count of at most NB - 1 blocks")[1]

            def linear(p):
                def hot(i, n):
                    for k in range(2):
                        col = i * BODY + (2 * n + k)
                        last = dve.tensor_scalar(onehot[:, n % 4, k, :], iota128[:, :], dloc[:, bass.ds(col, 1)],
                                                 cw[:, bass.ds(col, 1)] if p.weighted else None, ALU.is_equal,
                                                 *([ALU.mult] if p.weighted else []))
                    last.then_inc(p.onehot, 1)

                def add(i, n, blks):
                    dve.wait_ge(p.mm, START + i * PAIRS + (n + 1))
                    for k in range(2):
                        add_chunk(p.added, i * BODY + (2 * n + k), blks[2 * n + k], p.width,
                                  sum_ps[n % 2][:, k * 256:k * 256 + p.width])

                if p is pass_a:
                    take_fields(0, 16)
                    dve.wait_ge(fields_taken, 1)
                for h in range(2):
                    list_half(gring, p.index, h, h * HALF, p.idx_ready)
                if p is pass_b:
                    dve.wait_ge(S["aggT"].out, S["aggT"].end)
                clear(p)
                if p is pass_b:
                    dve.wait_ge(S["own_o0"].out, S["own_o0"].end)
                    link(dve.tensor_tensor(nD, nD, nA, ALU.add))
                hot(0, 0)
                with dve.Fori(0, ITERS) as i:
                    blks = block_numbers(1, i)
                    for n in range(PAIRS):
                        if n:
                            add(i, n - 1, blks)
                        if n == 2 and p is pass_a:
                            take_fields(i + 1, i * 16 + 32)
                        if n == 4 and p is pass_a:
                            dve.wait_ge(fields_taken, i + 2)
                        if n == 4:
                            list_half(gring, p.index, 0, i * BODY + BODY, p.idx_ready)
                        hot(i, n + 1)
                    add(i, PAIRS - 1, blks)
                    list_half(gring, p.index, 1, i * BODY + (BODY + HALF), p.idx_ready)
                dve.wait_ge(p.added, START + NCH)

            def message(L):
                def hot(i, n):
                    for k in range(2):
                        last = dve.tensor_scalar(onehot[:, n % 4, k, :], iota128[:, :],
                                                 dloc[:, bass.ds(i * BODY + (2 * n + k), 1)], None, ALU.is_equal)
                    last.then_inc(L.onehot, 1)

                def half_total(i, n):
                    if n % 4 == 0:
                        dve.wait_ge(L.loaded[n // 4], i * 16 + 16)
                    dve.wait_ge(L.gathered[n], i * 32 + (L.gathered0 + 32))
                    dve.wait_ge(L.relu, START + i * PAIRS + (n - 1))
                    dve.tensor_copy(pre[:, n % 2, :, 2 * D], sloc[:, bass.ds(i * BODY + 2 * n, 2)])
                    c = 2 * (n % 4)
                    dve.tensor_tensor(pre[:, n % 2, :, 0:2 * D].rearrange("p k (d f) -> p k d f", d=2),
                                      gat_sb[:, n, :, :].rearrange("p k (d f) -> p k d f", d=2),
                                      e_sb[:, n // 4, c:c + 2, :].unsqueeze(2).to_broadcast([P, 2, 2, D]),
                                      ALU.add).then_inc(L.half, 1)

                def total(i, n):
                    dve.wait_ge(L.half, i * PAIRS + (n + 1))
                    dve.wait_ge(L.pre, i * PAIRS + (n + 1))
                    dve.tensor_tensor(pre[:, n % 2, :, 0:2 * D], pre[:, n % 2, :, 0:2 * D],
                                      pre_ps[n % 4][:, :].rearrange("p (k f) -> p k f", k=2),
                                      ALU.add).then_inc(L.summed, 1)

                def add(i, n, blks):
                    dve.wait_ge(L.mm, START + i * PAIRS + (n + 1))
                    if L.m == 0:
                        dve.wait_ge(L.c6, START + i * BODY + 2 * n)
                        dve.tensor_tensor(c6, sum_ps[n % 2][:, 256:256 + 2 * TYPES].rearrange("p (k t) -> p k t", k=2),
                                          types1h[:, bass.ds(i * BODY + 2 * n, 2), :], ALU.mult).then_inc(L.c6, 1)
                    for k in range(2):
                        add_chunk(L.added, i * BODY + (2 * n + k), blks[2 * n + k], D,
                                  sum_ps[n % 2][:, k * D:(k + 1) * D])
                    if L.m == 0:
                        dve.wait_ge(L.c6, START + i * BODY + (2 * n + 1))
                        dve.tensor_reduce(cw[:, bass.ds(i * BODY + 2 * n, 2)], c6, AX_X, ALU.add).then_inc(L.c6, 1)

                for n in range(2):
                    dve.memset(pre[:, n, :, 2 * D + 1], 1.0)
                for h in range(2):
                    list_half(gring, srcidx, h, h * HALF, L.idx_ready)
                list_half(pring, posidx, 0, 0, L.pos_ready)
                clear(L)
                hot(0, 0)
                hot(0, 1)
                with dve.Fori(0, ITERS) as i:
                    blks = block_numbers(1, i)
                    half_total(i, 0)
                    for n in range(PAIRS):
                        total(i, n)
                        hot(i, n + 2)
                        if n < PAIRS - 1:
                            half_total(i, n + 1)
                        if n:
                            add(i, n - 1, blks)
                        if n == 4:
                            list_half(gring, srcidx, 0, i * BODY + BODY, L.idx_ready)
                            for k in range(4, PAIRS):
                                dve.wait_ge(L.sent[k], i * 32 + L.sent0[k])
                            list_half(pring, posidx, 1, i * BODY + HALF, L.pos_ready)
                    add(i, PAIRS - 1, blks)
                    list_half(gring, srcidx, 1, i * BODY + (BODY + HALF), L.idx_ready)
                    for k in range(4):
                        dve.wait_ge(L.sent[k], i * 32 + (L.sent0[k] + 32))
                    list_half(pring, posidx, 0, i * BODY + BODY, L.pos_ready)
                dve.wait_ge(L.added, START + NCH)

            def backward(L):
                def hot(i, n):
                    dve.wait_ge(L.b_in[n // 2], i * 16 + 16)
                    c = 2 * (n % 2)
                    dve.tensor_tensor(back_hot[:, n % 8, :, :], iota128[:, :].unsqueeze(1).to_broadcast([P, 2, P]),
                                      hb_in[:, n // 2, c:c + 2, D:D + 1].to_broadcast([P, 2, P]),
                                      ALU.is_equal).then_inc(L.b_onehot["dve"], 1)

                def add(i, n, blks):
                    dve.wait_ge(L.b_mm, START + i * BACK_PAIRS + (n + 1))
                    add_pair(L.b_added, i * BACK_BODY + 2 * n, blks[2 * (n % PAIRS)], blks[2 * (n % PAIRS) + 1], HB,
                             back_ps[n % 4][:, 0:HB], back_ps[n % 4][:, 256:256 + HB])

                link(dve.memset(acc_odd, 0.0))
                with dve.Fori(0, BACK_ITERS) as i:
                    for n in range(BACK_PAIRS):
                        if n + 1 in HOT_BY["dve"]:
                            hot(i, n + 1)
                        if n:
                            add(i, n - 1, blks)
                        if n % PAIRS == 0:
                            blks = block_numbers(0, i * 2 + n // PAIRS)
                    add(i, BACK_PAIRS - 1, blks)
                dve.wait_ge(L.b_added, START + NCH)
                for g in range(GROUPS):
                    b = slice(blocks_of(g)[0], blocks_of(g)[-1] + 1)
                    dve.tensor_tensor(acc[:, b, 0:HB], acc[:, b, 0:HB], acc_odd[:, b, 0:HB], ALU.add)\
                        .then_inc(ready[f"accT{L.m}"], 1)
                dve.wait_ge(ready[f"accT{L.m}"], GROUPS)

            def norm(k, to, prepare, done=None):
                def of(g, t):
                    return t[:, blocks_of(g)[0]:blocks_of(g)[-1] + 1]

                for g in range(GROUPS):
                    prepare(g)
                    link(dve.tensor_reduce(of(g, small[:, 2, :]), of(g, nD), AX_X, ALU.add))
                    dve.tensor_scalar(of(g, small[:, 0, :]), of(g, small[:, 2, :]), -1.0 / D, None, ALU.mult)\
                        .then_inc(norm_mean, 1)
                dve.wait_ge(norm_std, k + 1)
                link(dve.reciprocal(small[:, 3, :], small[:, 6, :]))
                for g in range(GROUPS):
                    for b in blocks_of(g):
                        last = dve.tensor_scalar(to[:, b, :], nD[:, b, :], small[:, 0, b:b + 1],
                                                 small[:, 3, b:b + 1], ALU.add, ALU.mult)
                    if done is not None:
                        last.then_inc(done, 1)
                if done is None:
                    link(last)

            def sum_of(name, add_t):
                def prepare(g):
                    st = S[name]
                    dve.wait_ge(st.mm, st.mm0 + g + 1)
                    dve.tensor_tensor(span(nD, g), banks[g % 4][:, 0:width(g)], span(add_t, g), ALU.add)\
                        .then_inc(st.out, 1)
                    dve.wait_ge(st.out, st.out0 + g + 1)
                return prepare

            def take_out(name, dst_t, add_t):
                st = S[name]
                for g in range(GROUPS):
                    dve.wait_ge(st.mm, st.mm0 + g + 1)
                    dve.tensor_tensor(span(dst_t, g), banks[g % 4][:, 0:width(g)], span(add_t, g), ALU.add)\
                        .then_inc(st.out, 1)
                dve.wait_ge(st.out, st.end)

            def over_features(t):
                return t.unsqueeze(2).to_broadcast([P, NB, D])

            dve.wait_ge(map_in, 16)
            linear(pass_a)
            link(dve.tensor_reduce(indeg[:, :], acc[:, :, D:ACCW], AX_X, ALU.add))
            link(dve.tensor_scalar(invdeg[:, :], indeg[:, :], 1.0, None, ALU.max))
            link(dve.reciprocal(invdeg[:, :], invdeg[:, :]))

            def means(done):
                for g in range(GROUPS):
                    b = slice(blocks_of(g)[0], blocks_of(g)[-1] + 1)
                    dve.tensor_tensor(acc[:, b, 0:D], acc[:, b, 0:D],
                                      invdeg[:, b].unsqueeze(2).to_broadcast([P, len(blocks_of(g)), D]), ALU.mult)\
                        .then_inc(done, 1)

            means(ready["aggT"])
            link(dve.tensor_scalar(icnt[:, :, :], acc[:, :, D:ACCW], 1.0, None, ALU.max))
            link(dve.reciprocal(icnt[:, :, :], icnt[:, :, :]))
            take_other_fields()
            linear(pass_b)
            means(ready["agg2T"])
            norm(0, nA, sum_of("o0", nD), ready["x1T"])
            for L in layers:
                dve.wait_ge(S[f"uw{L.m}"].out, S[f"uw{L.m}"].end)
                message(L)
                backward(L)
                link(dve.tensor_tensor(small[:, 4, :], indeg[:, :], acc[:, :, HB - 1], ALU.add))
                dve.tensor_tensor(nE, ident[:, :].unsqueeze(1).to_broadcast([P, NB, D]),
                                  over_features(small[:, 4, :]), ALU.mult).then_inc(ready[f"accT{L.m}"], 1)
                take_out(f"new{L.m}", nC, nD)
                if L.m == 0:
                    dve.wait_ge(S["emb0"].out, S["emb0"].end)
            norm(1, nA, sum_of("o1", nA), ready["x2T"])
            linear(pass_c)
            dve.wait_ge(S["r2"].out, S["r2"].end)

            def all_types(g):
                b = slice(blocks_of(g)[0], blocks_of(g)[-1] + 1)
                link(dve.tensor_tensor(nD[:, b, :], acc[:, b, 0:D], nC[:, b, :], ALU.add))

            def scaled_and_added(g):
                b = slice(blocks_of(g)[0], blocks_of(g)[-1] + 1)
                shape = [P, len(blocks_of(g)), D]
                link(dve.tensor_tensor(nD[:, b, :], nD[:, b, :], spread[:, 2:3, :].to_broadcast(shape), ALU.mult))
                link(dve.tensor_tensor(nD[:, b, :], nD[:, b, :], spread[:, 3:4, :].to_broadcast(shape), ALU.add))
                link(dve.scalar_tensor_tensor(out=nD[:, b, :], in0=nD[:, b, :], scalar=0.0, in1=nA[:, b, :],
                                              op0=ALU.max, op1=ALU.add))

            norm(2, nD, all_types)
            norm(3, nA, scaled_and_added, ready["hT"])
            linear(pass_d)
            dve.tensor_tensor(nC, acc[:, :, 0:D], nA, ALU.add).then_inc(ready["hT"], 1)

            def residual(g):
                dve.wait_ge(S["o3"].out, S["o3"].out0 + g + 1)
                link(dve.tensor_tensor(span(nD, g), span(nD, g), span(nA, g), ALU.add))

            norm(4, nC, residual, out_done)

        @block.tensor
        def _(pe):
            pe.wait_ge(consts, 8)
            pe.wait_ge(w_in, 16 * (2 + len(SPREAD)))
            for m in range(2):
                w1b = W(f"m{m}w1", D, D)
                pe.matmul(banks[1][:, m * D:(m + 1) * D], W("ew2t"), w1b, start=True, stop=True)
                row = banks[1][0:1, 256 + m * D:256 + (m + 1) * D]
                pe.matmul(row, W("eb2"), w1b, start=True, stop=False)
                last = pe.matmul(row, ones[0:1, 0:1], R(f"m{m}b1"), start=False, stop=True)
            last.then_inc(fold_mm, 1)
            pe.wait_ge(folded, 1)
            pe.matmul(banks[6][:, 0:EW], ones[0:1, :], c_row[0:1, :, :].rearrange("p m f -> p (m f)"),
                      start=True, stop=True).then_inc(fold_mm, 1)

            def features(i, g):
                pe.wait_ge(ea_in[g], i * 16 + 16)
                pe.wait_ge(ea_turned_out, START + i * SORT_GROUPS + max(g - 1, 0))
                for k in range(2):
                    last = pe.transpose(banks[g % 2][:, k * P:(k + 1) * P],
                                        ea_sb[:, g, k * 2 * D_EDGE:(k + 1) * 2 * D_EDGE], ident[:, :])
                last.then_inc(ea_turned, 1)

            def hidden(i, g):
                pe.wait_ge(ea_turned_out, START + i * SORT_GROUPS + (g + 1))
                pe.wait_ge(e_hid_out, START + i * SORT_GROUPS + max(g - 1, 0))
                pe.matmul(banks[2 + g % 2][:, 0:2 * P], W("ewa"), ea_t[:, g % 2, :], start=True, stop=True)
                pe.matmul(banks[2 + g % 2][:, 2 * P:4 * P], W("ewb"), ea_t[:, g % 2, :], start=True, stop=True)\
                    .then_inc(e_hid, 1)

            def own_part(i, g):
                pe.wait_ge(e_hid_out, START + i * SORT_GROUPS + (g + 1))
                pe.wait_ge(rec_ready, START + i * SORT_GROUPS + max(g - 1, 0))
                for k in range(2):
                    for j in range(2):
                        last = pe.matmul(banks[4 + 2 * (g % 2) + k][:, j * EW:(j + 1) * EW],
                                         hid_sb[:, g % 2, (2 * k + j) * P:(2 * k + j + 1) * P], we2[:, :],
                                         start=True, stop=True)
                last.then_inc(e_mm, 1)

            def sort_body(i, prev):
                for g in range(SORT_GROUPS):
                    features(i, g)
                    if g:
                        own_part(i, g - 1)
                    else:
                        own_part(prev, SORT_GROUPS - 1)
                    hidden(i, g)

            features(0, 0)
            hidden(0, 0)
            own_part(0, 0)
            pe.wait_ge(folded, 2)
            for turn in range(2):
                pe.wait_ge(rank_tot, (turn + 1) * NB)
                pe.matmul(banks[7][:, 0:NB], tri[:, :], small[:, 0, :], start=True, stop=True)
                pe.matmul(banks[7][:, 64:64 + NB], ones[:, :], small[:, 0, :], start=True, stop=True)\
                    .then_inc(rank_sum, 1)
                for b in range(NB):
                    pe.wait_ge(slot_rows, turn * NB + b + 1)
                    last = pe.matmul(banks[6][:, 0:EC], ident[:, :], running[:, b, :], start=b == 0, stop=b == NB - 1)
                last.then_inc(slot_sums, 1)
            pe.wait_ge(ranked, 1)
            for g in range(1, SORT_GROUPS):
                features(0, g)
                if g > 1:
                    own_part(0, g - 1)
                hidden(0, g)
            with pe.Fori(0, SORT_ITERS - 1) as j:
                sort_body(j + 1, j)
            own_part(SORT_ITERS - 1, SORT_GROUPS - 1)

            def groups(name, emit):
                st = S[name]
                before = list(S).index(name) - 1
                if before >= 0:
                    last_stage = list(S.values())[before]
                    pe.wait_ge(last_stage.out, last_stage.end)
                for g in range(st.groups):
                    if g >= 4:
                        pe.wait_ge(st.out, st.out0 + g - 3)
                    emit(g, banks[g % 4]).then_inc(st.mm, 1)

            def turn(name, src_t, made=None):
                def emit(g, bank):
                    if made is not None:
                        pe.wait_ge(made, g + 1)
                    for j, b in enumerate(blocks_of(g)):
                        last = pe.transpose(bank[:, j * P:(j + 1) * P], src_t[:, b, 0:D], ident[:, :])
                    return last
                groups(name, emit)

            def product(name, weight, in_t):
                groups(name, lambda g, bank: pe.matmul(bank[:, 0:width(g)], weight, span(in_t, g),
                                                       start=True, stop=True))

            def node_rows(name, parts, bias=None):
                def emit(g, bank):
                    for j, b in enumerate(blocks_of(g)):
                        o = bank[:, j * P:(j + 1) * P]
                        if bias is not None:
                            pe.matmul(o, ones[0:1, :], bias, start=True, stop=False)
                        for k, (in_t, weight) in enumerate(parts):
                            last = pe.matmul(o, in_t[:, b, :], weight, start=bias is None and k == 0,
                                             stop=k == len(parts) - 1)
                    return last
                groups(name, emit)

            def block_numbers(which, i):
                return nc.values_load_multi_w_load_instructions(
                    blkrow[0:1, which, bass.ds(i * BODY, BODY)], engines=PE_ENGINE, min_val=0, max_val=NB - 1,
                    skip_runtime_bounds_check_because="a chunk's block is a count of at most NB - 1 blocks")[1]

            def linear(p):
                with pe.Fori(0, ITERS) as i:
                    for n in range(PAIRS):
                        pe.wait_ge(p.onehot, i * PAIRS + (n + 1))
                        pe.wait_ge(p.added, START + i * BODY + 2 * (n - 1))
                        pe.wait_ge(p.gathered[n], i * 32 + (p.gathered0 + 32))
                        for k in range(2):
                            if p.counts:
                                pe.matmul(sum_ps[n % 2][:, k * 256 + D:k * 256 + ACCW], onehot[:, n % 4, k, :],
                                          types1h[:, bass.ds(i * BODY + (2 * n + k), 1), :]
                                          .rearrange("p a t -> p (a t)"), start=True, stop=True)
                            last = pe.matmul(sum_ps[n % 2][:, k * 256:k * 256 + D], onehot[:, n % 4, k, :],
                                             gat_sb[:, n, k, 0:D], start=True, stop=True)
                        last.then_inc(p.mm, 1)

            def message(L):
                def turned(n, count):
                    pe.wait_ge(L.onehot, count + 1)
                    pe.wait_ge(L.turned_out, START + (count - 1))
                    for k in range(2):
                        last = pe.transpose(tr_ps[n % 2][:, k * P:(k + 1) * P], onehot[:, n % 4, k, :], ident[:, :])
                    last.then_inc(L.turned, 1)

                def local_part(i, n, blks):
                    pe.wait_ge(L.turned_out, START + i * PAIRS + (n + 1))
                    pe.wait_ge(L.summed, START + i * PAIRS + (n - 3))
                    for k in range(2):
                        last = pe.matmul(pre_ps[n % 4][:, k * 2 * D:(k + 1) * 2 * D],
                                         ot_sb[:, n % 4, k * P:(k + 1) * P],
                                         lt[:, bass.ds(blks[2 * n + k], 1), :].rearrange("p a f -> p (a f)"),
                                         start=True, stop=True)
                    last.then_inc(L.pre, 1)

                def sums(i, n, blks):
                    pe.wait_ge(L.relu, START + i * PAIRS + (n + 1))
                    pe.wait_ge(L.added, START + i * BODY + 2 * (n - 1))
                    for k in range(2):
                        if L.m == 0:
                            if k == 0:
                                pe.wait_ge(L.c6, START + i * BODY + 2 * (n - 1))
                            pe.matmul(sum_ps[n % 2][:, 256 + k * TYPES:256 + (k + 1) * TYPES],
                                      ot_sb[:, n % 4, k * P:(k + 1) * P],
                                      icnt[:, bass.ds(blks[2 * n + k], 1), :].rearrange("p a t -> p (a t)"),
                                      start=True, stop=True)
                        last = pe.matmul(sum_ps[n % 2][:, k * D:(k + 1) * D], onehot[:, n % 4, k, :],
                                         hf_sb[:, n % 2, k, :], start=True, stop=True)
                    last.then_inc(L.mm, 1)

                turned(0, 0)
                with pe.Fori(0, ITERS) as i:
                    blks = block_numbers(1, i)
                    for n in range(PAIRS):
                        turned(n + 1, i * PAIRS + (n + 1))
                        local_part(i, n, blks)
                        if n:
                            sums(i, n - 1, blks)
                    sums(i, PAIRS - 1, blks)

            def backward(L):
                pe.wait_ge(L.added, START + NCH)
                with pe.Fori(0, BACK_ITERS) as i:
                    for n in range(BACK_PAIRS):
                        who = next(who for who in HOT_BY if n in HOT_BY[who])
                        pe.wait_ge(L.b_onehot[who], START + hot_count(who, i, n))
                        pe.wait_ge(L.b_added, START + i * BACK_BODY + 2 * (n - 3))
                        for k in range(2):
                            last = pe.matmul(back_ps[n % 4][:, k * 256:k * 256 + HB], back_hot[:, n % 8, k, :],
                                             hb_in[:, n // 2, 2 * (n % 2) + k, :], start=True, stop=True)
                        last.then_inc(L.b_mm, 1)

            pe.wait_ge(x_in, 16)
            turn("xT", nA)
            linear(pass_a)
            turn("aggT", acc, ready["aggT"])
            pe.wait_ge(S["aggT"].out, S["aggT"].end)
            node_rows("h1", [(nC, W("w1l")), (nB, W("w1r"))], R("b1"))
            pe.wait_ge(S["h1"].out, S["h1"].end)
            turn("h1T", nD)
            pe.wait_ge(S["h1T"].out, S["h1T"].end)
            node_rows("own_o0", [(nB, W("w2r"))], R("b2"))
            linear(pass_b)
            turn("agg2T", acc, ready["agg2T"])
            pe.wait_ge(S["agg2T"].out, S["agg2T"].end)
            node_rows("o0", [(nC, W("w2l"))])
            turn("x1T", nA, ready["x1T"])
            pe.wait_ge(S["x1T"].out, S["x1T"].end)
            product("nh", W("nw1"), nB)
            pe.wait_ge(S["nh"].out, S["nh"].end)
            product("emb", W("nw2"), nC)
            pe.wait_ge(S["emb"].out, S["emb"].end)
            for L in layers:
                m = L.m

                def emit(g, bank):
                    for j in range(min(2, NB - 2 * g)):
                        o = bank[:, j * 2 * D:(j + 1) * 2 * D]
                        last = pe.matmul(o, nD[:, 2 * g + j, :], wca[:, m, :, :].rearrange("p k f -> p (k f)"),
                                         start=True, stop=True)
                    return last
                groups(f"uw{m}", emit)
                pe.wait_ge(S[f"uw{m}"].out, S[f"uw{m}"].end)
                message(L)
                backward(L)
                turn(f"accT{m}", acc, ready[f"accT{m}"])
                pe.wait_ge(S[f"accT{m}"].out, S[f"accT{m}"].end)
                pe.wait_ge(ready[f"accT{m}"], GROUPS + 1)

                def emit_new(g, bank):
                    pe.matmul(bank[:, 0:width(g)], W(f"m{m}w2"), span(nB, g), start=True, stop=False)
                    return pe.matmul(bank[:, 0:width(g)], spread[:, m, :], span(nE, g), start=False, stop=True)
                groups(f"new{m}", emit_new)
                pe.wait_ge(S[f"new{m}"].out, S[f"new{m}"].end)
                product(f"ah{m}", W("aw1"), nC)
                pe.wait_ge(S[f"ah{m}"].out, S[f"ah{m}"].end)
                if m == 0:
                    product("emb0", W("aw2"), nB)
                    pe.wait_ge(S["emb0"].out, S["emb0"].end)
                else:
                    node_rows("o1", [(nB, W("aw2"))], R("ab2"))
            turn("x2T", nA, ready["x2T"])
            pe.wait_ge(S["x2T"].out, S["x2T"].end)

            def emit_y(g, bank):
                b, h = divmod(g, 2)
                lo, hi = ((0, 4 * D), (4 * D, TYPES * D))[h]
                return pe.matmul(bank[:, 0:hi - lo], nB[:, b, :], W("wl", lo, hi - lo), start=True, stop=True)
            groups("y", emit_y)
            pe.wait_ge(S["y"].out, S["y"].end)
            node_rows("r2", [(nB, wrs[:, :])], l2_row[0:1, :])
            linear(pass_c)
            linear(pass_d)
            pe.wait_ge(ready["hT"], GROUPS + 1)
            turn("hT", nC)
            pe.wait_ge(S["hT"].out, S["hT"].end)
            node_rows("o3", [(nB, W("w3"))], R("b3"))


def kernel(**inputs):
    import numpy as np
    import concourse.bacc as bacc
    from concourse.bass_utils import run_bass_kernel_spmd

    a = {k: np.asarray(v) for k, v in inputs.items()}

    def edge_list(v, fill):
        flat = np.full(EPAD, fill, v.dtype)
        flat[:N_EDGES] = v
        return flat.reshape(P, EC)

    parts = {
        "w1l": a["L0_gnn_W1l"].T, "w1r": a["L0_gnn_W1r"].T, "w2l": a["L0_gnn_W2l"].T, "w2r": a["L0_gnn_W2r"].T,
        "ewa": a["L1_gnn_ew1"], "ewb": np.concatenate([np.zeros_like(a["L1_gnn_ew1"]), a["L1_gnn_ew1"]]),
        "ew2t": a["L1_gnn_ew2"].T, "w3": a["L3_gnn_W"].T,
        "wl": a["L2_gnn_W_l"].transpose(1, 0, 2).reshape(D, TYPES * D),
        "wr": a["L2_gnn_W_r"].transpose(1, 0, 2).reshape(D, TYPES * D),
    }
    for name in ("nw1", "nw2", "aw1", "aw2", "m0w2", "m1w2"):
        parts[name] = a["L1_gnn_" + name]
    for name in ("m0w1", "m1w1"):
        parts[name] = a["L1_gnn_" + name].reshape(3, D, D).transpose(1, 0, 2).reshape(D, 3 * D)
    for name in ("nb1", "nb2", "ab1", "ab2", "eb1", "eb2"):
        parts[name] = a["L1_gnn_" + name].reshape(D, 1)
    wpack = np.zeros((P, W_COLS), np.float32)
    for name, (lo, hi) in W_AT.items():
        wpack[:parts[name].shape[0], lo:hi] = parts[name]
    row_parts = {"b1": a["L0_gnn_b1"], "b2": a["L0_gnn_b2"], "ab2": a["L1_gnn_ab2"], "b3": a["L3_gnn_b"],
                 "m0b1": a["L1_gnn_m0b1"], "m1b1": a["L1_gnn_m1b1"], "m0b2": a["L1_gnn_m0b2"],
                 "m1b2": a["L1_gnn_m1b2"], "gamma": a["L2_gnn_gamma"], "beta": a["L2_gnn_beta"],
                 "lb": np.concatenate([a["L2_gnn_b"].reshape(-1), a["L2_gnn_emb"].reshape(-1)])}
    rows = np.zeros((1, R_COLS), np.float32)
    for name, (lo, hi) in R_AT.items():
        rows[0, lo:hi] = row_parts[name]
    x = np.zeros((NPAD, D), np.float32)
    x[:N_NODES] = a["x"]
    ea = np.zeros((EPAD, D_EDGE), np.float32)
    ea[:N_EDGES] = a["edge_attr_64"]
    arrays = {"src_in": edge_list(a["src"], NPAD), "dst_in": edge_list(a["dst"], NPAD),
              "type_in": edge_list(a["edge_type_6"], 0), "x_in_rows": x, "ea_in_rows": ea,
              "wpack_in": wpack, "rows_in": rows}
    nc = bacc.Bacc("TRN2", target_bir_lowering=False, num_devices=1)
    args = [nc.dram_tensor(n, v.shape, mybir.dt.from_np(v.dtype), kind="ExternalInput").ap()
            for n, v in arrays.items()]
    args.append(nc.dram_tensor("out_rows", (N_NODES, D), F32, kind="ExternalOutput").ap())
    gnn_kernel(nc, *args)
    r = run_bass_kernel_spmd(nc, [arrays], core_ids=[0])
    return r.results[0]["out_rows"]
```
